# Optimizing a Trainium2 kernel written in Bass

```python
import numpy as np
import jax
import jax.numpy as jnp

def _softmax(x, axis=-1):
    return jax.nn.softmax(x, axis=axis)

def _gelu(x):
    return jax.nn.gelu(x, approximate=True)

def _silu(x):
    return jax.nn.silu(x)

def _sigmoid(x):
    return jax.nn.sigmoid(x)

def _layernorm(x, axis=-1, eps=1e-05):
    m = jnp.mean(x, axis=axis, keepdims=True)
    v = jnp.var(x, axis=axis, keepdims=True)
    return (x - m) / jnp.sqrt(v + eps)

def _scatter_add(tgt, idx, src, axis=0):
    return tgt.at[idx].add(src)

def _segment_sum(src, seg, n):
    return jax.ops.segment_sum(src, seg, n)
kernel_name = 'mk_gnn_resnorm_d2_gnn_r8_87232d'

def setup_inputs(seed: int=0):
    np.random.seed(seed)
    _w = jnp.asarray

    def _rec_inputs():
        import jax
        import jax.numpy as jnp
        _gk = jax.random.key(seed)
        x = -0.0001126 + 1 * jax.random.normal(jax.random.fold_in(_gk, 1), (1250, 768), jnp.float32)
        _s = jax.random.randint(jax.random.fold_in(_gk, 2), (20000,), 0, 1250, jnp.int32)
        _d = jax.random.randint(jax.random.fold_in(_gk, 3), (20000,), 0, 1250, jnp.int32)
        _loop = jnp.arange(1250, dtype=jnp.int32)
        src = jnp.concatenate([_s, _d, _loop])
        dst = jnp.concatenate([_d, _s, _loop])
        _o = jnp.argsort(dst, stable=True)
        src = src[_o]
        dst = dst[_o]
        edge_type_34 = jax.random.randint(jax.random.fold_in(_gk, 12), (41250,), 0, 34, jnp.int32)
        return (x, src, dst, edge_type_34)
    x, src, dst, edge_type_34 = _rec_inputs()

    def _L0_gnn_setup():
        import jax, jax.numpy as jnp
        import numpy as np
        N = 1250
        E = 20000
        D = 768
        H1, C1 = (4, 192)
        H2, C2 = (2, 96)
        EPS = 1e-05
        NEG_SLOPE = 0.2

        def layer_norm(x, g, b):
            mu = x.mean(-1, keepdims=True)
            var = ((x - mu) ** 2).mean(-1, keepdims=True)
            return (x - mu) * jax.lax.rsqrt(var + EPS) * g + b

        def gat_conv(x, src, dst, W, a_src, a_dst, bias, H, C, n):
            h = (x @ W).reshape(n, H, C)
            s_src = (h * a_src).sum(-1)
            s_dst = (h * a_dst).sum(-1)
            e = jax.nn.leaky_relu(s_src[src] + s_dst[dst], NEG_SLOPE)
            emax = jax.ops.segment_max(e, dst, num_segments=n)
            ee = jnp.exp(e - emax[dst])
            denom = jax.ops.segment_sum(ee, dst, num_segments=n)
            alpha = ee / denom[dst]
            out = jax.ops.segment_sum(alpha[:, :, None] * h[src], dst, num_segments=n)
            return out.reshape(n, H * C) + bias
        key = jax.random.key(seed)
        ks = jax.random.split(key, 16)
        sd = 1.0 / np.sqrt(D)
        inp = {'x': jax.random.normal(ks[0], (N, D), jnp.float32), 'edge_index': jax.random.randint(ks[1], (2, E), 0, N, jnp.int64), 'norm_g': jnp.ones((D,), jnp.float32), 'norm_b': jnp.zeros((D,), jnp.float32), 'W1': jax.random.normal(ks[2], (D, H1 * C1), jnp.float32) * sd, 'a_src1': jax.random.normal(ks[3], (H1, C1), jnp.float32) * sd, 'a_dst1': jax.random.normal(ks[4], (H1, C1), jnp.float32) * sd, 'b1': jnp.zeros((H1 * C1,), jnp.float32), 'W2': jax.random.normal(ks[5], (H1 * C1, H2 * C2), jnp.float32) * sd, 'a_src2': jax.random.normal(ks[6], (H2, C2), jnp.float32) * sd, 'a_dst2': jax.random.normal(ks[7], (H2, C2), jnp.float32) * sd, 'b2': jnp.zeros((H2 * C2,), jnp.float32), 'Wu': jax.random.normal(ks[8], (D + H2 * C2, D), jnp.float32) / np.sqrt(D + H2 * C2), 'bu': jnp.zeros((D,), jnp.float32)}
        return inp
    _L0_gnn_all = _L0_gnn_setup()
    _L0_gnn_in = {k: v for k, v in _L0_gnn_all.items() if k in ('norm_g', 'norm_b', 'W1', 'a_src1', 'a_dst1', 'b1', 'W2', 'a_src2', 'a_dst2', 'b2', 'Wu', 'bu')}
    del _L0_gnn_all

    def _L1_gnn_setup():
        import jax, jax.numpy as jnp
        import numpy as np
        N_NODES = 1250
        N_EDGES = 12500
        N_REL = 34
        DIM = 768

        def _graph_encoder(x, edge_index, edge_type, W_rel, W_root, b_rgcn, W_gcn, b_gcn):
            n = x.shape[0]
            src, dst = (edge_index[0], edge_index[1])
            ones = jnp.ones((src.shape[0],), dtype=x.dtype)
            seg = edge_type * n + dst
            agg = jax.ops.segment_sum(x[src], seg, num_segments=N_REL * n)
            cnt = jax.ops.segment_sum(ones, seg, num_segments=N_REL * n)
            mean = agg.reshape(N_REL, n, -1) / jnp.maximum(cnt, 1.0).reshape(N_REL, n, 1)
            h1 = jnp.einsum('rni,rio->no', mean, W_rel) + x @ W_root + b_rgcn
            xw = h1 @ W_gcn
            deg = jax.ops.segment_sum(ones, dst, num_segments=n) + 1.0
            dinv = jax.lax.rsqrt(deg)
            norm = dinv[src] * dinv[dst]
            out = jax.ops.segment_sum(xw[src] * norm[:, None], dst, num_segments=n)
            out = out + xw * (dinv * dinv)[:, None]
            return out + b_gcn
        key = jax.random.key(seed)
        ks = jax.random.split(key, 6)
        scale = 1.0 / np.sqrt(DIM)
        x = jax.random.normal(ks[0], (N_NODES, DIM), dtype=jnp.float32)
        edge_index = jax.random.randint(ks[1], (2, N_EDGES), 0, N_NODES, dtype=jnp.int32)
        edge_type = jax.random.randint(ks[2], (N_EDGES,), 0, N_REL, dtype=jnp.int32)
        W_rel = jax.random.normal(ks[3], (N_REL, DIM, DIM), dtype=jnp.float32) * scale
        W_root = jax.random.normal(ks[4], (DIM, DIM), dtype=jnp.float32) * scale
        b_rgcn = jnp.zeros((DIM,), dtype=jnp.float32)
        W_gcn = jax.random.normal(ks[5], (DIM, DIM), dtype=jnp.float32) * scale
        b_gcn = jnp.zeros((DIM,), dtype=jnp.float32)
        return {'x': x, 'edge_index': edge_index, 'edge_type': edge_type, 'W_rel': W_rel, 'W_root': W_root, 'b_rgcn': b_rgcn, 'W_gcn': W_gcn, 'b_gcn': b_gcn}
    _L1_gnn_all = _L1_gnn_setup()
    _L1_gnn_in = {k: v for k, v in _L1_gnn_all.items() if k in ('W_rel', 'W_root', 'b_rgcn', 'W_gcn', 'b_gcn')}
    del _L1_gnn_all
    return {'x': x, 'src': src, 'dst': dst, 'edge_type_34': edge_type_34, 'L0_gnn_norm_g': _L0_gnn_in['norm_g'], 'L0_gnn_norm_b': _L0_gnn_in['norm_b'], 'L0_gnn_W1': _L0_gnn_in['W1'], 'L0_gnn_a_src1': _L0_gnn_in['a_src1'], 'L0_gnn_a_dst1': _L0_gnn_in['a_dst1'], 'L0_gnn_b1': _L0_gnn_in['b1'], 'L0_gnn_W2': _L0_gnn_in['W2'], 'L0_gnn_a_src2': _L0_gnn_in['a_src2'], 'L0_gnn_a_dst2': _L0_gnn_in['a_dst2'], 'L0_gnn_b2': _L0_gnn_in['b2'], 'L0_gnn_Wu': _L0_gnn_in['Wu'], 'L0_gnn_bu': _L0_gnn_in['bu'], 'L1_gnn_W_rel': _L1_gnn_in['W_rel'], 'L1_gnn_W_root': _L1_gnn_in['W_root'], 'L1_gnn_b_rgcn': _L1_gnn_in['b_rgcn'], 'L1_gnn_W_gcn': _L1_gnn_in['W_gcn'], 'L1_gnn_b_gcn': _L1_gnn_in['b_gcn']}

def reference(x, src, dst, edge_type_34, L0_gnn_norm_g, L0_gnn_norm_b, L0_gnn_W1, L0_gnn_a_src1, L0_gnn_a_dst1, L0_gnn_b1, L0_gnn_W2, L0_gnn_a_src2, L0_gnn_a_dst2, L0_gnn_b2, L0_gnn_Wu, L0_gnn_bu, L1_gnn_W_rel, L1_gnn_W_root, L1_gnn_b_rgcn, L1_gnn_W_gcn, L1_gnn_b_gcn):
    import jax
    import jax.numpy as jnp

    def _L0_gnn_ref(x, edge_index, norm_g, norm_b, W1, a_src1, a_dst1, b1, W2, a_src2, a_dst2, b2, Wu, bu):
        import jax, jax.numpy as jnp
        import numpy as np
        N = 1250
        E = 20000
        D = 768
        H1, C1 = (4, 192)
        H2, C2 = (2, 96)
        EPS = 1e-05
        NEG_SLOPE = 0.2

        def layer_norm(x, g, b):
            mu = x.mean(-1, keepdims=True)
            var = ((x - mu) ** 2).mean(-1, keepdims=True)
            return (x - mu) * jax.lax.rsqrt(var + EPS) * g + b

        def gat_conv(x, src, dst, W, a_src, a_dst, bias, H, C, n):
            h = (x @ W).reshape(n, H, C)
            s_src = (h * a_src).sum(-1)
            s_dst = (h * a_dst).sum(-1)
            e = jax.nn.leaky_relu(s_src[src] + s_dst[dst], NEG_SLOPE)
            emax = jax.ops.segment_max(e, dst, num_segments=n)
            ee = jnp.exp(e - emax[dst])
            denom = jax.ops.segment_sum(ee, dst, num_segments=n)
            alpha = ee / denom[dst]
            out = jax.ops.segment_sum(alpha[:, :, None] * h[src], dst, num_segments=n)
            return out.reshape(n, H * C) + bias
        loops = jnp.arange(N, dtype=edge_index.dtype)
        src = jnp.concatenate([edge_index[0], loops])
        dst = jnp.concatenate([edge_index[1], loops])
        x_norm = layer_norm(x, norm_g, norm_b)
        out1 = gat_conv(x_norm, src, dst, W1, a_src1, a_dst1, b1, H1, C1, N)
        out2 = gat_conv(out1, src, dst, W2, a_src2, a_dst2, b2, H2, C2, N)
        combined = jnp.concatenate([x, out2], axis=-1)
        return combined @ Wu + bu

    def _L1_gnn_ref(x, edge_index, edge_type, W_rel, W_root, b_rgcn, W_gcn, b_gcn):
        import jax, jax.numpy as jnp
        import numpy as np
        N_NODES = 1250
        N_EDGES = 12500
        N_REL = 34
        DIM = 768

        def _graph_encoder(x, edge_index, edge_type, W_rel, W_root, b_rgcn, W_gcn, b_gcn):
            n = x.shape[0]
            src, dst = (edge_index[0], edge_index[1])
            ones = jnp.ones((src.shape[0],), dtype=x.dtype)
            seg = edge_type * n + dst
            agg = jax.ops.segment_sum(x[src], seg, num_segments=N_REL * n)
            cnt = jax.ops.segment_sum(ones, seg, num_segments=N_REL * n)
            mean = agg.reshape(N_REL, n, -1) / jnp.maximum(cnt, 1.0).reshape(N_REL, n, 1)
            h1 = jnp.einsum('rni,rio->no', mean, W_rel) + x @ W_root + b_rgcn
            xw = h1 @ W_gcn
            deg = jax.ops.segment_sum(ones, dst, num_segments=n) + 1.0
            dinv = jax.lax.rsqrt(deg)
            norm = dinv[src] * dinv[dst]
            out = jax.ops.segment_sum(xw[src] * norm[:, None], dst, num_segments=n)
            out = out + xw * (dinv * dinv)[:, None]
            return out + b_gcn
        return _graph_encoder(x, edge_index, edge_type, W_rel, W_root, b_rgcn, W_gcn, b_gcn)
    edge_index = jnp.stack([src, dst])
    x = _layernorm(x + _L0_gnn_ref(x, edge_index, L0_gnn_norm_g, L0_gnn_norm_b, L0_gnn_W1, L0_gnn_a_src1, L0_gnn_a_dst1, L0_gnn_b1, L0_gnn_W2, L0_gnn_a_src2, L0_gnn_a_dst2, L0_gnn_b2, L0_gnn_Wu, L0_gnn_bu), axis=-1)
    x = _layernorm(x + _L1_gnn_ref(x, edge_index, edge_type_34, L1_gnn_W_rel, L1_gnn_W_root, L1_gnn_b_rgcn, L1_gnn_W_gcn, L1_gnn_b_gcn), axis=-1)
    return x

_drawn_inputs = setup_inputs


def setup_inputs(seed=0):
    import zlib

    import numpy as np

    out = dict(_drawn_inputs(seed))
    spreads = {'L0_gnn_norm_g': (1.0, 0.6),
     'L0_gnn_norm_b': (0.0, 0.1),
     'L0_gnn_b1': (0.0, 0.1),
     'L0_gnn_b2': (0.0, 0.1),
     'L0_gnn_bu': (0.0, 0.1),
     'L1_gnn_b_rgcn': (0.0, 0.1),
     'L1_gnn_b_gcn': (0.0, 0.1)}
    factors = {'L0_gnn_a_dst1': 8.0, 'L0_gnn_a_src2': 8.0, 'L0_gnn_a_dst2': 8.0}
    for name, (base, spread) in spreads.items():
        noise = np.random.default_rng([zlib.crc32(name.encode()), seed]).standard_normal(out[name].shape)
        drawn = base * np.exp(spread * noise) if base else spread * noise
        out[name] = jnp.asarray(drawn.astype(out[name].dtype))
    for name, factor in factors.items():
        out[name] = (out[name] * factor).astype(out[name].dtype)
    return out
```

```python
from contextlib import ExitStack

import concourse.bass as bass
from concourse import mybir

ALU = mybir.AluOpType
ACT = mybir.ActivationFunctionType
AX = mybir.AxisListType
F32, F32R, F16, BF16, I32 = (mybir.dt.float32, mybir.dt.float32r, mybir.dt.float16,
                             mybir.dt.bfloat16, mybir.dt.int32)
ABSMAX = bass.bass_isa.ReduceOp.absmax

P = 128


def cdiv(a, b):
    return -(-a // b)


def program(nc, x, src, dst, etype, norm_g, norm_b, W1, a_src1, a_dst1, b1, W2, a_src2, a_dst2, b2,
            Wu, bu, W_rel, W_root, b_rgcn, W_gcn, b_gcn, out):
    N, D = x.shape
    E = src.shape[0]
    R = W_rel.shape[0]
    H1, C1 = a_src1.shape
    H2, C2 = a_src2.shape
    D2 = H2 * C2
    NT = cdiv(N, P)
    KT = D // P
    LAST = N - (NT - 1) * P
    EPS, SLOPE, BIG = 1e-5, 0.2, 1e30
    XBITS = 10
    XSCALE = float(1 << XBITS)

    def rows(n):
        return LAST if n == NT - 1 else P

    EP = max(p for p in range(1, P + 1) if E % p == 0)
    EC = E // EP
    UT = 4
    UE = UT * P
    UNITS = (E + NT * UE) // UE
    ET = UNITS * UT
    CW = N + R
    BANK = 512
    CBANKS = [(a, min(a + BANK, CW)) for a in range(0, CW, BANK)]
    NBANKS = [(a, min(a + BANK, N)) for a in range(0, N, BANK)]
    HALVES = 2
    CH = D // HALVES

    ctx = ExitStack()
    with ctx:
        def sb(name, shape, dt):
            return ctx.enter_context(nc.sbuf_tensor(name, shape, dt))

        def sem(name):
            return ctx.enter_context(nc.semaphore(name))

        bank = [ctx.enter_context(nc.psum_tensor(f"bank{i}", [P, BANK], F32)) for i in range(8)]

        A0 = 0
        B0 = A0 + NT * CW * 4
        H0 = B0 + NT * N * 4
        M0 = H0 + NT * H1 * (C1 + 1) * 4
        V0 = M0 + NT * N * 2
        VSIZE = 22656
        arena = sb("arena", [P, (V0 + VSIZE) // 4], F32)

        def view(at, shape, dt=F32, parts=P):
            n = 1
            for s in shape:
                n *= s
            size = n * (2 if dt in (F16, BF16) else 4)
            assert at % 4 == 0 and size % 4 == 0 and at + size <= V0 + VSIZE, (at, size)
            v = arena[0:parts, at // 4:(at + size) // 4]
            if dt != F32:
                v = v.bitcast(dt)
            if len(shape) == 2:
                v = v.rearrange("p (a b) -> p a b", a=shape[0])
            elif len(shape) == 3:
                v = v.rearrange("p (a b c) -> p a b c", a=shape[0], b=shape[1])
            return v

        ident = sb("ident", [P, P], F32)
        ones = sb("ones", [P, P], F32)
        tri = sb("tri", [P, P], F32)
        iota = sb("iota", [P, N], F16)
        zeros = sb("zeros", [P, P], F16)
        src_s = sb("src_s", [P, ET], F32)
        dst_s = sb("dst_s", [P, ET], F32)
        typ_s = sb("typ_s", [P, ET], F32)
        w_s = typ_s
        idx_y = sb("idx_y", [P, ET], I32)
        idx_w = sb("idx_w", [P, ET], I32)
        unit_bucket = sb("unit_bucket", [P, UNITS], I32)
        row_a = sb("row_a", [P, D], F32)
        w_now = sb("w_now", [P, UT], F32)
        idx_now = sb("idx_now", [P, UT], I32)
        gcol = sb("gcol", [P, KT], F32)
        bcol = sb("bcol", [P, KT], F32)
        brcol = sb("brcol", [P, KT], F32)
        W1a = sb("W1a", [P, KT, 2 * H1], F32)
        W2a = sb("W2a", [P, KT, 2 * H2], F32)
        s1 = sb("s1", [P, NT, 2 * H1], F32)
        s2 = sb("s2", [P, NT, 2 * H2], F32)
        mx = sb("mx", [P, NT, H1], F32)
        zz = sb("zz", [P, NT, H1], F32)
        lmax = sb("lmax", [P, NT, H1], F32)
        rden = sb("rden", [P, NT], F32)
        stats = sb("stats", [P, NT, 12], F32)
        mv = sb("mv", [P, NT, 2], F32)
        sd = sb("sd", [P, NT], F32)
        rstd = sb("rstd", [P, NT], F32)
        deg = sb("deg", [P, NT], F32)
        dsq = sb("dsq", [P, NT], F32)
        dinv = sb("dinv", [P, NT], F32)
        rel_inv = src_s[:, 0:NT * R].rearrange("p (b r) -> p b r", r=R)
        epsc = sb("epsc", [P, 1], F32)
        small = sb("small", [P, 8 * NT], F32)
        credit = sb("credit", [P, 8], F32)
        smalli = sb("smalli", [P, NT], I32)
        agg_oh = sb("agg_oh", [P, UT, P], F32R)
        agg_hi = sb("agg_hi", [P, UT, CH], F32R)
        agg_lo = sb("agg_lo", [P, UT, CH], F32R)
        wabs = sb("wabs", [P, 2], F32)
        wgm = sb("wgm", [P, 2], F32)
        wexp = sb("wexp", [P, 4], I32)
        wscale = sb("wscale", [P, 2], F32)
        winv = sb("winv", [P, 2], F32)

        y_dram = [nc.dram_tensor(f"y_half{q}", (R * N, CH), F32, kind="Internal").ap() for q in range(HALVES)]
        w_dram = nc.dram_tensor("rel_inv_dram", (NT * P * R, 1), F32, kind="Internal").ap()
        credit_dram = nc.dram_tensor("credit_dram", (4, 16), F32, kind="Internal").ap()
        x1_dram = nc.dram_tensor("x1_dram", (N, D), F32, kind="Internal").ap()

        ia = [A0]

        def ix(shape, dt=F32):
            n = 1
            for s in shape:
                n *= s
            v = view(ia[0], shape, dt, EP)
            ia[0] += n * 4
            return v
        src_i, dst_i, typ_i, tmp_i = (ix([EC], I32) for _ in range(4))
        src_f, typ_f, dloc_f, dbk_f, lane_f, tile_f, pos_f = (ix([EC]) for _ in range(7))
        ohb = ix([NT, EC])
        scan = ix([NT, EC])
        ones_e = ix([EC])
        assert ia[0] <= B0
        counts = view(A0, [NT, CW])
        countsf = view(A0, [NT * CW])
        out1 = view(A0, [NT, D])
        TILE = 5000
        wkA = A0 + NT * D * 4
        ring = [view(wkA + TILE * i, [N]) for i in range(4)]
        assert wkA + 4 * TILE <= B0
        h2 = view(A0, [NT, H2, C2 + 1])
        out2 = view(A0 + NT * H2 * (C2 + 1) * 4, [NT, D2])
        xnT = view(B0, [KT, N])
        cT = view(B0, [NT, N])
        xs = view(H0, [NT, D])
        h1a = view(H0, [NT, H1, C1 + 1])
        o1T = view(H0, [KT, N])
        W1s = view(M0, [KT, D])
        a1s = view(M0 + KT * D * 4, [D])
        a1d = view(M0 + KT * D * 4 + D * 4, [D])
        mask = view(M0, [NT, N], BF16)
        NL = 5
        oh_l = view(V0, [NL, 3, P], F16)
        oh_t = view(V0 + NL * 3 * P * 2, [NL, ET], F16)
        oh_s = view(V0, [2 * UT, CW], F16)
        oh_d = view(V0 + 2 * UT * CW * 2, [2 * UT, P], F16)
        prod = view(V0 + 18432, [D])
        W2s = view(V0, [KT, D2])
        bc1 = view(V0 + 4608, [N])
        bcL = view(V0 + 4608 + TILE, [N])
        diag = view(V0 + 4608 + 2 * TILE, [NT, P])
        iota_i = view(V0, [N], I32)

        prod2 = ring[0][:, 0:D2]
        a2s = view(V0 + 19728, [D2])
        a2d = view(V0 + 19728 + 4 * D2, [D2])
        b2row = view(V0 + 19728 + 8 * D2, [D2])
        o2T = view(A0 + NT * H2 * (C2 + 1) * 4 + NT * D2 * 4, [H2, N], F32, C2)
        xt = [view(wkA + i * D * 4, [D]) for i in range(2)]
        xT = [view(wkA + (2 + i) * D * 4, [KT, P]) for i in range(2)]
        yt = [view(wkA + (4 + i) * D * 4, [D]) for i in range(2)]
        Wux = view(M0, [KT, D])
        Wuo = view(M0 + KT * D * 4, [H2, D], F32, C2)
        XH = view(H0, [KT, N], F16)
        XL = view(H0 + KT * N * 2, [KT, N], F16)
        WB = KT * CH * 4
        w_raw = [view(A0 + i * WB, [KT, CH]) for i in range(2)]
        w_hi = [view(A0 + 2 * WB + i * WB, [KT, CH], F16) for i in range(2)]
        w_lo = [view(A0 + 2 * WB + i * WB + WB // 2, [KT, CH], F16) for i in range(2)]
        ybuf = [view(A0 + 4 * WB + i * CH * 4, [CH]) for i in range(4)]
        graw = [view(A0 + 4 * WB + (4 + i) * CH * 4, [CH]) for i in range(UT)]
        hs = view(M0, [NT, D])
        hs_flat = view(M0, [NT * D])
        Wg = view(A0, [KT, D])
        hT = [view(A0 + 2 * WB + i * D * 4, [KT, P]) for i in range(2)]
        x1t = [view(A0 + 2 * WB + (2 + i) * D * 4, [D]) for i in range(2)]
        ot = [view(A0 + 2 * WB + (4 + i) * D * 4, [D]) for i in range(2)]
        assert A0 + 4 * WB + 8 * CH * 4 <= B0 and 2 * WB + 6 * D * 4 <= B0 - A0
        assert M0 + NT * D * 4 <= V0 + VSIZE and M0 + (KT + 1) * D * 4 + D * 4 <= V0 + VSIZE

        idx_loaded, x_loaded, w1_loaded, w2_loaded, vec_loaded = (sem(n) for n in (
            "idx_loaded", "x_loaded", "w1_loaded", "w2_loaded", "vec_loaded"))
        const_ready = sem("const_ready")
        pool_seq, dve_seq = sem("pool_seq"), sem("dve_seq")
        iota_ready = sem("iota_ready")
        std_ready = sem("std_ready")
        var_ready = sem("var_ready")
        xn_ready = sem("xn_ready")
        w1a_ready = sem("w1a_ready")
        xnT_psum, xnT_ready = sem("xnT_psum"), sem("xnT_ready")
        s1_psum, s1_ready = sem("s1_psum"), sem("s1_ready")
        h_psum, h_ready = sem("h_psum"), sem("h_ready")
        part_tot, part_psum = sem("part_tot"), sem("part_psum")
        oh_ready, oh_free = sem("oh_ready"), sem("oh_free")
        sort_psum, sorted_ready = sem("sort_psum"), sem("sorted_ready")
        units_ready = sem("units_ready")
        cnt_oh = sem("cnt_oh")
        cnt_psum, cnt_copied = sem("cnt_psum"), sem("cnt_copied")
        counts_ready, mask_ready, h_ones = sem("counts_ready"), sem("mask_ready"), sem("h_ones")
        rel_inv_ready, rel_inv_stored = sem("rel_inv_ready"), sem("rel_inv_stored")
        deg_ready, deg_sqrt = sem("deg_ready"), sem("deg_sqrt")
        cT_psum, cT_ready = sem("cT_psum"), sem("cT_ready")
        row_loaded = sem("row_loaded")
        a2_loaded, w2a_ready = sem("a2_loaded"), sem("w2a_ready")

        class Gat:
            def __init__(g, name, H, C, s, h, res, brow):
                g.H, g.C, g.s, g.h, g.res, g.brow = H, C, s, h, res, brow
                g.per = BANK // (C + 1)
                g.diag, g.bc_psum, g.bc = sem(f"{name}_diag"), sem(f"{name}_bc_psum"), sem(f"{name}_bc")
                g.max, g.lk, g.t, g.ex = sem(f"{name}_max"), sem(f"{name}_lk"), sem(f"{name}_t"), sem(f"{name}_ex")
                g.p, g.pv, g.out = sem(f"{name}_p"), sem(f"{name}_pv"), sem(f"{name}_out")

            def acc(g, b, r, lo=0, hi=None):
                at = (b % g.per) * (g.C + 1)
                return bank[b // g.per][0:r, at + lo:at + (g.C + 1 if hi is None else hi)]

        gat1 = Gat("gat1", H1, C1, s1, h1a, out1, row_a)
        gat2 = Gat("gat2", H2, C2, s2, h2, out2, b2row)
        o1T_psum, o1T_ready = sem("o1T_psum"), sem("o1T_ready")
        h2_psum, h2_ready, s2_psum, s2_ready = sem("h2_psum"), sem("h2_ready"), sem("s2_psum"), sem("s2_ready")
        o2T_psum, o2T_ready = sem("o2T_psum"), sem("o2T_ready")
        wu_loaded = sem("wu_loaded")
        xt_loaded = [sem("xt_loaded0"), sem("xt_loaded1")]
        xT_psum, xT_ready, y_psum, y_var, y_std, x1_ready = (sem(n) for n in (
            "xT_psum", "xT_ready", "y_psum", "y_var", "y_std", "x1_ready"))
        x1T_psum, x1_hi, x1_lo = (sem(n) for n in ("x1T_psum", "x1_hi", "x1_lo"))
        x1_stored = [sem("x1_stored0"), sem("x1_stored1")]
        w_loaded = [sem("w_loaded0"), sem("w_loaded1")]
        w_max, w_gmax, w_chain, w_scaled, w_hi_ready, w_lo_ready = (sem(n) for n in (
            "w_max", "w_gmax", "w_chain", "w_scaled", "w_hi_ready", "w_lo_ready"))
        r_psum, r_copied, hs_zero = sem("r_psum"), sem("r_copied"), sem("hs_zero")
        y_stored = [sem(f"y_stored{i}") for i in range(4)]
        edge_w = sem("edge_w")
        w_loaded_now = [sem(f"w_loaded_now{t}") for t in range(UT)]
        idx_copied = sem("idx_copied")
        g_loaded = [sem(f"g_loaded{i}") for i in range(UT)]
        e_hi, e_lo, e_sum, e_added = sem("e_hi"), sem("e_lo"), sem("e_sum"), sem("e_added")
        wg_loaded, hT_psum, hT_ready, xw_psum, xw_ready = (sem(n) for n in (
            "wg_loaded", "hT_psum", "hT_ready", "xw_psum", "xw_ready"))
        x1_loaded = [sem("x1_loaded0"), sem("x1_loaded1")]
        gcn_psum, o_var, o_std, o_ready = sem("gcn_psum"), sem("o_var"), sem("o_std"), sem("o_ready")
        out_stored = [sem("out_stored0"), sem("out_stored1")]

        PAIRS = R // 2
        STEPS = HALVES * (R + 1)
        RB = 5
        YB = 4
        PER = cdiv(UNITS, 2 * (PAIRS - 2))
        AGG_PAIRS = UNITS // (2 * PER)
        UNIT_AT = [1, 4, 7][:PER]
        assert R % 2 == 0 and UNITS == AGG_PAIRS * 2 * PER and AGG_PAIRS <= PAIRS - 2
        assert NT % RB == 0 and 2 * NT % YB == 0 and R * NT % YB == 0

        def step(q, i, j):
            return i * 2 + (q * (R + 1) + 1 + j)

        def wslot(q, j):
            return (q * (R + 1) + 1 + j) % 2

        def wuse(q, i, j):
            return i + ((q * (R + 1) + 1 + j) // 2 + 1)

        def yslot(j, n):
            return (j * NT + n) % YB

        def yuse(q, i, j, n):
            return i * (2 * NT // YB) + (q * R * NT // YB + (j * NT + n) // YB)

        class Count:
            def __init__(self, s):
                self.s, self.n = s, 0

            def add(self, ins, k=1):
                self.n += k
                ins.then_inc(self.s, k)
                return self.n

        block = ctx.enter_context(nc.Block())

        @block.sync
        def _(sp):
            for t, v in ((dst, dst_i), (src, src_i), (etype, typ_i)):
                sp.dma_start(v, t.rearrange("(p c) -> p c", p=EP)).then_inc(idx_loaded, 16)
            full = (NT - 1) * P
            sp.dma_start(xs[:, 0:NT - 1, :], x[0:full, :].rearrange("(n p) d -> p n d", p=P)).then_inc(x_loaded, 16)
            sp.dma_start(xs[0:LAST, NT - 1, :], x[full:N, :]).then_inc(x_loaded, 16)
            sp.dma_start(W1s, W1.rearrange("(k p) o -> p k o", p=P)).then_inc(w1_loaded, 16)
            sp.dma_start(row_a[:, :], b1.partition_broadcast(P)).then_inc(row_loaded, 16)
            sp.wait_ge(counts_ready, 1)
            sp.dma_start(W2s, W2.rearrange("(k p) o -> p k o", p=P)).then_inc(w2_loaded, 16)
            for t, v in ((a_src2, a2s), (a_dst2, a2d)):
                sp.dma_start(v, t.rearrange("h c -> (h c)").partition_broadcast(P)).then_inc(a2_loaded, 16)
            sp.dma_start(b2row, b2.partition_broadcast(P)).then_inc(a2_loaded, 16)
            sp.wait_ge(rel_inv_ready, 1)
            sp.dma_start(w_dram.rearrange("(b p r) one -> p b (r one)", b=NT, p=P), rel_inv[:, :, :])\
                .then_inc(rel_inv_stored, 16)
            sp.wait_ge(gat1.out, H1)
            sp.dma_start(row_a[:, :], bu.partition_broadcast(P)).then_inc(row_loaded, 16)
            sp.wait_ge(gat2.max, NT * H2)
            sp.dma_start(Wux, Wu[0:D, :].rearrange("(k p) o -> p k o", p=P)).then_inc(wu_loaded, 16)
            sp.dma_start(Wuo, Wu[D:D + D2, :].rearrange("(k p) o -> p k o", p=C2)).then_inc(wu_loaded, 16)
            sp.wait_ge(gat2.out, H2)
            for n in range(NT):
                r = rows(n)
                if n >= 2:
                    sp.wait_ge(x1_ready, n - 1)
                sp.dma_start(xt[n % 2][0:r, :], x[n * P:n * P + r, :]).then_inc(xt_loaded[n % 2], 16)
                if n >= 1:
                    sp.wait_ge(x1_ready, n)
                    sp.dma_start(x1_dram[(n - 1) * P:n * P, :], yt[(n - 1) % 2][:, :]).then_inc(x1_stored[(n - 1) % 2], 16)
            sp.wait_ge(x1_ready, NT)
            sp.dma_start(x1_dram[(NT - 1) * P:N, :], yt[(NT - 1) % 2][0:LAST, :]).then_inc(x1_stored[(NT - 1) % 2], 16)
            for i in range(2):
                sp.wait_ge(x1_stored[i], 16 * len(range(i, NT, 2)))
            sp.dma_start(row_a[:, :], b_gcn.partition_broadcast(P)).then_inc(row_loaded, 16)
            for i in range(YB):
                sp.dma_start(credit_dram[i:i + 1, :], ones[0:1, 0:16]).then_inc(y_stored[i], 16)

            W_rel_v = W_rel.rearrange("r (k p) o -> p r k o", p=P)
            W_root_v = W_root.rearrange("(k p) o -> p k o", p=P)

            def load(q, i, j):
                o = slice(q * CH, (q + 1) * CH)
                v = W_root_v[:, :, o] if j < 0 else \
                    W_rel_v[:, bass.ds(i * 2 + j, 1), :, o].rearrange("p a k o -> p (a k) o")
                sp.dma_start(w_raw[wslot(q, j)], v).then_inc(w_loaded[wslot(q, j)], 16)

            def store(q, i, j):
                for n in range(NT):
                    sp.wait_ge(r_copied, step(q, i, j) * NT + n + 1)
                    sp.dma_start(y_dram[q][bass.ds((i * 2 + j) * N + n * P, rows(n)), :],
                                 ybuf[yslot(j, n)][0:rows(n), :]).then_inc(y_stored[yslot(j, n)], 16)

            sp.wait_ge(x1_lo, NT)
            load(0, 0, -1)
            load(0, 0, 0)
            for q in range(HALVES):
                sp.wait_ge(w_lo_ready, step(q, 0, -1) + 1)
                load(q, 0, 1)
                with sp.Fori(0, PAIRS - 1) as i:
                    for j in range(2):
                        sp.wait_ge(w_lo_ready, step(q, i, j) + 1)
                        load(q, i + 1, j)
                        store(q, i, j)
                for j in range(2):
                    if q + 1 < HALVES:
                        sp.wait_ge(w_lo_ready, step(q, PAIRS - 1, j) + 1)
                        load(q + 1, 0, j - 1)
                    store(q, PAIRS - 1, j)
            sp.wait_ge(w_lo_ready, STEPS)
            sp.dma_start(Wg, W_gcn.rearrange("(k p) o -> p k o", p=P)).then_inc(wg_loaded, 16)
            sp.wait_ge(r_psum, STEPS * NT)
            for n in range(NT):
                r = rows(n)
                if n >= 2:
                    sp.wait_ge(o_ready, n - 1)
                sp.dma_start(x1t[n % 2][0:r, :], x1_dram[n * P:n * P + r, :]).then_inc(x1_loaded[n % 2], 16)
                if n >= 1:
                    sp.wait_ge(o_ready, n)
                    sp.dma_start(out[(n - 1) * P:n * P, :], ot[(n - 1) % 2][:, :]).then_inc(out_stored[(n - 1) % 2], 16)
            sp.wait_ge(o_ready, NT)
            sp.dma_start(out[(NT - 1) * P:N, :], ot[(NT - 1) % 2][0:LAST, :]).then_inc(out_stored[(NT - 1) % 2], 16)
            for i in range(2):
                sp.wait_ge(out_stored[i], 16 * len(range(i, NT, 2)))

        @block.gpsimd
        def _(pool):
            n = Count(pool_seq)
            nc.gpsimd.iota(iota_i, pattern=[[1, N]], base=0, channel_multiplier=0).then_inc(iota_ready, 1)
            nc.gpsimd.memset(ones[:, :], 1.0).then_inc(const_ready, 1)
            nc.gpsimd.memset(zeros[:, :], 0.0).then_inc(const_ready, 1)
            nc.gpsimd.memset(epsc[:, :], EPS).then_inc(const_ready, 1)
            nc.gpsimd.memset(s1[:, :, :], 0.0).then_inc(const_ready, 1)
            nc.gpsimd.memset(s2[:, :, :], 0.0).then_inc(const_ready, 1)
            n.add(nc.gpsimd.memset(ident[:, :], 0.0))
            n.add(nc.gpsimd.memset(tri[:, :], 1.0))
            pool.wait_ge(pool_seq, 2)
            nc.gpsimd.affine_select(out=ident[:, :], in_=ident[:, :], compare_op=ALU.not_equal, fill=1.0, base=0,
                                    pattern=[[-1, P]], channel_multiplier=1).then_inc(const_ready, 1)
            nc.gpsimd.affine_select(out=tri[:, :], in_=tri[:, :], compare_op=ALU.is_gt, fill=0.0, base=0,
                                    pattern=[[1, P]], channel_multiplier=-1).then_inc(const_ready, 1)
            pool.wait_ge(xnT_psum, len(NBANKS) * KT)
            nc.gpsimd.memset(h1a[:, :, :, C1:C1 + 1], 1.0).then_inc(h_ones, 1)
            pool.wait_ge(o1T_psum, len(NBANKS) * KT)
            nc.gpsimd.memset(h2[:, :, :, C2:C2 + 1], 1.0).then_inc(h_ones, 1)
            pool.wait_ge(rel_inv_stored, 16)
            with pool.Fori(0, UNITS) as u:
                nc.gpsimd.tensor_copy(idx_now[:, :], idx_w[:, bass.ds(u * UT, UT)]).then_inc(idx_copied, 1)
                pool.wait_ge(idx_copied, u + 1)
                pool.nop(nofuse=True)
                for t in range(UT):
                    nc.gpsimd.indirect_dma_start(
                        out=w_now[:, t:t + 1], out_offset=None, in_=w_dram,
                        in_offset=bass.IndirectOffsetOnAxis(ap=idx_now[:, t:t + 1], axis=0)).then_inc(w_loaded_now[t], 16)
                for t in range(UT):
                    pool.wait_ge(w_loaded_now[t], (u + 1) * 16)
                nc.gpsimd.tensor_copy(w_s[:, bass.ds(u * UT, UT)], w_now[:, :]).then_inc(edge_w, 1)
                pool.wait_ge(edge_w, u + 1)
            pool.wait_ge(x1_lo, NT)
            nc.gpsimd.memset(hs[:, NT - 1, :], 0.0).then_inc(hs_zero, 1)

            def largest(q, i, j):
                c = slice(wslot(q, j), wslot(q, j) + 1)
                pool.wait_ge(w_max, step(q, i, j) + 1)
                pool.nop(nofuse=True)
                nc.gpsimd.partition_all_reduce(wgm[:, c], wabs[:, c], P, ABSMAX).then_inc(w_gmax, 1)

            def gather(q, u):
                for t in range(UT):
                    pool.wait_ge(e_lo, (q * UNITS + u) * UT + t + 1)
                    nc.gpsimd.tensor_copy(idx_now[:, t:t + 1], idx_y[:, bass.ds(u * UT + t, 1)]).then_inc(idx_copied, 1)
                    pool.wait_ge(idx_copied, (q * UNITS + u) * UT + t + 1 + UNITS)
                    pool.nop(nofuse=True)
                    nc.gpsimd.indirect_dma_start(
                        out=graw[t], out_offset=None, in_=y_dram[q],
                        in_offset=bass.IndirectOffsetOnAxis(ap=idx_now[:, t:t + 1], axis=0))\
                        .then_inc(g_loaded[t], 16)

            def stored(q):
                for i in range(YB):
                    pool.wait_ge(y_stored[i], 16 * ((q + 1) * R * NT // YB + 1))

            largest(0, 0, -1)
            largest(0, 0, 0)
            for q in range(HALVES):
                largest(q, 0, 1)
                if q:
                    stored(q - 1)
                    with pool.Fori(0, AGG_PAIRS) as i:
                        for j in range(2):
                            for k in range(PER):
                                gather(q - 1, (i * 2 + j) * PER + k)
                            largest(q, i + 1, j)
                with pool.Fori(AGG_PAIRS if q else 0, PAIRS - 1) as i:
                    for j in range(2):
                        largest(q, i + 1, j)
                if q + 1 < HALVES:
                    for j in range(2):
                        largest(q + 1, 0, j - 1)
            stored(HALVES - 1)
            with pool.Fori(0, UNITS) as u:
                gather(HALVES - 1, u)

        @block.scalar
        def _(act):
            col = lambda v: v.rearrange("(k p) -> p k", p=P)
            with nc.allow_non_contiguous_dma(reason="short vectors, a few hundred elements"):
                act.dma_start(gcol[:, :], col(norm_g)).then_inc(vec_loaded, 16)
                act.dma_start(bcol[:, :], col(norm_b)).then_inc(vec_loaded, 16)
                act.dma_start(brcol[:, :], col(b_rgcn)).then_inc(vec_loaded, 16)
            act.dma_start(a1s, a_src1.rearrange("h c -> (h c)").partition_broadcast(P)).then_inc(vec_loaded, 16)
            act.dma_start(a1d, a_dst1.rearrange("h c -> (h c)").partition_broadcast(P)).then_inc(vec_loaded, 16)
            act.wait_ge(const_ready, 7)
            act.wait_ge(var_ready, NT)
            nc.scalar.activation(sd[:, :], mv[:, :, 1], ACT.Sqrt, bias=epsc[:, 0:1]).then_inc(std_ready, 1)
            act.wait_ge(vec_loaded, 80)
            for g in range(len(NBANKS)):
                a, b = NBANKS[g]
                for k in range(KT):
                    act.wait_ge(xnT_psum, g * KT + k + 1)
                    nc.scalar.activation(xnT[:, k, a:b], bank[(g * KT + k) % 6][:, 0:b - a], ACT.Identity,
                                         bias=bcol[:, k:k + 1], scale=gcol[:, k:k + 1]).then_inc(xnT_ready, 1)
            act.wait_ge(s1_psum, 1)
            act.wait_ge(const_ready, 7)
            w = 2 * H1
            nc.scalar.copy(s1[:, 0:NT - 1, :], bank[7][:, 0:w * (NT - 1)].rearrange("p (n h) -> p n h", h=w))
            nc.scalar.copy(s1[0:LAST, NT - 1, :], bank[7][0:LAST, w * (NT - 1):w * NT]).then_inc(s1_ready, 1)
            hh = H1 // HALVES
            for n in range(NT):
                r = rows(n)
                for q in range(HALVES):
                    i = n * HALVES + q
                    act.wait_ge(h_psum, i + 1)
                    nc.scalar.copy(h1a[0:r, n, q * hh:(q + 1) * hh, 0:C1],
                                   bank[i % 4][0:r, 0:CH].rearrange("p (h c) -> p h c", h=hh)).then_inc(h_ready, 1)
            act.wait_ge(sort_psum, 1)
            nc.scalar.copy(src_s[:, :], bank[0][:, 0:ET]).then_inc(sorted_ready, 1)
            nc.scalar.activation(dst_s[:, :], bank[1][:, 0:ET], ACT.Copy, bias=-1.0).then_inc(sorted_ready, 1)
            nc.scalar.copy(typ_s[:, :], bank[2][:, 0:ET]).then_inc(sorted_ready, 1)
            act.wait_ge(units_ready, 1)
            nc.scalar.copy(credit[:, 0:1], ones[:, 0:1]).then_inc(cnt_copied, len(CBANKS))
            with act.Fori(0, UNITS) as u:
                b = act.value_load(unit_bucket[0:1, bass.ds(u, 1)], min_val=0, max_val=NT - 1)
                for j, (lo, hi) in enumerate(CBANKS):
                    act.wait_ge(cnt_psum, (u + 1) * len(CBANKS) + j + 2)
                    nc.scalar.copy(countsf[:, bass.ds(b * CW + lo, hi - lo)],
                                   bank[j][:, 0:hi - lo]).then_inc(cnt_copied, 1)
            for c in range(NT):
                for g, (a, b) in enumerate(NBANKS):
                    i = c * len(NBANKS) + g
                    act.wait_ge(cT_psum, i + 1)
                    nc.scalar.copy(cT[0:rows(c), c, a:b], bank[i % 6][0:rows(c), 0:b - a]).then_inc(cT_ready, 1)
            act.wait_ge(deg_ready, 1)
            nc.scalar.activation(dsq[:, :], deg[:, :], ACT.Sqrt).then_inc(deg_sqrt, 1)

            def gat(g):
                def row(i, dst):
                    act.wait_ge(g.bc_psum, i + 1)
                    for j, (a, b) in enumerate(NBANKS):
                        ins = nc.scalar.copy(dst[:, a:b], bank[5 + j][:, 0:b - a])
                    ins.then_inc(g.bc, 1)
                for h in range(g.H):
                    if h:
                        act.wait_ge(g.max, NT * h)
                    row(h, bc1)

                def leaky(i):
                    h, c = divmod(i, NT)
                    r = rows(c)
                    if c == 0:
                        if h == 0:
                            act.wait_ge(g.max, NT * g.H)
                        else:
                            act.wait_ge(g.t, NT * h)
                            act.wait_ge(g.lk, NT * h)
                        row(g.H + 2 * h, bc1)
                        row(g.H + 2 * h + 1, bcL)
                        act.wait_ge(g.bc, g.H + 2 * h + 1)
                    if i >= 4:
                        act.wait_ge(g.pv, i - 3)
                    nc.scalar.activation(ring[i % 4][0:r, :], bc1[0:r, :], ACT.Identity,
                                         bias=mx[0:r, c, h:h + 1]).then_inc(g.lk, 1)

                leaky(0)
                for i in range(g.H * NT):
                    if (i + 1) % NT:
                        leaky(i + 1)
                    r = rows(i % NT)
                    act.wait_ge(g.t, i + 1)
                    nc.scalar.activation(ring[i % 4][0:r, :], ring[i % 4][0:r, :], ACT.Exp).then_inc(g.ex, 1)
                    if (i + 1) % NT == 0 and i + 1 < g.H * NT:
                        leaky(i + 1)

            gat(gat1)
            for g, (a, b) in enumerate(NBANKS):
                for k in range(KT):
                    i = g * KT + k
                    act.wait_ge(o1T_psum, i + 1)
                    nc.scalar.copy(o1T[:, k, a:b], bank[i % 6][:, 0:b - a]).then_inc(o1T_ready, 1)
            act.wait_ge(s2_psum, 1)
            w = 2 * H2
            nc.scalar.copy(s2[:, 0:NT - 1, :], bank[7][:, 0:w * (NT - 1)].rearrange("p (n h) -> p n h", h=w))
            nc.scalar.copy(s2[0:LAST, NT - 1, :], bank[7][0:LAST, w * (NT - 1):w * NT]).then_inc(s2_ready, 1)
            for n in range(NT):
                r = rows(n)
                act.wait_ge(h2_psum, n + 1)
                nc.scalar.copy(h2[0:r, n, :, 0:C2],
                               bank[n % 4][0:r, 0:D2].rearrange("p (h c) -> p h c", h=H2)).then_inc(h2_ready, 1)
            gat(gat2)
            for j in range(H2):
                for g, (a, b) in enumerate(NBANKS):
                    i = j * len(NBANKS) + g
                    act.wait_ge(o2T_psum, i + 1)
                    nc.scalar.copy(o2T[:, j, a:b], bank[i][0:C2, 0:b - a]).then_inc(o2T_ready, 1)

            def x1_high(n):
                r = rows(n)
                act.wait_ge(x1T_psum, n + 1)
                for j in range(2):
                    k0, k1 = (0, 4) if j == 0 else (4, KT)
                    ins = nc.scalar.activation(XH[:, k0:k1, n * P:n * P + r],
                                               bank[6 + j][:, 0:(k1 - k0) * P].rearrange("p (k n) -> p k n", n=P)[:, :, 0:r],
                                               ACT.Copy, scale=XSCALE)
                ins.then_inc(x1_hi, 1)

            for n in range(NT):
                r = rows(n)
                act.wait_ge(xT_psum, n + 1)
                if n >= 2:
                    act.wait_ge(y_psum, n - 1)
                for j in range(2):
                    k0, k1 = (0, 4) if j == 0 else (4, KT)
                    ins = nc.scalar.copy(xT[n % 2][:, k0:k1, 0:r],
                                         bank[j][:, 0:(k1 - k0) * P].rearrange("p (k n) -> p k n", n=P)[:, :, 0:r])
                ins.then_inc(xT_ready, 1)
                act.wait_ge(y_var, n + 1)
                nc.scalar.activation(sd[0:r, n:n + 1], rstd[0:r, n:n + 1], ACT.Sqrt).then_inc(y_std, 1)
                if n:
                    x1_high(n - 1)
            x1_high(NT - 1)

            def high(q, i, j):
                c = wslot(q, j)
                act.wait_ge(w_scaled, step(q, i, j) + 1)
                nc.scalar.activation(w_hi[c], w_raw[c], ACT.Copy, scale=wscale[:, c:c + 1]).then_inc(w_hi_ready, 1)

            def edge_high(q, u):
                for t in range(UT):
                    act.wait_ge(g_loaded[t], (q * UNITS + u + 1) * 16)
                    act.wait_ge(e_sum, q * UNITS + u + 1)
                    nc.scalar.activation(agg_hi[:, t, :], graw[t], ACT.Copy, scale=w_s[:, bass.ds(u * UT + t, 1)])\
                        .then_inc(e_hi, 1)

            def copy_out(q, i, j, n):
                c = wslot(q, j)
                r = rows(n)
                act.wait_ge(r_psum, step(q, i, j) * NT + n + 1)
                if j < 0:
                    to = hs[0:r, n, q * CH:(q + 1) * CH]
                else:
                    to = ybuf[yslot(j, n)][0:r, :]
                    act.wait_ge(y_stored[yslot(j, n)], (yuse(q, i, j, n) + 1) * 16)
                nc.scalar.activation(to, bank[n % RB][0:r, 0:CH], ACT.Copy, scale=winv[0:r, c:c + 1]).then_inc(r_copied, 1)

            def one_step(q, i, j, edges):
                for n in range(NT):
                    if edges and n in UNIT_AT:
                        edge_high(q - 1, (i * 2 + j) * PER + UNIT_AT.index(n))
                    copy_out(q, i, j, n)

            act.wait_ge(edge_w, UNITS)
            high(0, 0, -1)
            high(0, 0, 0)
            act.wait_ge(hs_zero, 1)
            for q in range(HALVES):
                one_step(q, 0, -1, False)
                high(q, 0, 1)
                if q:
                    with act.Fori(0, AGG_PAIRS) as i:
                        for j in range(2):
                            one_step(q, i, j, True)
                            high(q, i + 1, j)
                with act.Fori(AGG_PAIRS if q else 0, PAIRS - 1) as i:
                    for j in range(2):
                        one_step(q, i, j, False)
                        high(q, i + 1, j)
                for j in range(2):
                    one_step(q, PAIRS - 1, j, False)
                    if q + 1 < HALVES:
                        high(q + 1, 0, j - 1)
            with act.Fori(0, UNITS) as u:
                edge_high(HALVES - 1, u)

            def xw_out(n):
                r = rows(n)
                for q in range(HALVES):
                    act.wait_ge(xw_psum, HALVES * n + q + 1)
                    nc.scalar.activation(hs[0:r, n, q * CH:(q + 1) * CH], bank[2 + 2 * (n % 2) + q][0:r, 0:CH], ACT.Copy,
                                         scale=dinv[0:r, n:n + 1]).then_inc(xw_ready, 1)
            for n in range(NT):
                r = rows(n)
                act.wait_ge(hT_psum, n + 1)
                if n >= 2:
                    act.wait_ge(xw_psum, HALVES * (n - 1))
                for k in range(KT):
                    ins = nc.scalar.activation(hT[n % 2][:, k, 0:r], bank[k // 4][:, (k % 4) * P:(k % 4) * P + r],
                                               ACT.Identity, bias=brcol[:, k:k + 1])
                ins.then_inc(hT_ready, 1)
                if n:
                    xw_out(n - 1)
            xw_out(NT - 1)
            for n in range(NT):
                r = rows(n)
                act.wait_ge(o_var, n + 1)
                nc.scalar.activation(sd[0:r, n:n + 1], rstd[0:r, n:n + 1], ACT.Sqrt).then_inc(o_std, 1)

        @block.vector
        def _(dve):
            seq = Count(dve_seq)

            def after(ins):
                dve.wait_ge(dve_seq, seq.add(ins))

            dve.wait_ge(iota_ready, 1)
            nc.vector.memset(mv[:, :, :], 1.0)
            after(nc.vector.tensor_copy(iota[:, :], iota_i))
            dve.wait_ge(x_loaded, 32)
            for n in range(NT):
                r = rows(n)
                nc.vector.bn_stats(stats[0:r, n, 0:6], xs[0:r, n, 0:D // 2])
                after(nc.vector.bn_stats(stats[0:r, n, 6:12], xs[0:r, n, D // 2:D]))
                nc.vector.bn_aggr(mv[0:r, n, :], stats[0:r, n, :]).then_inc(var_ready, 1)
            dve.wait_ge(std_ready, 1)
            after(nc.vector.reciprocal(rstd[:, :], sd[:, :]))
            for n in range(NT):
                r = rows(n)
                nc.vector.tensor_scalar(xs[0:r, n, :], xs[0:r, n, :], mv[0:r, n, 0:1], rstd[0:r, n:n + 1],
                                        ALU.subtract, ALU.mult).then_inc(xn_ready, 1)
            dve.wait_ge(w1_loaded, 16)
            dve.wait_ge(vec_loaded, 80)
            for k in range(KT):
                for j, a in enumerate((a1s, a1d)):
                    after(nc.vector.tensor_tensor(prod, W1s[:, k, :], a, ALU.mult))
                    ins = nc.vector.tensor_reduce(W1a[:, k, j * H1:(j + 1) * H1],
                                                  prod.rearrange("p (h c) -> p h c", h=H1), AX.X, ALU.add)
                    after(ins)
            nc.vector.memset(prod[:, 0:1], 0.0).then_inc(w1a_ready, 1)

            dve.wait_ge(idx_loaded, 48)
            nc.vector.tensor_copy(src_f, src_i)
            nc.vector.tensor_copy(typ_f, typ_i)
            nc.vector.memset(ones_e, 1.0)
            after(nc.vector.tensor_scalar(tmp_i, dst_i, P - 1, None, ALU.bitwise_and))
            after(nc.vector.tensor_scalar(dloc_f, tmp_i, 1.0, None, ALU.add))
            after(nc.vector.tensor_scalar(tmp_i, dst_i, 7, None, ALU.arith_shift_right))
            after(nc.vector.tensor_copy(dbk_f, tmp_i))
            for k in range(NT):
                after(nc.vector.tensor_scalar(ohb[:, k, :], dbk_f, float(k), None, ALU.is_equal))
                after(nc.vector.tensor_tensor_scan(scan[:, k, :], ones_e, ohb[:, k, :], 0.0, ALU.mult, ALU.add))
            tot = small[0:EP, 0:NT]
            nc.vector.tensor_copy(tot, scan[:, :, EC - 1]).then_inc(part_tot, 1)
            dve.wait_ge(part_psum, 1)
            fcnt, uend, ustart, base = (small[:, i * NT:(i + 1) * NT] for i in range(1, 5))
            after(nc.vector.tensor_scalar(smalli[:, :], bank[6][:, NT:2 * NT], float(UE - 1), None, ALU.add))
            after(nc.vector.tensor_scalar(smalli[:, :], smalli[:, :], UE.bit_length() - 1, None, ALU.arith_shift_right))
            after(nc.vector.tensor_scalar(fcnt, smalli[:, :], 1.0, None, ALU.max))
            after(nc.vector.tensor_tensor_scan(uend, ones[:, 0:NT], fcnt, 0.0, ALU.mult, ALU.add))
            after(nc.vector.tensor_tensor(ustart, uend, fcnt, ALU.subtract))
            after(nc.vector.tensor_scalar(base, ustart, float(UE), -1.0, ALU.mult, ALU.add))
            after(nc.vector.tensor_tensor(base[0:EP], base[0:EP], bank[6][0:EP, 0:NT], ALU.add))
            for k in range(NT):
                after(nc.vector.scalar_tensor_tensor(scan[:, k, :], scan[:, k, :], base[0:EP, k:k + 1], ohb[:, k, :],
                                                     ALU.add, ALU.mult))
                if k:
                    after(nc.vector.tensor_tensor(scan[:, 0, :], scan[:, 0, :], scan[:, k, :], ALU.add))
            after(nc.vector.tensor_copy(dst_i, scan[:, 0, :]))
            after(nc.vector.tensor_scalar(tmp_i, dst_i, P - 1, None, ALU.bitwise_and))
            after(nc.vector.tensor_copy(lane_f, tmp_i))
            after(nc.vector.tensor_scalar(tmp_i, dst_i, 7, None, ALU.arith_shift_right))
            after(nc.vector.tensor_copy(tile_f, tmp_i))
            bu_f = view(V0 + 16384, [UNITS])
            bt_f = view(V0 + 16384 + 4 * UNITS, [ET])
            after(nc.vector.tensor_scalar(bu_f, iota[:, 0:UNITS], uend[:, 0:1], None, ALU.is_ge))
            for k in range(1, NT - 1):
                after(nc.vector.scalar_tensor_tensor(bu_f, iota[:, 0:UNITS], uend[:, k:k + 1], bu_f, ALU.is_ge, ALU.add))
            after(nc.vector.tensor_copy(bt_f.rearrange("p (u t) -> p u t", t=UT),
                                        bu_f.unsqueeze(2).broadcast_to([P, UNITS, UT])))
            nc.vector.tensor_copy(unit_bucket[:, :], bu_f).then_inc(units_ready, 1)
            with dve.Fori(0, EC // (2 * NL)) as i:
                for j in range(2 * NL):
                    c = i * (2 * NL) + j
                    s = j % NL
                    at = bass.ds(c, 1)
                    dve.wait_ge(oh_free, c + 1)
                    nc.vector.tensor_scalar(oh_l[0:EP, s, 0, :], iota[0:EP, 0:P], lane_f[:, at], src_f[:, at],
                                            ALU.is_equal, ALU.mult)
                    nc.vector.tensor_scalar(oh_l[0:EP, s, 1, :], iota[0:EP, 0:P], lane_f[:, at], dloc_f[:, at],
                                            ALU.is_equal, ALU.mult)
                    nc.vector.tensor_scalar(oh_l[0:EP, s, 2, :], iota[0:EP, 0:P], lane_f[:, at], typ_f[:, at],
                                            ALU.is_equal, ALU.mult)
                    nc.vector.tensor_scalar(oh_t[0:EP, s, :], iota[0:EP, 0:ET], tile_f[:, at], None,
                                            ALU.is_equal).then_inc(oh_ready, 1)
            dve.wait_ge(sorted_ready, 3)
            nc.vector.scalar_tensor_tensor(idx_y[:, :], typ_s[:, :], float(N), src_s[:, :], ALU.mult, ALU.add)
            after(nc.vector.scalar_tensor_tensor(bt_f, bt_f, float(P), dst_s[:, :], ALU.mult, ALU.add))
            after(nc.vector.scalar_tensor_tensor(bt_f, bt_f, float(R), typ_s[:, :], ALU.mult, ALU.add))
            after(nc.vector.tensor_scalar(idx_w[:, :], bt_f, 0.0, None, ALU.max))
            with dve.Fori(0, UNITS // 2) as i:
                for j in range(2):
                    u = i * 2 + j
                    dve.wait_ge(cnt_psum, u * len(CBANKS) + 1)
                    for t in range(UT):
                        at = bass.ds(u * UT + t, 1)
                        s = j * UT + t
                        nc.vector.tensor_scalar(oh_d[:, s, :], iota[:, 0:P], dst_s[:, at], None, ALU.is_equal)
                        nc.vector.tensor_scalar(oh_s[:, s, N:CW], iota[:, 0:R], typ_s[:, at], None, ALU.is_equal)
                        nc.vector.tensor_scalar(oh_s[:, s, 0:N], iota[:, 0:N], src_s[:, at], None,
                                                ALU.is_equal).then_inc(cnt_oh, 1)
            dve.wait_ge(cnt_copied, (UNITS + 1) * len(CBANKS))
            for b in range(NT - 1, 0, -1):
                after(nc.vector.tensor_tensor(counts[:, b, :], counts[:, b, :], counts[:, b - 1, :], ALU.subtract))
            for b in range(NT):
                r = rows(b)
                ins = nc.vector.tensor_tensor(counts[0:r, b, b * P:b * P + r], counts[0:r, b, b * P:b * P + r],
                                              ident[0:r, 0:r], ALU.add)
            ins.then_inc(counts_ready, 1)
            dve.wait_ge(counts_ready, 1)
            nc.vector.tensor_reduce(deg[:, :], counts[:, :, 0:N], AX.X, ALU.add)
            after(nc.vector.tensor_scalar(rel_inv[:, :, :], counts[:, :, N:CW], 1.0, None, ALU.max))
            nc.vector.reciprocal(rel_inv[:, :, :], rel_inv[:, :, :]).then_inc(rel_inv_ready, 1)
            nc.vector.tensor_scalar(deg[:, :], deg[:, :], 1.0, None, ALU.max).then_inc(deg_ready, 1)
            dve.wait_ge(h_ready, NT * HALVES)
            for b in range(NT):
                nc.vector.tensor_scalar(mask[:, b, :], counts[:, b, 0:N], 0.0, -BIG, ALU.is_equal,
                                        ALU.mult).then_inc(mask_ready, 1)
            dve.wait_ge(deg_ready, 1)

            def rsqrt(r, sq, v):
                after(nc.vector.reciprocal(r, sq))
                after(nc.vector.tensor_tensor(v, v, r, ALU.mult))
                after(nc.vector.tensor_tensor(v, v, r, ALU.mult))
                after(nc.vector.tensor_scalar(v, v, -0.5, 1.5, ALU.mult, ALU.add))
                after(nc.vector.tensor_tensor(r, r, v, ALU.mult))

            dve.wait_ge(deg_sqrt, 1)
            rsqrt(dinv[:, :], dsq[:, :], deg[:, :])
            dve.wait_ge(w2_loaded, 16)
            dve.wait_ge(a2_loaded, 48)
            dve.wait_ge(cT_psum, NT * len(NBANKS))
            for k in range(KT):
                for j, a in enumerate((a2s, a2d)):
                    after(nc.vector.tensor_tensor(prod2, W2s[:, k, :], a, ALU.mult))
                    after(nc.vector.tensor_reduce(W2a[:, k, j * H2:(j + 1) * H2],
                                                  prod2.rearrange("p (h c) -> p h c", h=H2), AX.X, ALU.add))
            nc.vector.memset(credit[:, 2:3], 0.0).then_inc(w2a_ready, 1)

            def gat(g, s_ready):
                dve.wait_ge(s_ready, 1)
                nd = [0]

                def spread(colv):
                    if nd[0]:
                        dve.wait_ge(g.bc_psum, nd[0])
                    nd[0] += 1
                    nc.vector.tensor_tensor(diag, ident[:, :].unsqueeze(1).broadcast_to([P, NT, P]),
                                            colv.unsqueeze(2).broadcast_to([P, NT, P]), ALU.mult).then_inc(g.diag, 1)

                spread(g.s[:, :, 0])
                for h in range(g.H):
                    if h + 1 < g.H:
                        spread(g.s[:, :, h + 1])
                    dve.wait_ge(g.bc, h + 1)
                    for b in range(NT):
                        i = h * NT + b
                        if i >= 2:
                            dve.wait_ge(g.max, i - 1)
                        nc.vector.tensor_tensor_reduce(ring[i % 2], bc1, mask[:, b, :], 1.0, -3e38, ALU.add, ALU.max,
                                                       mx[:, b, h:h + 1]).then_inc(g.max, 1)
                dve.wait_ge(g.max, NT * g.H)
                z, l = zz[:, :, 0:g.H], lmax[:, :, 0:g.H]
                after(nc.vector.tensor_tensor(z, mx[:, :, 0:g.H], g.s[:, :, g.H:2 * g.H], ALU.add))
                after(nc.vector.scalar_tensor_tensor(l, z, SLOPE, z, ALU.mult, ALU.max))
                g_src, g_dst = g.s[:, :, 0:g.H], g.s[:, :, g.H:2 * g.H]
                after(nc.vector.tensor_tensor(z, g_dst, l, ALU.subtract))
                after(nc.vector.scalar_tensor_tensor(l, g_dst, SLOPE, l, ALU.mult, ALU.subtract))
                after(nc.vector.tensor_scalar(mx[:, :, 0:g.H], g_src, SLOPE, None, ALU.mult))

                def minus(i):
                    h, c = divmod(i, NT)
                    r = rows(c)
                    if c == 0:
                        spread(lmax[:, :, h])
                        spread(zz[:, :, h])
                        dve.wait_ge(g.bc, g.H + 2 * h + 2)
                    dve.wait_ge(g.lk, i + 1)
                    nc.vector.scalar_tensor_tensor(ring[i % 4][0:r, :], bcL[0:r, :], g.s[0:r, c, h:h + 1],
                                                   ring[i % 4][0:r, :], ALU.add, ALU.max).then_inc(g.t, 1)

                def normalise(h):
                    dve.wait_ge(g.pv, NT * (h + 1))
                    for b in range(NT):
                        r = rows(b)
                        ins = nc.vector.reciprocal(rden[0:r, b:b + 1], g.acc(b, r, g.C))
                    after(ins)
                    for b in range(NT):
                        r = rows(b)
                        at = slice(h * g.C, (h + 1) * g.C)
                        ins = nc.vector.scalar_tensor_tensor(g.res[0:r, b, at], g.acc(b, r, 0, g.C), rden[0:r, b:b + 1],
                                                             g.brow[0:r, at], ALU.mult, ALU.add)
                    ins.then_inc(g.out, 1)
                    dve.wait_ge(g.out, h + 1)

                minus(0)
                for i in range(g.H * NT):
                    h, c = divmod(i, NT)
                    r = rows(c)
                    if (i + 1) % NT:
                        minus(i + 1)
                    dve.wait_ge(g.ex, i + 1)
                    dve.wait_ge(cT_ready, NT * len(NBANKS)) if i == 0 else None
                    nc.vector.scalar_tensor_tensor(ring[i % 4][0:r, :], ring[i % 4][0:r, :], 1.0, cT[0:r, c, :],
                                                   ALU.min, ALU.mult).then_inc(g.p, 1)
                    if c == NT - 1:
                        normalise(h)
                        if h + 1 < g.H:
                            minus(i + 1)

            dve.wait_ge(mask_ready, NT)
            dve.wait_ge(row_loaded, 16)
            gat(gat1, s1_ready)
            gat(gat2, s2_ready)

            dve.wait_ge(row_loaded, 32)

            def x1_low(n):
                r = rows(n)
                dve.wait_ge(x1_hi, n + 1)
                for j in range(2):
                    k0, k1 = (0, 4) if j == 0 else (4, KT)
                    ins = nc.vector.scalar_tensor_tensor(
                        XL[:, k0:k1, n * P:n * P + r],
                        bank[6 + j][:, 0:(k1 - k0) * P].rearrange("p (k n) -> p k n", n=P)[:, :, 0:r], XSCALE,
                        XH[:, k0:k1, n * P:n * P + r], ALU.mult, ALU.subtract)
                ins.then_inc(x1_lo, 1)

            def layernorm(y, r, n, sem_var, sem_std, done_):
                nc.vector.bn_stats(stats[0:r, n, 0:6], y[0:r, 0:D // 2])
                after(nc.vector.bn_stats(stats[0:r, n, 6:12], y[0:r, D // 2:D]))
                after(nc.vector.bn_aggr(mv[0:r, n, :], stats[0:r, n, :]))
                c = slice(n, n + 1)
                nc.vector.tensor_scalar(rstd[0:r, c], mv[0:r, n, 1:2], EPS, None, ALU.add).then_inc(sem_var, 1)
                dve.wait_ge(sem_std, n + 1)
                rsqrt(small[0:r, c], sd[0:r, c], rstd[0:r, c])
                nc.vector.tensor_scalar(y[0:r, :], y[0:r, :], mv[0:r, n, 0:1], small[0:r, c],
                                        ALU.subtract, ALU.mult).then_inc(done_, 1)

            for n in range(NT):
                r = rows(n)
                y = yt[n % 2]
                dve.wait_ge(xt_loaded[n % 2], 16 * (n // 2 + 1))
                dve.wait_ge(y_psum, n + 1)
                if n >= 2:
                    dve.wait_ge(x1_stored[n % 2], 16 * (n // 2))
                    dve.wait_ge(x1T_psum, n - 1)
                for q in range(HALVES):
                    o = slice(q * CH, (q + 1) * CH)
                    ins = nc.vector.tensor_tensor(y[0:r, o], bank[2 + 2 * (n % 2) + q][0:r, 0:CH], xt[n % 2][0:r, o], ALU.add)
                after(ins)
                after(nc.vector.tensor_tensor(y[0:r, :], y[0:r, :], row_a[0:r, :], ALU.add))
                layernorm(y, r, n, y_var, y_std, x1_ready)
                if n:
                    x1_low(n - 1)
            x1_low(NT - 1)

            def prepare(q, i, j):
                c, m = wslot(q, j), step(q, i, j)
                dve.wait_ge(w_loaded[c], wuse(q, i, j) * 16)
                nc.vector.tensor_reduce(wabs[:, c:c + 1], w_raw[c], AX.XY, ALU.max, apply_absolute_value=True)\
                    .then_inc(w_max, 1)
                dve.wait_ge(w_gmax, m + 1)
                e, f = wexp[:, 2 * c:2 * c + 1], wexp[:, 2 * c + 1:2 * c + 2]
                bits = lambda v: v[:, c:c + 1].bitcast(I32)
                chain = (
                    (e, bits(wgm), 23, None, ALU.logical_shift_right),
                    (e, e, -1.0, float(127 + 127 + 14), ALU.mult, ALU.add),
                    (e, e, 240.0, 1.0, ALU.min, ALU.max),
                    (f, e, -1.0, float(2 * 127 - XBITS), ALU.mult, ALU.add),
                    (bits(winv), f, 23, None, ALU.logical_shift_left))
                for k, op in enumerate(chain):
                    nc.vector.tensor_scalar(*op).then_inc(w_chain, 1)
                    dve.wait_ge(w_chain, m * len(chain) + k + 1)
                nc.vector.tensor_scalar(bits(wscale), e, 23, None, ALU.logical_shift_left).then_inc(w_scaled, 1)
                dve.wait_ge(w_hi_ready, m + 1)
                nc.vector.scalar_tensor_tensor(w_lo[c], w_raw[c], wscale[:, c:c + 1], w_hi[c],
                                               ALU.mult, ALU.subtract).then_inc(w_lo_ready, 1)

            def edge_low(q, u):
                for t in range(UT):
                    at = bass.ds(u * UT + t, 1)
                    V = q * UNITS + u
                    dve.wait_ge(e_sum, V + 1)
                    nc.vector.tensor_scalar(agg_oh[:, t, :], iota[:, 0:P], dst_s[:, at], None, ALU.is_equal)
                    dve.wait_ge(e_hi, V * UT + t + 1)
                    nc.vector.scalar_tensor_tensor(agg_lo[:, t, :], graw[t], w_s[:, at], agg_hi[:, t, :].bitcast(F32),
                                                   ALU.mult, ALU.subtract).then_inc(e_lo, 1)

            def edge_add(q, u):
                b = dve.value_load(unit_bucket[0:1, bass.ds(u, 1)], min_val=0, max_val=NT - 1)
                o = bass.ds(b * D + q * CH, CH)
                dve.wait_ge(e_sum, q * UNITS + u + 2)
                dve.wait_ge(e_added, q * UNITS + u + 1)
                nc.vector.tensor_tensor(hs_flat[:, o], hs_flat[:, o], bank[5][:, 0:CH], ALU.add).then_inc(e_added, 1)

            nc.vector.memset(credit[:, 4:5], 0.0).then_inc(e_lo, UT)
            nc.vector.memset(credit[:, 5:6], 0.0).then_inc(e_added, 1)
            prepare(0, 0, -1)
            prepare(0, 0, 0)
            for q in range(HALVES):
                dve.wait_ge(r_copied, (step(q, 0, -1) + 1) * NT)
                prepare(q, 0, 1)
                if q:
                    with dve.Fori(0, AGG_PAIRS) as i:
                        for j in range(2):
                            for k in range(PER):
                                edge_low(q - 1, (i * 2 + j) * PER + k)
                                edge_add(q - 1, (i * 2 + j) * PER + k)
                            dve.wait_ge(r_copied, (step(q, i, j) + 1) * NT)
                            prepare(q, i + 1, j)
                with dve.Fori(AGG_PAIRS if q else 0, PAIRS - 1) as i:
                    for j in range(2):
                        dve.wait_ge(r_copied, (step(q, i, j) + 1) * NT)
                        prepare(q, i + 1, j)
                for j in range(2):
                    dve.wait_ge(r_copied, (step(q, PAIRS - 1, j) + 1) * NT)
                    if q + 1 < HALVES:
                        prepare(q + 1, 0, j - 1)
            with dve.Fori(0, UNITS) as u:
                edge_low(HALVES - 1, u)
                edge_add(HALVES - 1, u)

            dve.wait_ge(row_loaded, 48)
            for n in range(NT):
                r = rows(n)
                y = ot[n % 2]
                dve.wait_ge(x1_loaded[n % 2], 16 * (n // 2 + 1))
                dve.wait_ge(gcn_psum, n + 1)
                if n >= 2:
                    dve.wait_ge(out_stored[n % 2], 16 * (n // 2))
                for q in range(HALVES):
                    o = slice(q * CH, (q + 1) * CH)
                    ins = nc.vector.scalar_tensor_tensor(y[0:r, o], bank[2 + 2 * (n % 2) + q][0:r, 0:CH],
                                                         dinv[0:r, n:n + 1], x1t[n % 2][0:r, o], ALU.mult, ALU.add)
                after(ins)
                after(nc.vector.tensor_tensor(y[0:r, :], y[0:r, :], row_a[0:r, :], ALU.add))
                layernorm(y, r, n, o_var, o_std, o_ready)

        @block.tensor
        def _(pe):
            pe.wait_ge(const_ready, 7)
            for g, (a, b) in enumerate(NBANKS):
                pe.wait_ge(xn_ready, cdiv(b, P))
                for k in range(KT):
                    i = g * KT + k
                    if i >= 6:
                        pe.wait_ge(xnT_ready, i - 5)
                    for n in range(a // P, cdiv(b, P)):
                        r = rows(n)
                        ins = nc.tensor.transpose(bank[i % 6][:, n * P - a:n * P - a + r], xs[0:r, n, k * P:(k + 1) * P],
                                                  ident[0:r, 0:r])
                    ins.then_inc(xnT_psum, 1)
            pe.wait_ge(xnT_ready, len(NBANKS) * KT)
            pe.wait_ge(w1a_ready, 1)
            w = 2 * H1
            for n in range(NT):
                r = rows(n)
                for k in range(KT):
                    ins = nc.tensor.matmul(bank[7][0:r, w * n:w * n + w], xnT[:, k, n * P:n * P + r], W1a[:, k, :],
                                           start=(k == 0), stop=(k == KT - 1))
            ins.then_inc(s1_psum, 1)
            for n in range(NT):
                r = rows(n)
                for q in range(HALVES):
                    i = n * HALVES + q
                    if i >= 4:
                        pe.wait_ge(h_ready, i - 3)
                    for k in range(KT):
                        ins = nc.tensor.matmul(bank[i % 4][0:r, 0:CH], xnT[:, k, n * P:n * P + r],
                                               W1s[:, k, q * CH:(q + 1) * CH], start=(k == 0), stop=(k == KT - 1))
                    ins.then_inc(h_psum, 1)
            pe.wait_ge(h_ready, NT * HALVES)
            pe.wait_ge(part_tot, 1)
            nc.tensor.matmul(bank[6][0:EP, 0:NT], tri[0:EP, 0:EP], small[0:EP, 0:NT], start=True, stop=True)
            nc.tensor.matmul(bank[6][:, NT:2 * NT], ones[0:EP, :], small[0:EP, 0:NT], start=True,
                             stop=True).then_inc(part_psum, 1)
            for f in range(3):
                ins = nc.tensor.matmul(bank[f][:, 0:ET], zeros[:, :], iota[:, 0:ET], start=True, stop=True)
            ins.then_inc(oh_free, NL)
            with pe.Fori(0, EC // (2 * NL)) as i:
                for j in range(2 * NL):
                    c = i * (2 * NL) + j
                    s = j % NL
                    pe.wait_ge(oh_ready, c + 1)
                    for f in range(3):
                        ins = nc.tensor.matmul(bank[f][:, 0:ET], oh_l[0:EP, s, f, :], oh_t[0:EP, s, :],
                                               start=False, stop=False, skip_group_check=True)
                    ins.then_inc(oh_free, 1)
            nc.tensor.matmul(bank[3][:, 0:8], zeros[:, :], iota[:, 0:8], start=True, stop=True).then_inc(sort_psum, 1)
            pe.wait_ge(sorted_ready, 3)
            for j, (lo, hi) in enumerate(CBANKS):
                ins = nc.tensor.matmul(bank[j][:, 0:hi - lo], zeros[:, :], iota[:, 0:hi - lo], start=True, stop=True)
            ins.then_inc(cnt_psum, len(CBANKS) + 1)
            with pe.Fori(0, UNITS // 2) as i:
                for jj in range(2):
                    u = i * 2 + jj
                    for j, (lo, hi) in enumerate(CBANKS):
                        pe.wait_ge(cnt_copied, u * len(CBANKS) + j + 1)
                        for t in range(UT):
                            if j == 0:
                                pe.wait_ge(cnt_oh, u * UT + t + 1)
                            s = jj * UT + t
                            ins = nc.tensor.matmul(bank[j][:, 0:hi - lo], oh_d[:, s, :], oh_s[:, s, lo:hi],
                                                   start=False, stop=False, skip_group_check=True)
                        ins.then_inc(cnt_psum, 1)
            pe.wait_ge(counts_ready, 1)
            pe.wait_ge(cnt_copied, (UNITS + 1) * len(CBANKS))
            for c in range(NT):
                for g, (a, b) in enumerate(NBANKS):
                    i = c * len(NBANKS) + g
                    if i >= 6:
                        pe.wait_ge(cT_ready, i - 5)
                    for n in range(a // P, cdiv(b, P)):
                        r = rows(n)
                        ins = nc.tensor.transpose(bank[i % 6][0:rows(c), n * P - a:n * P - a + r],
                                                  counts[0:r, n, c * P:c * P + rows(c)], ident[0:r, 0:r])
                    ins.then_inc(cT_psum, 1)
            pe.wait_ge(cT_ready, NT * len(NBANKS))

            def gat(g, ones_wait):
                nb = [0]

                def row():
                    pe.wait_ge(g.diag, nb[0] + 1)
                    if nb[0]:
                        pe.wait_ge(g.bc, nb[0])
                    nb[0] += 1
                    flat = diag.rearrange("p n q -> p (n q)")
                    for j, (a, b) in enumerate(NBANKS):
                        ins = nc.tensor.matmul(bank[5 + j][:, 0:b - a], ones[:, :], flat[:, a:b], start=True, stop=True)
                    ins.then_inc(g.bc_psum, 1)

                for h in range(g.H):
                    row()
                pe.wait_ge(h_ones, ones_wait)
                for h in range(g.H):
                    row()
                    row()
                    for c in range(NT):
                        pe.wait_ge(g.p, h * NT + c + 1)
                        if c == 0 and h:
                            pe.wait_ge(g.out, h)
                        rc = rows(c)
                        for b in range(NT):
                            r = rows(b)
                            ins = nc.tensor.matmul(g.acc(b, r), ring[(h * NT + c) % 4][0:rc, b * P:b * P + r],
                                                   g.h[0:rc, c, h, :], start=(c == 0 and b % g.per == 0),
                                                   stop=(c == NT - 1), skip_group_check=True)
                        ins.then_inc(g.pv, 1)

            gat(gat1, 1)
            pe.wait_ge(gat1.out, H1)
            for g, (a, b) in enumerate(NBANKS):
                for k in range(KT):
                    i = g * KT + k
                    if i >= 6:
                        pe.wait_ge(o1T_ready, i - 5)
                    for n in range(a // P, cdiv(b, P)):
                        r = rows(n)
                        ins = nc.tensor.transpose(bank[i % 6][:, n * P - a:n * P - a + r], out1[0:r, n, k * P:(k + 1) * P],
                                                  ident[0:r, 0:r])
                    ins.then_inc(o1T_psum, 1)
            pe.wait_ge(o1T_ready, len(NBANKS) * KT)
            pe.wait_ge(w2a_ready, 1)
            w = 2 * H2
            for n in range(NT):
                r = rows(n)
                for k in range(KT):
                    ins = nc.tensor.matmul(bank[7][0:r, w * n:w * n + w], o1T[:, k, n * P:n * P + r], W2a[:, k, :],
                                           start=(k == 0), stop=(k == KT - 1))
            ins.then_inc(s2_psum, 1)
            for n in range(NT):
                r = rows(n)
                if n >= 4:
                    pe.wait_ge(h2_ready, n - 3)
                for k in range(KT):
                    ins = nc.tensor.matmul(bank[n % 4][0:r, 0:D2], o1T[:, k, n * P:n * P + r], W2s[:, k, :],
                                           start=(k == 0), stop=(k == KT - 1))
                ins.then_inc(h2_psum, 1)
            pe.wait_ge(h2_ready, NT)
            pe.wait_ge(s2_ready, 1)
            gat(gat2, 2)
            pe.wait_ge(gat2.out, H2)
            pe.wait_ge(gat2.bc, 3 * H2)
            for j in range(H2):
                for g, (a, b) in enumerate(NBANKS):
                    i = j * len(NBANKS) + g
                    for n in range(a // P, cdiv(b, P)):
                        r = rows(n)
                        ins = nc.tensor.transpose(bank[i][0:C2, n * P - a:n * P - a + r], out2[0:r, n, j * C2:(j + 1) * C2],
                                                  ident[0:r, 0:r])
                    ins.then_inc(o2T_psum, 1)
            pe.wait_ge(o2T_ready, H2 * len(NBANKS))

            def x1_turn(n):
                r = rows(n)
                pe.wait_ge(x1_ready, n + 1)
                if n:
                    pe.wait_ge(x1_lo, n)
                for k in range(KT):
                    ins = nc.tensor.transpose(bank[6 + k // 4][:, (k % 4) * P:(k % 4) * P + r],
                                              yt[n % 2][0:r, k * P:(k + 1) * P], ident[0:r, 0:r])
                ins.then_inc(x1T_psum, 1)

            pe.wait_ge(wu_loaded, 32)
            for n in range(NT):
                r = rows(n)
                pe.wait_ge(xt_loaded[n % 2], 16 * (n // 2 + 1))
                if n:
                    pe.wait_ge(xT_ready, n)
                for k in range(KT):
                    ins = nc.tensor.transpose(bank[k // 4][:, (k % 4) * P:(k % 4) * P + r],
                                              xt[n % 2][0:r, k * P:(k + 1) * P], ident[0:r, 0:r])
                ins.then_inc(xT_psum, 1)
                pe.wait_ge(xT_ready, n + 1)
                if n >= 2:
                    pe.wait_ge(x1_ready, n - 1)
                for q in range(HALVES):
                    o = slice(q * CH, (q + 1) * CH)
                    acc = bank[2 + 2 * (n % 2) + q][0:r, 0:CH]
                    for k in range(KT):
                        nc.tensor.matmul(acc, xT[n % 2][:, k, 0:r], Wux[:, k, o], start=(k == 0), stop=False)
                    for j in range(H2):
                        ins = nc.tensor.matmul(acc, o2T[:, j, n * P:n * P + r], Wuo[:, j, o], start=False,
                                               stop=(j == H2 - 1))
                ins.then_inc(y_psum, 1)
                if n:
                    x1_turn(n - 1)
            x1_turn(NT - 1)

            def edge_sum(q, u):
                V = q * UNITS + u
                pe.wait_ge(e_lo, (V + 1) * UT + UT)
                pe.wait_ge(e_added, V + 1)
                for t in range(UT):
                    nc.tensor.matmul(bank[5][:, 0:CH], agg_oh[:, t, :], agg_hi[:, t, :], start=(t == 0), stop=False)
                    ins = nc.tensor.matmul(bank[5][:, 0:CH], agg_oh[:, t, :], agg_lo[:, t, :], start=False,
                                           stop=(t == UT - 1))
                ins.then_inc(e_sum, 1)

            def one_step(q, i, j, edges):
                c, m = wslot(q, j), step(q, i, j)
                pe.wait_ge(w_lo_ready, m + 1)
                for n in range(NT):
                    r = rows(n)
                    if edges and n in UNIT_AT:
                        edge_sum(q - 1, (i * 2 + j) * PER + UNIT_AT.index(n))
                    if n >= RB or not (q == 0 and j < 0):
                        pe.wait_ge(r_copied, m * NT + (n - RB + 1))
                    acc = bank[n % RB][0:r, 0:CH]
                    for k in range(KT):
                        xh, xl = XH[:, k, n * P:n * P + r], XL[:, k, n * P:n * P + r]
                        nc.tensor.matmul(acc, xh, w_hi[c][:, k, :], start=(k == 0), stop=False)
                        nc.tensor.matmul(acc, xh, w_lo[c][:, k, :], start=False, stop=False)
                        ins = nc.tensor.matmul(acc, xl, w_hi[c][:, k, :], start=False, stop=(k == KT - 1))
                    ins.then_inc(r_psum, 1)

            pe.wait_ge(x1_lo, NT)
            nc.tensor.matmul(bank[7][:, 0:2], zeros[:, :], iota[:, 0:2], start=True, stop=True)\
                .then_inc(e_sum, 1)
            for q in range(HALVES):
                one_step(q, 0, -1, False)
                if q:
                    with pe.Fori(0, AGG_PAIRS) as i:
                        for j in range(2):
                            one_step(q, i, j, True)
                with pe.Fori(AGG_PAIRS if q else 0, PAIRS) as i:
                    for j in range(2):
                        one_step(q, i, j, False)
            with pe.Fori(0, UNITS) as u:
                edge_sum(HALVES - 1, u)

            pe.wait_ge(e_added, HALVES * UNITS + 1)
            pe.wait_ge(r_copied, STEPS * NT)
            pe.wait_ge(wg_loaded, 16)

            def xw(n):
                r = rows(n)
                pe.wait_ge(hT_ready, n + 1)
                if n >= 2:
                    pe.wait_ge(xw_ready, HALVES * (n - 1))
                for q in range(HALVES):
                    for k in range(KT):
                        ins = nc.tensor.matmul(bank[2 + 2 * (n % 2) + q][0:r, 0:CH], hT[n % 2][:, k, 0:r],
                                               Wg[:, k, q * CH:(q + 1) * CH], start=(k == 0), stop=(k == KT - 1))
                    ins.then_inc(xw_psum, 1)

            for n in range(NT):
                r = rows(n)
                if n:
                    pe.wait_ge(hT_ready, n)
                for k in range(KT):
                    ins = nc.tensor.transpose(bank[k // 4][:, (k % 4) * P:(k % 4) * P + r], hs[0:r, n, k * P:(k + 1) * P],
                                              ident[0:r, 0:r])
                ins.then_inc(hT_psum, 1)
                if n:
                    xw(n - 1)
            xw(NT - 1)
            pe.wait_ge(xw_ready, HALVES * NT)
            for n in range(NT):
                r = rows(n)
                if n >= 2:
                    pe.wait_ge(o_var, n - 1)
                for q in range(HALVES):
                    for c in range(NT):
                        rc = rows(c)
                        ins = nc.tensor.matmul(bank[2 + 2 * (n % 2) + q][0:r, 0:CH], cT[0:rc, c, n * P:n * P + r],
                                               hs[0:rc, c, q * CH:(q + 1) * CH], start=(c == 0), stop=(c == NT - 1))
                ins.then_inc(gcn_psum, 1)


_INS = ['x', 'src', 'dst', 'edge_type_34', 'L0_gnn_norm_g', 'L0_gnn_norm_b', 'L0_gnn_W1', 'L0_gnn_a_src1',
        'L0_gnn_a_dst1', 'L0_gnn_b1', 'L0_gnn_W2', 'L0_gnn_a_src2', 'L0_gnn_a_dst2', 'L0_gnn_b2', 'L0_gnn_Wu',
        'L0_gnn_bu', 'L1_gnn_W_rel', 'L1_gnn_W_root', 'L1_gnn_b_rgcn', 'L1_gnn_W_gcn', 'L1_gnn_b_gcn']
_OUTS = [((1250, 768), 'float32')]


def kernel(**inputs):
    import numpy as _np
    import concourse.bacc as _bacc
    from concourse import mybir as _mybir
    from concourse.bass_utils import run_bass_kernel_spmd as _run

    nc = _bacc.Bacc("TRN2", target_bir_lowering=False, num_devices=1)
    arrays, args = {}, []
    for name in _INS:
        a = _np.ascontiguousarray(inputs[name])
        arrays[f"in_{name}_dram"] = a
        args.append(nc.dram_tensor(f"in_{name}_dram", a.shape, _mybir.dt.from_np(a.dtype), kind="ExternalInput").ap())
    for i, (shape, dtype) in enumerate(_OUTS):
        dt = _mybir.dt.from_np(_np.dtype(dtype))
        args.append(nc.dram_tensor(f"out_{i}_dram", shape, dt, kind="ExternalOutput").ap())
    program(nc, *args)
    r = _run(nc, [arrays], core_ids=[0])
    got = tuple(r.results[0][f"out_{i}_dram"] for i in range(len(_OUTS)))
    return got[0]
```

```python
from contextlib import ExitStack

import concourse.bass as bass
from concourse import mybir

ALU = mybir.AluOpType
ACT = mybir.ActivationFunctionType
AX = mybir.AxisListType
F32, F32R, F16, BF16, I32 = (mybir.dt.float32, mybir.dt.float32r, mybir.dt.float16,
                             mybir.dt.bfloat16, mybir.dt.int32)
ABSMAX = bass.bass_isa.ReduceOp.absmax

P = 128


def cdiv(a, b):
    return -(-a // b)


def program(nc, x, src, dst, etype, norm_g, norm_b, W1, a_src1, a_dst1, b1, W2, a_src2, a_dst2, b2,
            Wu, bu, W_rel, W_root, b_rgcn, W_gcn, b_gcn, out):
    N, D = x.shape
    E = src.shape[0]
    R = W_rel.shape[0]
    H1, C1 = a_src1.shape
    H2, C2 = a_src2.shape
    D2 = H2 * C2
    NT = cdiv(N, P)
    KT = D // P
    LAST = N - (NT - 1) * P
    EPS, SLOPE, BIG = 1e-5, 0.2, 1e30
    XBITS = 10
    XSCALE = float(1 << XBITS)

    def rows(n):
        return LAST if n == NT - 1 else P

    EP = max(p for p in range(1, P + 1) if E % p == 0)
    EC = E // EP
    UT = 4
    UE = UT * P
    UNITS = (E + NT * UE) // UE
    ET = UNITS * UT
    CW = N + R
    BANK = 512
    CBANKS = [(a, min(a + BANK, CW)) for a in range(0, CW, BANK)]
    NBANKS = [(a, min(a + BANK, N)) for a in range(0, N, BANK)]
    HALVES = 2
    CH = D // HALVES

    ctx = ExitStack()
    with ctx:
        def sb(name, shape, dt):
            return ctx.enter_context(nc.sbuf_tensor(name, shape, dt))

        def sem(name):
            return ctx.enter_context(nc.semaphore(name))

        bank = [ctx.enter_context(nc.psum_tensor(f"bank{i}", [P, BANK], F32)) for i in range(8)]

        A0 = 0
        B0 = A0 + NT * CW * 4
        H0 = B0 + NT * N * 4
        M0 = H0 + NT * H1 * (C1 + 1) * 4
        V0 = M0 + NT * N * 2
        VSIZE = 22656
        arena = sb("arena", [P, (V0 + VSIZE) // 4], F32)

        def view(at, shape, dt=F32, parts=P):
            n = 1
            for s in shape:
                n *= s
            size = n * (2 if dt in (F16, BF16) else 4)
            assert at % 4 == 0 and size % 4 == 0 and at + size <= V0 + VSIZE, (at, size)
            v = arena[0:parts, at // 4:(at + size) // 4]
            if dt != F32:
                v = v.bitcast(dt)
            if len(shape) == 2:
                v = v.rearrange("p (a b) -> p a b", a=shape[0])
            elif len(shape) == 3:
                v = v.rearrange("p (a b c) -> p a b c", a=shape[0], b=shape[1])
            return v

        ident = sb("ident", [P, P], F32)
        ones = sb("ones", [P, P], F32)
        tri = sb("tri", [P, P], F32)
        iota = sb("iota", [P, N], F16)
        zeros = sb("zeros", [P, P], F16)
        src_s = sb("src_s", [P, ET], F32)
        dst_s = sb("dst_s", [P, ET], F32)
        typ_s = sb("typ_s", [P, ET], F32)
        w_s = typ_s
        idx_y = sb("idx_y", [P, ET], I32)
        idx_w = sb("idx_w", [P, ET], I32)
        unit_bucket = sb("unit_bucket", [P, UNITS], I32)
        row_a = sb("row_a", [P, D], F32)
        w_now = sb("w_now", [P, UT], F32)
        idx_now = sb("idx_now", [P, 2, UT], I32)
        gcol = sb("gcol", [P, KT], F32)
        bcol = sb("bcol", [P, KT], F32)
        brcol = sb("brcol", [P, KT], F32)
        W1a = sb("W1a", [P, KT, 2 * H1], F32)
        W2a = sb("W2a", [P, KT, 2 * H2], F32)
        s1 = sb("s1", [P, NT, 2 * H1], F32)
        s2 = sb("s2", [P, NT, 2 * H2], F32)
        mx = sb("mx", [P, NT, H1], F32)
        zz = sb("zz", [P, NT, H1], F32)
        lmax = sb("lmax", [P, NT, H1], F32)
        rden = sb("rden", [P, NT], F32)
        stats = sb("stats", [P, NT, 12], F32)
        mv = sb("mv", [P, NT, 2], F32)
        sd = sb("sd", [P, NT], F32)
        rstd = sb("rstd", [P, NT], F32)
        deg = sb("deg", [P, NT], F32)
        dsq = sb("dsq", [P, NT], F32)
        dinv = sb("dinv", [P, NT], F32)
        rel_inv = src_s[:, 0:NT * R].rearrange("p (b r) -> p b r", r=R)
        epsc = sb("epsc", [P, 1], F32)
        small = sb("small", [P, 8 * NT], F32)
        credit = sb("credit", [P, 8], F32)
        smalli = sb("smalli", [P, NT], I32)
        agg_oh = sb("agg_oh", [P, UT, P], F32R)
        agg_hi = sb("agg_hi", [P, UT, CH], F32R)
        agg_lo = sb("agg_lo", [P, UT, CH], F32R)
        wabs = sb("wabs", [P, 2], F32)
        wgm = sb("wgm", [P, 2], F32)
        wexp = sb("wexp", [P, 4], I32)
        wscale = sb("wscale", [P, 2], F32)
        winv = sb("winv", [P, 2], F32)

        y_dram = [nc.dram_tensor(f"y_half{q}", (R * N, CH), F32, kind="Internal").ap() for q in range(HALVES)]
        w_dram = nc.dram_tensor("rel_inv_dram", (NT * P * R, 1), F32, kind="Internal").ap()
        credit_dram = nc.dram_tensor("credit_dram", (4, 16), F32, kind="Internal").ap()
        x1_dram = nc.dram_tensor("x1_dram", (N, D), F32, kind="Internal").ap()

        ia = [A0]

        def ix(shape, dt=F32):
            n = 1
            for s in shape:
                n *= s
            v = view(ia[0], shape, dt, EP)
            ia[0] += n * 4
            return v
        src_i, dst_i, typ_i, tmp_i = (ix([EC], I32) for _ in range(4))
        src_f, typ_f, dloc_f, dbk_f, lane_f, tile_f, pos_f = (ix([EC]) for _ in range(7))
        ohb = ix([NT, EC])
        scan = ix([NT, EC])
        ones_e = ix([EC])
        oh_t = ohb[:, :, :].rearrange("p b c -> p (b c)").bitcast(F16)
        bu_f, bt_f = (view(ia[0] + 4 * k, [n]) for k, n in ((0, UNITS), (UNITS, ET)))
        assert ia[0] + 4 * (UNITS + ET) <= B0
        counts = view(A0, [NT, CW])
        countsf = view(A0, [NT * CW])
        out1 = view(A0, [NT, D])
        TILE = 5000
        wkA = A0 + NT * D * 4
        ring = [view(wkA + TILE * i, [N]) for i in range(4)]
        assert wkA + 4 * TILE <= B0
        h2 = view(A0, [NT, H2, C2 + 1])
        out2 = view(A0 + NT * H2 * (C2 + 1) * 4, [NT, D2])
        xnT = view(B0, [KT, N])
        cT = view(B0, [NT, N])
        xs = view(H0, [NT, D])
        h1a = view(H0, [NT, H1, C1 + 1])
        o1T = view(H0, [KT, N])
        W1s = view(M0, [KT, D])
        a1s = view(M0 + KT * D * 4, [D])
        a1d = view(M0 + KT * D * 4 + D * 4, [D])
        mask = view(M0, [NT, N], BF16)
        NL = 15
        oh_l = view(V0, [NL, 4, P], F16)
        oh_t = oh_t[:, 0:NL * ET].rearrange("p (s t) -> p s t", s=NL)
        assert EC % NL == 0 and NL * 4 * P * 2 <= 18432
        oh_s = view(V0, [2 * UT, CW], F16)
        oh_d = view(V0 + 2 * UT * CW * 2, [2 * UT, P], F16)
        prod = view(V0 + 18432, [D])
        W2s = view(V0, [KT, D2])
        bc1 = view(V0 + 4608, [N])
        bcL = view(V0 + 4608 + TILE, [N])
        diag = view(V0 + 4608 + 2 * TILE, [NT, P])
        iota_i = view(V0, [N], I32)

        prod2 = ring[0][:, 0:D2]
        a2s = view(V0 + 19728, [D2])
        a2d = view(V0 + 19728 + 4 * D2, [D2])
        b2row = view(V0 + 19728 + 8 * D2, [D2])
        o2T = view(A0 + NT * H2 * (C2 + 1) * 4 + NT * D2 * 4, [H2, N], F32, C2)
        xt = [view(at, [D]) for at in (wkA, wkA + D * 4, V0, V0 + D * 4)]
        XB = len(xt)
        xT = [view(wkA + (2 + i) * D * 4, [KT, P]) for i in range(2)]
        yt = [view(wkA + (4 + i) * D * 4, [D]) for i in range(2)]
        Wux = view(M0, [KT, D])
        Wuo = view(M0 + KT * D * 4, [H2, D], F32, C2)
        XH = view(H0, [KT, N], F16)
        XL = view(H0 + KT * N * 2, [KT, N], F16)
        WB = KT * CH * 4
        w_raw = [view(A0 + i * WB, [KT, CH]) for i in range(2)]
        w_hi = [view(A0 + 2 * WB + i * WB, [KT, CH], F16) for i in range(2)]
        w_lo = [view(A0 + 2 * WB + i * WB + WB // 2, [KT, CH], F16) for i in range(2)]
        ybuf = [view(A0 + 4 * WB + i * CH * 4, [CH]) for i in range(4)]
        graw = [view(A0 + 4 * WB + (4 + i) * CH * 4, [CH]) for i in range(UT)]
        graw += [view(M0 + NT * D * 4 + i * CH * 4, [CH]) for i in range(UT)]
        hs = view(M0, [NT, D])
        hs_flat = view(M0, [NT * D])
        Wg = view(A0, [KT, D])
        hT = [view(A0 + 2 * WB + i * D * 4, [KT, P]) for i in range(2)]
        x1t = [view(A0 + 2 * WB + (2 + i) * D * 4, [D]) for i in range(2)]
        ot = [view(A0 + 2 * WB + (4 + i) * D * 4, [D]) for i in range(2)]
        assert A0 + 4 * WB + 8 * CH * 4 <= B0 and 2 * WB + 6 * D * 4 <= B0 - A0
        assert M0 + NT * D * 4 + UT * CH * 4 <= V0 + VSIZE and M0 + (KT + 1) * D * 4 + D * 4 <= V0 + VSIZE

        idx_loaded, x_loaded, w1_loaded, w2_loaded, vec_loaded = (sem(n) for n in (
            "idx_loaded", "x_loaded", "w1_loaded", "w2_loaded", "vec_loaded"))
        const_ready = sem("const_ready")
        pool_seq, dve_seq = sem("pool_seq"), sem("dve_seq")
        iota_ready = sem("iota_ready")
        std_ready = sem("std_ready")
        var_ready = sem("var_ready")
        xn_ready = sem("xn_ready")
        w1a_ready = sem("w1a_ready")
        xnT_psum, xnT_ready = sem("xnT_psum"), sem("xnT_ready")
        s1_psum, s1_ready = sem("s1_psum"), sem("s1_ready")
        h_psum, h_ready = sem("h_psum"), sem("h_ready")
        part_tot, part_psum = sem("part_tot"), sem("part_psum")
        oh_lane, oh_ready, oh_fields, oh_free = (sem(n) for n in ("oh_lane", "oh_ready", "oh_fields", "oh_free"))
        sort_psum, sorted_ready = sem("sort_psum"), sem("sorted_ready")
        units_ready = sem("units_ready")
        cnt_oh = sem("cnt_oh")
        cnt_psum, cnt_copied = sem("cnt_psum"), sem("cnt_copied")
        counts_ready, mask_ready, h_ones = sem("counts_ready"), sem("mask_ready"), sem("h_ones")
        rel_inv_ready, rel_inv_stored = sem("rel_inv_ready"), sem("rel_inv_stored")
        deg_ready, deg_sqrt = sem("deg_ready"), sem("deg_sqrt")
        cT_psum, cT_ready = sem("cT_psum"), sem("cT_ready")
        row_loaded = sem("row_loaded")
        a2_loaded, w2a_ready = sem("a2_loaded"), sem("w2a_ready")

        class Gat:
            def __init__(g, name, H, C, s, h, res, brow):
                g.H, g.C, g.s, g.h, g.res, g.brow = H, C, s, h, res, brow
                g.per = BANK // (C + 1)
                g.diag, g.bc_psum, g.bc = sem(f"{name}_diag"), sem(f"{name}_bc_psum"), sem(f"{name}_bc")
                g.max, g.lk, g.t, g.ex = sem(f"{name}_max"), sem(f"{name}_lk"), sem(f"{name}_t"), sem(f"{name}_ex")
                g.p, g.pv, g.out = sem(f"{name}_p"), sem(f"{name}_pv"), sem(f"{name}_out")

            def acc(g, b, r, lo=0, hi=None):
                at = (b % g.per) * (g.C + 1)
                return bank[b // g.per][0:r, at + lo:at + (g.C + 1 if hi is None else hi)]

        gat1 = Gat("gat1", H1, C1, s1, h1a, out1, row_a)
        gat2 = Gat("gat2", H2, C2, s2, h2, out2, b2row)
        o1T_psum, o1T_ready = sem("o1T_psum"), sem("o1T_ready")
        h2_psum, h2_ready, s2_psum, s2_ready = sem("h2_psum"), sem("h2_ready"), sem("s2_psum"), sem("s2_ready")
        o2T_psum, o2T_ready = sem("o2T_psum"), sem("o2T_ready")
        wu_loaded = sem("wu_loaded")
        xt_loaded = [sem(f"xt_loaded{i}") for i in range(XB)]
        xT_psum, xT_ready, y_psum, y_var, y_std, x1_ready = (sem(n) for n in (
            "xT_psum", "xT_ready", "y_psum", "y_var", "y_std", "x1_ready"))
        x1T_psum, x1_hi, x1_lo = (sem(n) for n in ("x1T_psum", "x1_hi", "x1_lo"))
        x1_stored = [sem("x1_stored0"), sem("x1_stored1")]
        w_loaded = [sem("w_loaded0"), sem("w_loaded1")]
        w_max, w_gmax, w_chain, w_scaled, w_hi_ready, w_lo_ready = (sem(n) for n in (
            "w_max", "w_gmax", "w_chain", "w_scaled", "w_hi_ready", "w_lo_ready"))
        r_psum, r_copied, hs_zero = sem("r_psum"), sem("r_copied"), sem("hs_zero")
        y_stored = [sem(f"y_stored{i}") for i in range(4)]
        edge_w = sem("edge_w")
        w_loaded_now = [sem(f"w_loaded_now{t}") for t in range(UT)]
        idx_copied = sem("idx_copied")
        g_loaded = [sem(f"g_loaded{i}") for i in range(2 * UT)]
        e_hi, e_lo, e_sum, e_added = sem("e_hi"), sem("e_lo"), sem("e_sum"), sem("e_added")
        wg_loaded, hT_psum, hT_ready, xw_psum, xw_ready = (sem(n) for n in (
            "wg_loaded", "hT_psum", "hT_ready", "xw_psum", "xw_ready"))
        x1_loaded = [sem("x1_loaded0"), sem("x1_loaded1")]
        gcn_psum, o_var, o_std, o_ready = sem("gcn_psum"), sem("o_var"), sem("o_std"), sem("o_ready")
        out_stored = [sem("out_stored0"), sem("out_stored1")]

        SORT_PARTS = 11
        SORT_STEPS = EC // NL // SORT_PARTS
        H_BANK, HB = 3, 3
        H_FIRST = 8
        assert SORT_PARTS * SORT_STEPS * NL == EC

        def h_with(m):
            left = NT * HALVES - H_FIRST
            return range(H_FIRST + left * m // SORT_PARTS, H_FIRST + left * (m + 1) // SORT_PARTS)

        PAIRS = R // 2
        STEPS = HALVES * (R + 1)
        RB = 5
        SUMS = 5
        YB = 4
        PER = cdiv(UNITS, 2 * (PAIRS - 2))
        AGG_PAIRS = UNITS // (2 * PER)
        SPLIT_AT = [1, 4, 7][:PER]
        UNIT_AT = [3, 6, 9][:PER]
        assert R % 2 == 0 and UNITS == AGG_PAIRS * 2 * PER and UNITS % 2 == 0 and AGG_PAIRS <= PAIRS - 2
        assert NT % RB == 0 and 2 * NT % YB == 0 and R * NT % YB == 0

        def step(q, i, j):
            return i * 2 + (q * (R + 1) + 1 + j)

        def wslot(q, j):
            return (q * (R + 1) + 1 + j) % 2

        def wuse(q, i, j):
            return i + ((q * (R + 1) + 1 + j) // 2 + 1)

        def yslot(j, n):
            return (j * NT + n) % YB

        def yuse(q, i, j, n):
            return i * (2 * NT // YB) + (q * R * NT // YB + (j * NT + n) // YB)

        def unit(q, i, m, c):
            return i * m + (c + q * UNITS), c % 2, i * (m // 2) + (c // 2 + q * (UNITS // 2))

        class Count:
            def __init__(self, s):
                self.s, self.n = s, 0

            def add(self, ins, k=1):
                self.n += k
                ins.then_inc(self.s, k)
                return self.n

        block = ctx.enter_context(nc.Block())

        @block.sync
        def _(sp):
            for t, v in ((dst, dst_i), (src, src_i), (etype, typ_i)):
                sp.dma_start(v, t.rearrange("(p c) -> p c", p=EP)).then_inc(idx_loaded, 16)
            full = (NT - 1) * P
            sp.dma_start(xs[:, 0:NT - 1, :], x[0:full, :].rearrange("(n p) d -> p n d", p=P)).then_inc(x_loaded, 16)
            sp.dma_start(xs[0:LAST, NT - 1, :], x[full:N, :]).then_inc(x_loaded, 16)
            sp.dma_start(W1s, W1.rearrange("(k p) o -> p k o", p=P)).then_inc(w1_loaded, 16)
            sp.dma_start(row_a[:, :], b1.partition_broadcast(P)).then_inc(row_loaded, 16)
            sp.wait_ge(counts_ready, 1)
            sp.dma_start(W2s, W2.rearrange("(k p) o -> p k o", p=P)).then_inc(w2_loaded, 16)
            for t, v in ((a_src2, a2s), (a_dst2, a2d)):
                sp.dma_start(v, t.rearrange("h c -> (h c)").partition_broadcast(P)).then_inc(a2_loaded, 16)
            sp.dma_start(b2row, b2.partition_broadcast(P)).then_inc(a2_loaded, 16)
            sp.wait_ge(rel_inv_ready, 1)
            sp.dma_start(w_dram.rearrange("(b p r) one -> p b (r one)", b=NT, p=P), rel_inv[:, :, :])\
                .then_inc(rel_inv_stored, 16)
            sp.wait_ge(gat1.out, H1)
            sp.dma_start(row_a[:, :], bu.partition_broadcast(P)).then_inc(row_loaded, 16)
            sp.wait_ge(gat2.max, NT * H2)
            sp.dma_start(Wux, Wu[0:D, :].rearrange("(k p) o -> p k o", p=P)).then_inc(wu_loaded, 16)
            sp.dma_start(Wuo, Wu[D:D + D2, :].rearrange("(k p) o -> p k o", p=C2)).then_inc(wu_loaded, 16)
            sp.wait_ge(gat2.out, H2)
            for n in range(NT):
                r = rows(n)
                m = n - XB
                if m >= 0:
                    sp.wait_ge(x1_ready, m + 1)
                    sp.dma_start(x1_dram[m * P:(m + 1) * P, :], yt[m % 2][:, :]).then_inc(x1_stored[m % 2], 16)
                sp.dma_start(xt[n % XB][0:r, :], x[n * P:n * P + r, :]).then_inc(xt_loaded[n % XB], 16)
            for m in range(NT - XB, NT):
                sp.wait_ge(x1_ready, m + 1)
                sp.dma_start(x1_dram[m * P:m * P + rows(m), :], yt[m % 2][0:rows(m), :]).then_inc(x1_stored[m % 2], 16)
            for i in range(2):
                sp.wait_ge(x1_stored[i], 16 * len(range(i, NT, 2)))
            sp.dma_start(row_a[:, :], b_gcn.partition_broadcast(P)).then_inc(row_loaded, 16)
            for i in range(YB):
                sp.dma_start(credit_dram[i:i + 1, :], ones[0:1, 0:16]).then_inc(y_stored[i], 16)

            W_rel_v = W_rel.rearrange("r (k p) o -> p r k o", p=P)
            W_root_v = W_root.rearrange("(k p) o -> p k o", p=P)

            def load(q, i, j):
                o = slice(q * CH, (q + 1) * CH)
                v = W_root_v[:, :, o] if j < 0 else \
                    W_rel_v[:, bass.ds(i * 2 + j, 1), :, o].rearrange("p a k o -> p (a k) o")
                sp.dma_start(w_raw[wslot(q, j)], v).then_inc(w_loaded[wslot(q, j)], 16)

            def store(q, i, j):
                for n in range(NT):
                    sp.wait_ge(r_copied, step(q, i, j) * NT + n + 1)
                    sp.dma_start(y_dram[q][bass.ds((i * 2 + j) * N + n * P, rows(n)), :],
                                 ybuf[yslot(j, n)][0:rows(n), :]).then_inc(y_stored[yslot(j, n)], 16)

            sp.wait_ge(x1_lo, NT)
            load(0, 0, -1)
            load(0, 0, 0)
            for q in range(HALVES):
                sp.wait_ge(w_lo_ready, step(q, 0, -1) + 1)
                load(q, 0, 1)
                with sp.Fori(0, PAIRS - 1) as i:
                    for j in range(2):
                        sp.wait_ge(w_lo_ready, step(q, i, j) + 1)
                        load(q, i + 1, j)
                        store(q, i, j)
                for j in range(2):
                    if q + 1 < HALVES:
                        sp.wait_ge(w_lo_ready, step(q, PAIRS - 1, j) + 1)
                        load(q + 1, 0, j - 1)
                    store(q, PAIRS - 1, j)
            sp.wait_ge(w_lo_ready, STEPS)
            sp.dma_start(Wg, W_gcn.rearrange("(k p) o -> p k o", p=P)).then_inc(wg_loaded, 16)
            sp.wait_ge(r_psum, STEPS * NT)
            for n in range(NT):
                r = rows(n)
                if n >= 2:
                    sp.wait_ge(o_ready, n - 1)
                sp.dma_start(x1t[n % 2][0:r, :], x1_dram[n * P:n * P + r, :]).then_inc(x1_loaded[n % 2], 16)
                if n >= 1:
                    sp.wait_ge(o_ready, n)
                    sp.dma_start(out[(n - 1) * P:n * P, :], ot[(n - 1) % 2][:, :]).then_inc(out_stored[(n - 1) % 2], 16)
            sp.wait_ge(o_ready, NT)
            sp.dma_start(out[(NT - 1) * P:N, :], ot[(NT - 1) % 2][0:LAST, :]).then_inc(out_stored[(NT - 1) % 2], 16)
            for i in range(2):
                sp.wait_ge(out_stored[i], 16 * len(range(i, NT, 2)))

        @block.gpsimd
        def _(pool):
            n = Count(pool_seq)
            nc.gpsimd.iota(iota_i, pattern=[[1, N]], base=0, channel_multiplier=0).then_inc(iota_ready, 1)
            nc.gpsimd.memset(ones[:, :], 1.0).then_inc(const_ready, 1)
            nc.gpsimd.memset(zeros[:, :], 0.0).then_inc(const_ready, 1)
            nc.gpsimd.memset(epsc[:, :], EPS).then_inc(const_ready, 1)
            nc.gpsimd.memset(s1[:, :, :], 0.0).then_inc(const_ready, 1)
            nc.gpsimd.memset(s2[:, :, :], 0.0).then_inc(const_ready, 1)
            n.add(nc.gpsimd.memset(ident[:, :], 0.0))
            n.add(nc.gpsimd.memset(tri[:, :], 1.0))
            pool.wait_ge(pool_seq, 2)
            nc.gpsimd.affine_select(out=ident[:, :], in_=ident[:, :], compare_op=ALU.not_equal, fill=1.0, base=0,
                                    pattern=[[-1, P]], channel_multiplier=1).then_inc(const_ready, 1)
            nc.gpsimd.affine_select(out=tri[:, :], in_=tri[:, :], compare_op=ALU.is_gt, fill=0.0, base=0,
                                    pattern=[[1, P]], channel_multiplier=-1).then_inc(const_ready, 1)
            pool.wait_ge(xnT_psum, len(NBANKS) * KT)
            nc.gpsimd.memset(h1a[:, :, :, C1:C1 + 1], 1.0).then_inc(h_ones, 1)
            pool.wait_ge(o1T_psum, len(NBANKS) * KT)
            nc.gpsimd.memset(h2[:, :, :, C2:C2 + 1], 1.0).then_inc(h_ones, 1)
            pool.wait_ge(x1_lo, NT)
            nc.gpsimd.memset(hs[:, NT - 1, :], 0.0).then_inc(hs_zero, 1)

            def largest(q, i, j):
                c = slice(wslot(q, j), wslot(q, j) + 1)
                pool.wait_ge(w_max, step(q, i, j) + 1)
                pool.nop(nofuse=True)
                nc.gpsimd.partition_all_reduce(wgm[:, c], wabs[:, c], P, ABSMAX).then_inc(w_gmax, 1)

            def weigh(u):
                nc.gpsimd.tensor_copy(idx_now[:, 0, :], idx_w[:, bass.ds(u * UT, UT)]).then_inc(idx_copied, 1)
                pool.wait_ge(idx_copied, u + 1)
                pool.nop(nofuse=True)
                for t in range(UT):
                    nc.gpsimd.indirect_dma_start(
                        out=w_now[:, t:t + 1], out_offset=None, in_=w_dram,
                        in_offset=bass.IndirectOffsetOnAxis(ap=idx_now[:, 0, t:t + 1], axis=0)).then_inc(w_loaded_now[t], 16)
                for t in range(UT):
                    pool.wait_ge(w_loaded_now[t], (u + 1) * 16)
                nc.gpsimd.tensor_copy(w_s[:, bass.ds(u * UT, UT)], w_now[:, :]).then_inc(edge_w, 1)
                pool.wait_ge(edge_w, u + 1)

            def gather(q, i, m, c):
                V, place, _ = unit(q, i, m, c)
                pool.wait_ge(e_hi, V * UT + UT)
                nc.gpsimd.tensor_copy(idx_now[:, place, :], idx_y[:, bass.ds((i * m + c) * UT, UT)]).then_inc(idx_copied, 1)
                pool.wait_ge(idx_copied, V + 1 + UNITS)
                for t in range(UT):
                    pool.wait_ge(e_lo, V * UT + t + 1)
                    pool.nop(nofuse=True)
                    nc.gpsimd.indirect_dma_start(
                        out=graw[place * UT + t], out_offset=None, in_=y_dram[q],
                        in_offset=bass.IndirectOffsetOnAxis(ap=idx_now[:, place, t:t + 1], axis=0))\
                        .then_inc(g_loaded[place * UT + t], 16)

            def stored(q):
                for i in range(YB):
                    pool.wait_ge(y_stored[i], 16 * ((q + 1) * R * NT // YB + 1))

            largest(0, 0, -1)
            largest(0, 0, 0)
            for q in range(HALVES):
                largest(q, 0, 1)
                if q:
                    stored(q - 1)
                else:
                    pool.wait_ge(rel_inv_stored, 16)
                with pool.Fori(0, AGG_PAIRS) as i:
                    for j in range(2):
                        for k in range(PER):
                            if q:
                                gather(q - 1, i, 2 * PER, j * PER + k)
                            else:
                                weigh(i * (2 * PER) + (j * PER + k))
                        largest(q, i + 1, j)
                with pool.Fori(AGG_PAIRS, PAIRS - 1) as i:
                    for j in range(2):
                        largest(q, i + 1, j)
                if q + 1 < HALVES:
                    for j in range(2):
                        largest(q + 1, 0, j - 1)
            stored(HALVES - 1)
            with pool.Fori(0, UNITS // 2) as i:
                gather(HALVES - 1, i, 2, 0)
                gather(HALVES - 1, i, 2, 1)

        @block.scalar
        def _(act):
            col = lambda v: v.rearrange("(k p) -> p k", p=P)
            with nc.allow_non_contiguous_dma(reason="short vectors, a few hundred elements"):
                act.dma_start(gcol[:, :], col(norm_g)).then_inc(vec_loaded, 16)
                act.dma_start(bcol[:, :], col(norm_b)).then_inc(vec_loaded, 16)
                act.dma_start(brcol[:, :], col(b_rgcn)).then_inc(vec_loaded, 16)
            act.dma_start(a1s, a_src1.rearrange("h c -> (h c)").partition_broadcast(P)).then_inc(vec_loaded, 16)
            act.dma_start(a1d, a_dst1.rearrange("h c -> (h c)").partition_broadcast(P)).then_inc(vec_loaded, 16)
            act.wait_ge(const_ready, 7)
            act.wait_ge(var_ready, NT)
            nc.scalar.activation(sd[:, :], mv[:, :, 1], ACT.Sqrt, bias=epsc[:, 0:1]).then_inc(std_ready, 1)
            act.wait_ge(vec_loaded, 80)
            for g in range(len(NBANKS)):
                a, b = NBANKS[g]
                for k in range(KT):
                    act.wait_ge(xnT_psum, g * KT + k + 1)
                    nc.scalar.activation(xnT[:, k, a:b], bank[(g * KT + k) % 6][:, 0:b - a], ACT.Identity,
                                         bias=bcol[:, k:k + 1], scale=gcol[:, k:k + 1]).then_inc(xnT_ready, 1)
            act.wait_ge(s1_psum, 1)
            act.wait_ge(const_ready, 7)
            w = 2 * H1
            nc.scalar.copy(s1[:, 0:NT - 1, :], bank[7][:, 0:w * (NT - 1)].rearrange("p (n h) -> p n h", h=w))
            nc.scalar.copy(s1[0:LAST, NT - 1, :], bank[7][0:LAST, w * (NT - 1):w * NT]).then_inc(s1_ready, 1)
            hh = H1 // HALVES

            def h_copy(i):
                n, q = divmod(i, HALVES)
                r = rows(n)
                act.wait_ge(h_psum, i + 1)
                nc.scalar.copy(h1a[0:r, n, q * hh:(q + 1) * hh, 0:C1],
                               bank[H_BANK + i % HB][0:r, 0:CH].rearrange("p (h c) -> p h c", h=hh)).then_inc(h_ready, 1)

            for i in range(H_FIRST):
                h_copy(i)
            for m in range(SORT_PARTS):
                with act.Fori(m * SORT_STEPS, (m + 1) * SORT_STEPS) as i:
                    for k in range(NL):
                        c = i * NL + k
                        at = bass.ds(c, 1)
                        act.wait_ge(oh_lane, c + 1)
                        nc.scalar.activation(oh_l[0:EP, k, 2, :], oh_l[0:EP, k, 0, :], ACT.Copy, scale=dloc_f[:, at])
                        nc.scalar.activation(oh_l[0:EP, k, 3, :], oh_l[0:EP, k, 0, :], ACT.Copy,
                                             scale=typ_f[:, at]).then_inc(oh_fields, 1)
                for i in h_with(m):
                    h_copy(i)
            act.wait_ge(sort_psum, 1)
            nc.scalar.copy(src_s[:, :], bank[0][:, 0:ET]).then_inc(sorted_ready, 1)
            nc.scalar.activation(dst_s[:, :], bank[1][:, 0:ET], ACT.Copy, bias=-1.0).then_inc(sorted_ready, 1)
            nc.scalar.copy(typ_s[:, :], bank[2][:, 0:ET]).then_inc(sorted_ready, 1)
            act.wait_ge(units_ready, 1)
            nc.scalar.copy(credit[:, 0:1], ones[:, 0:1]).then_inc(cnt_copied, len(CBANKS))
            with act.Fori(0, UNITS) as u:
                b = act.value_load(unit_bucket[0:1, bass.ds(u, 1)], min_val=0, max_val=NT - 1)
                for j, (lo, hi) in enumerate(CBANKS):
                    act.wait_ge(cnt_psum, (u + 1) * len(CBANKS) + j + 2)
                    nc.scalar.copy(countsf[:, bass.ds(b * CW + lo, hi - lo)],
                                   bank[j][:, 0:hi - lo]).then_inc(cnt_copied, 1)
            for c in range(NT):
                for g, (a, b) in enumerate(NBANKS):
                    i = c * len(NBANKS) + g
                    act.wait_ge(cT_psum, i + 1)
                    nc.scalar.copy(cT[0:rows(c), c, a:b], bank[i % 6][0:rows(c), 0:b - a]).then_inc(cT_ready, 1)
            act.wait_ge(deg_ready, 1)
            nc.scalar.activation(dsq[:, :], deg[:, :], ACT.Sqrt).then_inc(deg_sqrt, 1)

            def gat(g):
                def row(i, dst):
                    act.wait_ge(g.bc_psum, i + 1)
                    for j, (a, b) in enumerate(NBANKS):
                        ins = nc.scalar.copy(dst[:, a:b], bank[5 + j][:, 0:b - a])
                    ins.then_inc(g.bc, 1)
                for h in range(g.H):
                    if h:
                        act.wait_ge(g.max, NT * h)
                    row(h, bc1)

                def leaky(i):
                    h, c = divmod(i, NT)
                    r = rows(c)
                    if c == 0:
                        act.wait_ge(g.bc, g.H + 2 * h + 1)
                    if i >= 4:
                        act.wait_ge(g.pv, i - 3)
                    nc.scalar.activation(ring[i % 4][0:r, :], bc1[0:r, :], ACT.Identity,
                                         bias=mx[0:r, c, h:h + 1]).then_inc(g.lk, 1)

                act.wait_ge(g.max, NT * g.H)
                row(g.H, bc1)
                row(g.H + 1, bcL)
                leaky(0)
                for i in range(g.H * NT):
                    h, c = divmod(i, NT)
                    if c + 1 < NT:
                        leaky(i + 1)
                    r = rows(c)
                    act.wait_ge(g.t, i + 1)
                    nc.scalar.activation(ring[i % 4][0:r, :], ring[i % 4][0:r, :], ACT.Exp).then_inc(g.ex, 1)
                    if h + 1 < g.H and c == NT - 2:
                        act.wait_ge(g.lk, NT * (h + 1))
                        row(g.H + 2 * h + 2, bc1)
                    if h + 1 < g.H and c == NT - 1:
                        leaky(i + 1)
                        act.wait_ge(g.t, NT * (h + 1))
                        row(g.H + 2 * h + 3, bcL)

            gat(gat1)
            for g, (a, b) in enumerate(NBANKS):
                for k in range(KT):
                    i = g * KT + k
                    act.wait_ge(o1T_psum, i + 1)
                    nc.scalar.copy(o1T[:, k, a:b], bank[i % 6][:, 0:b - a]).then_inc(o1T_ready, 1)
            for n in range(NT):
                r = rows(n)
                act.wait_ge(h2_psum, n + 1)
                nc.scalar.copy(h2[0:r, n, :, 0:C2],
                               bank[n % 4][0:r, 0:D2].rearrange("p (h c) -> p h c", h=H2)).then_inc(h2_ready, 1)
            act.wait_ge(s2_psum, 1)
            w = 2 * H2
            nc.scalar.copy(s2[:, 0:NT - 1, :], bank[7][:, 0:w * (NT - 1)].rearrange("p (n h) -> p n h", h=w))
            nc.scalar.copy(s2[0:LAST, NT - 1, :], bank[7][0:LAST, w * (NT - 1):w * NT]).then_inc(s2_ready, 1)
            gat(gat2)
            for j in range(H2):
                for g, (a, b) in enumerate(NBANKS):
                    i = j * len(NBANKS) + g
                    act.wait_ge(o2T_psum, i + 1)
                    nc.scalar.copy(o2T[:, j, a:b], bank[i][0:C2, 0:b - a]).then_inc(o2T_ready, 1)

            def x1_high(n):
                r = rows(n)
                act.wait_ge(x1T_psum, n + 1)
                for j in range(2):
                    k0, k1 = (0, 4) if j == 0 else (4, KT)
                    ins = nc.scalar.activation(XH[:, k0:k1, n * P:n * P + r],
                                               bank[6 + j][:, 0:(k1 - k0) * P].rearrange("p (k n) -> p k n", n=P)[:, :, 0:r],
                                               ACT.Copy, scale=XSCALE)
                ins.then_inc(x1_hi, 1)

            def x_copy(n):
                r = rows(n)
                act.wait_ge(xT_psum, n + 1)
                if n >= 2:
                    act.wait_ge(y_psum, n - 1)
                for j in range(2):
                    k0, k1 = (0, 4) if j == 0 else (4, KT)
                    ins = nc.scalar.copy(xT[n % 2][:, k0:k1, 0:r],
                                         bank[j][:, 0:(k1 - k0) * P].rearrange("p (k n) -> p k n", n=P)[:, :, 0:r])
                ins.then_inc(xT_ready, 1)

            x_copy(0)
            for n in range(NT):
                r = rows(n)
                if n + 1 < NT:
                    x_copy(n + 1)
                act.wait_ge(y_var, n + 1)
                nc.scalar.activation(sd[0:r, n:n + 1], rstd[0:r, n:n + 1], ACT.Sqrt).then_inc(y_std, 1)
                if n:
                    x1_high(n - 1)
            x1_high(NT - 1)

            def high(q, i, j):
                c = wslot(q, j)
                act.wait_ge(w_scaled, step(q, i, j) + 1)
                nc.scalar.activation(w_hi[c], w_raw[c], ACT.Copy, scale=wscale[:, c:c + 1]).then_inc(w_hi_ready, 1)

            def edge_high(q, i, m, c):
                V, place, uses = unit(q, i, m, c)
                for t in range(UT):
                    act.wait_ge(g_loaded[place * UT + t], (uses + 1) * 16)
                    act.wait_ge(e_sum, V * UT + t + 1)
                    nc.scalar.activation(agg_hi[:, t, :], graw[place * UT + t], ACT.Copy,
                                         scale=w_s[:, bass.ds((i * m + c) * UT + t, 1)]).then_inc(e_hi, 1)

            def copy_out(q, i, j, n):
                c = wslot(q, j)
                r = rows(n)
                act.wait_ge(r_psum, step(q, i, j) * NT + n + 1)
                if j < 0:
                    to = hs[0:r, n, q * CH:(q + 1) * CH]
                else:
                    to = ybuf[yslot(j, n)][0:r, :]
                    act.wait_ge(y_stored[yslot(j, n)], (yuse(q, i, j, n) + 1) * 16)
                nc.scalar.activation(to, bank[n % RB][0:r, 0:CH], ACT.Copy, scale=winv[0:r, c:c + 1]).then_inc(r_copied, 1)

            def one_step(q, i, j, edges):
                for n in range(NT):
                    if edges and n in SPLIT_AT:
                        edge_high(q - 1, i, 2 * PER, j * PER + SPLIT_AT.index(n))
                    copy_out(q, i, j, n)

            nc.scalar.copy(credit[:, 1:2], ones[:, 0:1]).then_inc(e_hi, 2 * UT)
            high(0, 0, -1)
            high(0, 0, 0)
            act.wait_ge(hs_zero, 1)
            for q in range(HALVES):
                one_step(q, 0, -1, False)
                high(q, 0, 1)
                if q:
                    act.wait_ge(edge_w, UNITS)
                    with act.Fori(0, AGG_PAIRS) as i:
                        for j in range(2):
                            one_step(q, i, j, True)
                            high(q, i + 1, j)
                with act.Fori(AGG_PAIRS if q else 0, PAIRS - 1) as i:
                    for j in range(2):
                        one_step(q, i, j, False)
                        high(q, i + 1, j)
                for j in range(2):
                    one_step(q, PAIRS - 1, j, False)
                    if q + 1 < HALVES:
                        high(q + 1, 0, j - 1)
            with act.Fori(0, UNITS // 2) as i:
                edge_high(HALVES - 1, i, 2, 0)
                edge_high(HALVES - 1, i, 2, 1)

            def xw_out(n):
                r = rows(n)
                for q in range(HALVES):
                    act.wait_ge(xw_psum, HALVES * n + q + 1)
                    nc.scalar.activation(hs[0:r, n, q * CH:(q + 1) * CH], bank[2 + 2 * (n % 2) + q][0:r, 0:CH], ACT.Copy,
                                         scale=dinv[0:r, n:n + 1]).then_inc(xw_ready, 1)
            for n in range(NT):
                r = rows(n)
                act.wait_ge(hT_psum, n + 1)
                if n >= 2:
                    act.wait_ge(xw_psum, HALVES * (n - 1))
                for k in range(KT):
                    ins = nc.scalar.activation(hT[n % 2][:, k, 0:r], bank[k // 4][:, (k % 4) * P:(k % 4) * P + r],
                                               ACT.Identity, bias=brcol[:, k:k + 1])
                ins.then_inc(hT_ready, 1)
                if n:
                    xw_out(n - 1)
            xw_out(NT - 1)
            for n in range(NT):
                r = rows(n)
                act.wait_ge(o_var, n + 1)
                nc.scalar.activation(sd[0:r, n:n + 1], rstd[0:r, n:n + 1], ACT.Sqrt).then_inc(o_std, 1)

        @block.vector
        def _(dve):
            seq = Count(dve_seq)

            def after(ins):
                dve.wait_ge(dve_seq, seq.add(ins))

            dve.wait_ge(iota_ready, 1)
            nc.vector.memset(mv[:, :, :], 1.0)
            after(nc.vector.tensor_copy(iota[:, :], iota_i))
            dve.wait_ge(x_loaded, 32)
            for n in range(NT):
                r = rows(n)
                nc.vector.bn_stats(stats[0:r, n, 0:6], xs[0:r, n, 0:D // 2])
                after(nc.vector.bn_stats(stats[0:r, n, 6:12], xs[0:r, n, D // 2:D]))
                nc.vector.bn_aggr(mv[0:r, n, :], stats[0:r, n, :]).then_inc(var_ready, 1)
            dve.wait_ge(std_ready, 1)
            after(nc.vector.reciprocal(rstd[:, :], sd[:, :]))
            for n in range(NT):
                r = rows(n)
                nc.vector.tensor_scalar(xs[0:r, n, :], xs[0:r, n, :], mv[0:r, n, 0:1], rstd[0:r, n:n + 1],
                                        ALU.subtract, ALU.mult).then_inc(xn_ready, 1)
            dve.wait_ge(w1_loaded, 16)
            dve.wait_ge(vec_loaded, 80)
            for k in range(KT):
                for j, a in enumerate((a1s, a1d)):
                    after(nc.vector.tensor_tensor(prod, W1s[:, k, :], a, ALU.mult))
                    ins = nc.vector.tensor_reduce(W1a[:, k, j * H1:(j + 1) * H1],
                                                  prod.rearrange("p (h c) -> p h c", h=H1), AX.X, ALU.add)
                    after(ins)
            nc.vector.memset(prod[:, 0:1], 0.0).then_inc(w1a_ready, 1)

            dve.wait_ge(idx_loaded, 48)
            nc.vector.tensor_copy(src_f, src_i)
            nc.vector.tensor_copy(typ_f, typ_i)
            nc.vector.memset(ones_e, 1.0)
            after(nc.vector.tensor_scalar(tmp_i, dst_i, P - 1, None, ALU.bitwise_and))
            after(nc.vector.tensor_scalar(dloc_f, tmp_i, 1.0, None, ALU.add))
            after(nc.vector.tensor_scalar(tmp_i, dst_i, 7, None, ALU.arith_shift_right))
            after(nc.vector.tensor_copy(dbk_f, tmp_i))
            for k in range(NT):
                after(nc.vector.tensor_scalar(ohb[:, k, :], dbk_f, float(k), None, ALU.is_equal))
                after(nc.vector.tensor_tensor_scan(scan[:, k, :], ones_e, ohb[:, k, :], 0.0, ALU.mult, ALU.add))
            tot = small[0:EP, 0:NT]
            nc.vector.tensor_copy(tot, scan[:, :, EC - 1]).then_inc(part_tot, 1)
            dve.wait_ge(part_psum, 1)
            fcnt, uend, ustart, base = (small[:, i * NT:(i + 1) * NT] for i in range(1, 5))
            after(nc.vector.tensor_scalar(smalli[:, :], bank[6][:, NT:2 * NT], float(UE - 1), None, ALU.add))
            after(nc.vector.tensor_scalar(smalli[:, :], smalli[:, :], UE.bit_length() - 1, None, ALU.arith_shift_right))
            after(nc.vector.tensor_scalar(fcnt, smalli[:, :], 1.0, None, ALU.max))
            after(nc.vector.tensor_tensor_scan(uend, ones[:, 0:NT], fcnt, 0.0, ALU.mult, ALU.add))
            after(nc.vector.tensor_tensor(ustart, uend, fcnt, ALU.subtract))
            after(nc.vector.tensor_scalar(base, ustart, float(UE), -1.0, ALU.mult, ALU.add))
            after(nc.vector.tensor_tensor(base[0:EP], base[0:EP], bank[6][0:EP, 0:NT], ALU.add))
            for k in range(NT):
                after(nc.vector.scalar_tensor_tensor(scan[:, k, :], scan[:, k, :], base[0:EP, k:k + 1], ohb[:, k, :],
                                                     ALU.add, ALU.mult))
                if k:
                    after(nc.vector.tensor_tensor(scan[:, 0, :], scan[:, 0, :], scan[:, k, :], ALU.add))
            after(nc.vector.tensor_copy(dst_i, scan[:, 0, :]))
            after(nc.vector.tensor_scalar(tmp_i, dst_i, P - 1, None, ALU.bitwise_and))
            after(nc.vector.tensor_copy(lane_f, tmp_i))
            after(nc.vector.tensor_scalar(tmp_i, dst_i, 7, None, ALU.arith_shift_right))
            after(nc.vector.tensor_copy(tile_f, tmp_i))
            after(nc.vector.tensor_scalar(bu_f, iota[:, 0:UNITS], uend[:, 0:1], None, ALU.is_ge))
            for k in range(1, NT - 1):
                after(nc.vector.scalar_tensor_tensor(bu_f, iota[:, 0:UNITS], uend[:, k:k + 1], bu_f, ALU.is_ge, ALU.add))
            after(nc.vector.tensor_copy(bt_f.rearrange("p (u t) -> p u t", t=UT),
                                        bu_f.unsqueeze(2).broadcast_to([P, UNITS, UT])))
            nc.vector.tensor_copy(unit_bucket[:, :], bu_f).then_inc(units_ready, 1)
            with dve.Fori(0, EC // NL) as i:
                for k in range(NL):
                    c = i * NL + k
                    at = bass.ds(c, 1)
                    dve.wait_ge(oh_free, c + 1)
                    nc.vector.tensor_scalar(oh_l[0:EP, k, 0, :], iota[0:EP, 0:P], lane_f[:, at], None,
                                            ALU.is_equal).then_inc(oh_lane, 1)
                    nc.vector.tensor_scalar(oh_l[0:EP, k, 1, :], iota[0:EP, 0:P], lane_f[:, at], src_f[:, at],
                                            ALU.is_equal, ALU.mult)
                    nc.vector.tensor_scalar(oh_t[0:EP, k, :], iota[0:EP, 0:ET], tile_f[:, at], None,
                                            ALU.is_equal).then_inc(oh_ready, 1)
            dve.wait_ge(sorted_ready, 3)
            nc.vector.scalar_tensor_tensor(idx_y[:, :], typ_s[:, :], float(N), src_s[:, :], ALU.mult, ALU.add)
            after(nc.vector.scalar_tensor_tensor(bt_f, bt_f, float(P), dst_s[:, :], ALU.mult, ALU.add))
            after(nc.vector.scalar_tensor_tensor(bt_f, bt_f, float(R), typ_s[:, :], ALU.mult, ALU.add))
            after(nc.vector.tensor_scalar(idx_w[:, :], bt_f, 0.0, None, ALU.max))
            with dve.Fori(0, UNITS // 2) as i:
                for j in range(2):
                    u = i * 2 + j
                    dve.wait_ge(cnt_psum, u * len(CBANKS) + 1)
                    nc.vector.tensor_tensor(oh_s[:, j * UT:(j + 1) * UT, N:CW],
                                            iota[:, 0:R].unsqueeze(1).broadcast_to([P, UT, R]),
                                            typ_s[:, bass.ds(u * UT, UT)].unsqueeze(2).broadcast_to([P, UT, R]),
                                            ALU.is_equal)
                    for t in range(UT):
                        at = bass.ds(u * UT + t, 1)
                        s = j * UT + t
                        nc.vector.tensor_scalar(oh_d[:, s, :], iota[:, 0:P], dst_s[:, at], None, ALU.is_equal)
                        nc.vector.tensor_scalar(oh_s[:, s, 0:N], iota[:, 0:N], src_s[:, at], None,
                                                ALU.is_equal).then_inc(cnt_oh, 1)
            dve.wait_ge(cnt_copied, (UNITS + 1) * len(CBANKS))
            for b in range(NT - 1, 0, -1):
                after(nc.vector.tensor_tensor(counts[:, b, :], counts[:, b, :], counts[:, b - 1, :], ALU.subtract))
            for b in range(NT):
                r = rows(b)
                ins = nc.vector.tensor_tensor(counts[0:r, b, b * P:b * P + r], counts[0:r, b, b * P:b * P + r],
                                              ident[0:r, 0:r], ALU.add)
            ins.then_inc(counts_ready, 1)
            dve.wait_ge(counts_ready, 1)
            nc.vector.tensor_reduce(deg[:, :], counts[:, :, 0:N], AX.X, ALU.add)
            after(nc.vector.tensor_scalar(rel_inv[:, :, :], counts[:, :, N:CW], 1.0, None, ALU.max))
            nc.vector.reciprocal(rel_inv[:, :, :], rel_inv[:, :, :]).then_inc(rel_inv_ready, 1)
            nc.vector.tensor_scalar(deg[:, :], deg[:, :], 1.0, None, ALU.max).then_inc(deg_ready, 1)
            dve.wait_ge(h_ready, NT * HALVES)
            for b in range(NT):
                nc.vector.tensor_scalar(mask[:, b, :], counts[:, b, 0:N], 0.0, -BIG, ALU.is_equal,
                                        ALU.mult).then_inc(mask_ready, 1)
            dve.wait_ge(deg_ready, 1)

            def rsqrt(r, sq, v):
                after(nc.vector.reciprocal(r, sq))
                after(nc.vector.tensor_tensor(v, v, r, ALU.mult))
                after(nc.vector.tensor_tensor(v, v, r, ALU.mult))
                after(nc.vector.tensor_scalar(v, v, -0.5, 1.5, ALU.mult, ALU.add))
                after(nc.vector.tensor_tensor(r, r, v, ALU.mult))

            dve.wait_ge(deg_sqrt, 1)
            rsqrt(dinv[:, :], dsq[:, :], deg[:, :])
            def gat(g, s_ready):
                dve.wait_ge(s_ready, 1)
                nd = [0]

                def spread(colv):
                    if nd[0]:
                        dve.wait_ge(g.bc_psum, nd[0])
                    nd[0] += 1
                    nc.vector.tensor_tensor(diag, ident[:, :].unsqueeze(1).broadcast_to([P, NT, P]),
                                            colv.unsqueeze(2).broadcast_to([P, NT, P]), ALU.mult).then_inc(g.diag, 1)

                spread(g.s[:, :, 0])
                for h in range(g.H):
                    if h + 1 < g.H:
                        spread(g.s[:, :, h + 1])
                    dve.wait_ge(g.bc, h + 1)
                    for b in range(NT):
                        i = h * NT + b
                        if i >= 2:
                            dve.wait_ge(g.max, i - 1)
                        nc.vector.tensor_tensor_reduce(ring[i % 2], bc1, mask[:, b, :], 1.0, -3e38, ALU.add, ALU.max,
                                                       mx[:, b, h:h + 1]).then_inc(g.max, 1)
                dve.wait_ge(g.max, NT * g.H)
                z, l = zz[:, :, 0:g.H], lmax[:, :, 0:g.H]
                after(nc.vector.tensor_tensor(z, mx[:, :, 0:g.H], g.s[:, :, g.H:2 * g.H], ALU.add))
                after(nc.vector.scalar_tensor_tensor(l, z, SLOPE, z, ALU.mult, ALU.max))
                g_src, g_dst = g.s[:, :, 0:g.H], g.s[:, :, g.H:2 * g.H]
                after(nc.vector.tensor_tensor(z, g_dst, l, ALU.subtract))
                after(nc.vector.scalar_tensor_tensor(l, g_dst, SLOPE, l, ALU.mult, ALU.subtract))
                after(nc.vector.tensor_scalar(mx[:, :, 0:g.H], g_src, SLOPE, None, ALU.mult))

                def minus(i):
                    h, c = divmod(i, NT)
                    r = rows(c)
                    if c == 0:
                        dve.wait_ge(g.bc, g.H + 2 * h + 2)
                    dve.wait_ge(g.lk, i + 1)
                    nc.vector.scalar_tensor_tensor(ring[i % 4][0:r, :], bcL[0:r, :], g.s[0:r, c, h:h + 1],
                                                   ring[i % 4][0:r, :], ALU.add, ALU.max).then_inc(g.t, 1)

                def normalise(h):
                    dve.wait_ge(g.pv, NT * (h + 1))
                    for b in range(NT):
                        r = rows(b)
                        ins = nc.vector.reciprocal(rden[0:r, b:b + 1], g.acc(b, r, g.C))
                    after(ins)
                    for b in range(NT):
                        r = rows(b)
                        at = slice(h * g.C, (h + 1) * g.C)
                        ins = nc.vector.scalar_tensor_tensor(g.res[0:r, b, at], g.acc(b, r, 0, g.C), rden[0:r, b:b + 1],
                                                             g.brow[0:r, at], ALU.mult, ALU.add)
                    ins.then_inc(g.out, 1)
                    dve.wait_ge(g.out, h + 1)

                spread(lmax[:, :, 0])
                spread(zz[:, :, 0])
                minus(0)
                for i in range(g.H * NT):
                    h, c = divmod(i, NT)
                    r = rows(c)
                    if (i + 1) % NT:
                        minus(i + 1)
                    dve.wait_ge(g.ex, i + 1)
                    dve.wait_ge(cT_ready, NT * len(NBANKS)) if i == 0 else None
                    nc.vector.scalar_tensor_tensor(ring[i % 4][0:r, :], ring[i % 4][0:r, :], 1.0, cT[0:r, c, :],
                                                   ALU.min, ALU.mult).then_inc(g.p, 1)
                    if c >= NT - 2 and h + 1 < g.H:
                        spread(lmax[:, :, h + 1] if c == NT - 2 else zz[:, :, h + 1])
                    if c == NT - 1:
                        if h + 1 < g.H:
                            minus(i + 1)
                        normalise(h)

            dve.wait_ge(mask_ready, NT)
            dve.wait_ge(row_loaded, 16)
            dve.wait_ge(cT_psum, NT * len(NBANKS))
            gat(gat1, s1_ready)
            dve.wait_ge(w2_loaded, 16)
            dve.wait_ge(a2_loaded, 48)
            dve.wait_ge(gat1.pv, NT * H1)
            for k in range(KT):
                for j, a in enumerate((a2s, a2d)):
                    after(nc.vector.tensor_tensor(prod2, W2s[:, k, :], a, ALU.mult))
                    after(nc.vector.tensor_reduce(W2a[:, k, j * H2:(j + 1) * H2],
                                                  prod2.rearrange("p (h c) -> p h c", h=H2), AX.X, ALU.add))
            nc.vector.memset(credit[:, 2:3], 0.0).then_inc(w2a_ready, 1)

            gat(gat2, s2_ready)

            dve.wait_ge(row_loaded, 32)

            def x1_low(n):
                r = rows(n)
                dve.wait_ge(x1_hi, n + 1)
                for j in range(2):
                    k0, k1 = (0, 4) if j == 0 else (4, KT)
                    ins = nc.vector.scalar_tensor_tensor(
                        XL[:, k0:k1, n * P:n * P + r],
                        bank[6 + j][:, 0:(k1 - k0) * P].rearrange("p (k n) -> p k n", n=P)[:, :, 0:r], XSCALE,
                        XH[:, k0:k1, n * P:n * P + r], ALU.mult, ALU.subtract)
                ins.then_inc(x1_lo, 1)

            def layernorm(y, r, n, sem_var, sem_std, done_):
                nc.vector.bn_stats(stats[0:r, n, 0:6], y[0:r, 0:D // 2])
                after(nc.vector.bn_stats(stats[0:r, n, 6:12], y[0:r, D // 2:D]))
                after(nc.vector.bn_aggr(mv[0:r, n, :], stats[0:r, n, :]))
                c = slice(n, n + 1)
                nc.vector.tensor_scalar(rstd[0:r, c], mv[0:r, n, 1:2], EPS, None, ALU.add).then_inc(sem_var, 1)
                dve.wait_ge(sem_std, n + 1)
                rsqrt(small[0:r, c], sd[0:r, c], rstd[0:r, c])
                nc.vector.tensor_scalar(y[0:r, :], y[0:r, :], mv[0:r, n, 0:1], small[0:r, c],
                                        ALU.subtract, ALU.mult).then_inc(done_, 1)

            for n in range(NT):
                r = rows(n)
                y = yt[n % 2]
                dve.wait_ge(xt_loaded[n % XB], 16 * (n // XB + 1))
                dve.wait_ge(y_psum, n + 1)
                if n >= 2:
                    dve.wait_ge(x1_stored[n % 2], 16 * (n // 2))
                    dve.wait_ge(x1T_psum, n - 1)
                for q in range(HALVES):
                    o = slice(q * CH, (q + 1) * CH)
                    ins = nc.vector.tensor_tensor(y[0:r, o], bank[2 + 2 * (n % 2) + q][0:r, 0:CH], xt[n % XB][0:r, o], ALU.add)
                after(ins)
                after(nc.vector.tensor_tensor(y[0:r, :], y[0:r, :], row_a[0:r, :], ALU.add))
                layernorm(y, r, n, y_var, y_std, x1_ready)
                if n:
                    x1_low(n - 1)
            x1_low(NT - 1)

            def prepare(q, i, j):
                c, m = wslot(q, j), step(q, i, j)
                dve.wait_ge(w_loaded[c], wuse(q, i, j) * 16)
                nc.vector.tensor_reduce(wabs[:, c:c + 1], w_raw[c], AX.XY, ALU.max, apply_absolute_value=True)\
                    .then_inc(w_max, 1)
                dve.wait_ge(w_gmax, m + 1)
                e, f = wexp[:, 2 * c:2 * c + 1], wexp[:, 2 * c + 1:2 * c + 2]
                bits = lambda v: v[:, c:c + 1].bitcast(I32)
                chain = (
                    (e, bits(wgm), 23, None, ALU.logical_shift_right),
                    (e, e, -1.0, float(127 + 127 + 14), ALU.mult, ALU.add),
                    (e, e, 240.0, 1.0, ALU.min, ALU.max),
                    (f, e, -1.0, float(2 * 127 - XBITS), ALU.mult, ALU.add),
                    (bits(winv), f, 23, None, ALU.logical_shift_left))
                for k, op in enumerate(chain):
                    nc.vector.tensor_scalar(*op).then_inc(w_chain, 1)
                    dve.wait_ge(w_chain, m * len(chain) + k + 1)
                nc.vector.tensor_scalar(bits(wscale), e, 23, None, ALU.logical_shift_left).then_inc(w_scaled, 1)
                dve.wait_ge(w_hi_ready, m + 1)
                nc.vector.scalar_tensor_tensor(w_lo[c], w_raw[c], wscale[:, c:c + 1], w_hi[c],
                                               ALU.mult, ALU.subtract).then_inc(w_lo_ready, 1)

            def edge_low(q, i, m, c):
                V, place, _ = unit(q, i, m, c)
                for t in range(UT):
                    at = bass.ds((i * m + c) * UT + t, 1)
                    dve.wait_ge(e_sum, V * UT + t + 1)
                    nc.vector.tensor_scalar(agg_oh[:, t, :], iota[:, 0:P], dst_s[:, at], None, ALU.is_equal)
                    dve.wait_ge(e_hi, V * UT + (t + 1 + 2 * UT))
                    nc.vector.scalar_tensor_tensor(agg_lo[:, t, :], graw[place * UT + t], w_s[:, at],
                                                   agg_hi[:, t, :].bitcast(F32), ALU.mult, ALU.subtract).then_inc(e_lo, 1)

            def edge_add(q, i, m, c):
                V, place, _ = unit(q, i, m, c)
                b = dve.value_load(unit_bucket[0:1, bass.ds(i * m + c, 1)], min_val=0, max_val=NT - 1)
                o = bass.ds(b * D + q * CH, CH)
                dve.wait_ge(e_sum, V * UT + 2 * UT)
                dve.wait_ge(e_added, V + 2)
                nc.vector.tensor_tensor(hs_flat[:, o], hs_flat[:, o], bank[SUMS + place][:, 0:CH], ALU.add).then_inc(e_added, 1)

            nc.vector.memset(credit[:, 4:5], 0.0).then_inc(e_lo, 2 * UT)
            nc.vector.memset(credit[:, 5:6], 0.0).then_inc(e_added, 2)
            prepare(0, 0, -1)
            prepare(0, 0, 0)
            for q in range(HALVES):
                dve.wait_ge(r_copied, (step(q, 0, -1) + 1) * NT)
                prepare(q, 0, 1)
                if q:
                    with dve.Fori(0, AGG_PAIRS) as i:
                        for j in range(2):
                            for k in range(PER):
                                edge_low(q - 1, i, 2 * PER, j * PER + k)
                                edge_add(q - 1, i, 2 * PER, j * PER + k)
                            dve.wait_ge(r_copied, (step(q, i, j) + 1) * NT)
                            prepare(q, i + 1, j)
                with dve.Fori(AGG_PAIRS if q else 0, PAIRS - 1) as i:
                    for j in range(2):
                        dve.wait_ge(r_copied, (step(q, i, j) + 1) * NT)
                        prepare(q, i + 1, j)
                for j in range(2):
                    dve.wait_ge(r_copied, (step(q, PAIRS - 1, j) + 1) * NT)
                    if q + 1 < HALVES:
                        prepare(q + 1, 0, j - 1)
            last = HALVES - 1
            edge_low(last, 0, 2, 0)
            with dve.Fori(0, UNITS // 2 - 1) as i:
                edge_low(last, i, 2, 1)
                edge_add(last, i, 2, 0)
                edge_low(last, i, 2, 2)
                edge_add(last, i, 2, 1)
            edge_low(last, 0, 2, UNITS - 1)
            edge_add(last, 0, 2, UNITS - 2)
            edge_add(last, 0, 2, UNITS - 1)

            dve.wait_ge(row_loaded, 48)
            for n in range(NT):
                r = rows(n)
                y = ot[n % 2]
                dve.wait_ge(x1_loaded[n % 2], 16 * (n // 2 + 1))
                dve.wait_ge(gcn_psum, n + 1)
                if n >= 2:
                    dve.wait_ge(out_stored[n % 2], 16 * (n // 2))
                for q in range(HALVES):
                    o = slice(q * CH, (q + 1) * CH)
                    ins = nc.vector.scalar_tensor_tensor(y[0:r, o], bank[2 + 2 * (n % 2) + q][0:r, 0:CH],
                                                         dinv[0:r, n:n + 1], x1t[n % 2][0:r, o], ALU.mult, ALU.add)
                after(ins)
                after(nc.vector.tensor_tensor(y[0:r, :], y[0:r, :], row_a[0:r, :], ALU.add))
                layernorm(y, r, n, o_var, o_std, o_ready)

        @block.tensor
        def _(pe):
            pe.wait_ge(const_ready, 7)
            for g, (a, b) in enumerate(NBANKS):
                pe.wait_ge(xn_ready, cdiv(b, P))
                for k in range(KT):
                    i = g * KT + k
                    if i >= 6:
                        pe.wait_ge(xnT_ready, i - 5)
                    for n in range(a // P, cdiv(b, P)):
                        r = rows(n)
                        ins = nc.tensor.transpose(bank[i % 6][:, n * P - a:n * P - a + r], xs[0:r, n, k * P:(k + 1) * P],
                                                  ident[0:r, 0:r])
                    ins.then_inc(xnT_psum, 1)
            pe.wait_ge(xnT_ready, len(NBANKS) * KT)
            pe.wait_ge(part_tot, 1)
            nc.tensor.matmul(bank[6][0:EP, 0:NT], tri[0:EP, 0:EP], small[0:EP, 0:NT], start=True, stop=True)
            nc.tensor.matmul(bank[6][:, NT:2 * NT], ones[0:EP, :], small[0:EP, 0:NT], start=True,
                             stop=True).then_inc(part_psum, 1)
            pe.wait_ge(w1a_ready, 1)
            w = 2 * H1
            for n in range(NT):
                r = rows(n)
                for k in range(KT):
                    ins = nc.tensor.matmul(bank[7][0:r, w * n:w * n + w], xnT[:, k, n * P:n * P + r], W1a[:, k, :],
                                           start=(k == 0), stop=(k == KT - 1))
            ins.then_inc(s1_psum, 1)
            def h_product(i):
                n, q = divmod(i, HALVES)
                r = rows(n)
                if i >= HB:
                    pe.wait_ge(h_ready, i - HB + 1)
                for k in range(KT):
                    ins = nc.tensor.matmul(bank[H_BANK + i % HB][0:r, 0:CH], xnT[:, k, n * P:n * P + r],
                                           W1s[:, k, q * CH:(q + 1) * CH], start=(k == 0), stop=(k == KT - 1))
                ins.then_inc(h_psum, 1)

            for i in range(H_FIRST):
                h_product(i)
            for f in range(3):
                ins = nc.tensor.matmul(bank[f][:, 0:ET], zeros[:, :], iota[:, 0:ET], start=True, stop=True)
            ins.then_inc(oh_free, NL)
            for m in range(SORT_PARTS):
                with pe.Fori(m * SORT_STEPS, (m + 1) * SORT_STEPS) as i:
                    for k in range(NL):
                        c = i * NL + k
                        pe.wait_ge(oh_ready, c + 1)
                        pe.wait_ge(oh_fields, c + 1)
                        for f in range(3):
                            ins = nc.tensor.matmul(bank[f][:, 0:ET], oh_l[0:EP, k, 1 + f, :], oh_t[0:EP, k, :],
                                                   start=False, stop=False, skip_group_check=True)
                        ins.then_inc(oh_free, 1)
                for i in h_with(m):
                    h_product(i)
            nc.tensor.matmul(bank[6][:, 0:8], zeros[:, :], iota[:, 0:8], start=True, stop=True).then_inc(sort_psum, 1)
            pe.wait_ge(h_ready, NT * HALVES)
            pe.wait_ge(sorted_ready, 3)
            for j, (lo, hi) in enumerate(CBANKS):
                ins = nc.tensor.matmul(bank[j][:, 0:hi - lo], zeros[:, :], iota[:, 0:hi - lo], start=True, stop=True)
            ins.then_inc(cnt_psum, len(CBANKS) + 1)
            with pe.Fori(0, UNITS // 2) as i:
                for jj in range(2):
                    u = i * 2 + jj
                    for j, (lo, hi) in enumerate(CBANKS):
                        pe.wait_ge(cnt_copied, u * len(CBANKS) + j + 1)
                        for t in range(UT):
                            if j == 0:
                                pe.wait_ge(cnt_oh, u * UT + t + 1)
                            s = jj * UT + t
                            ins = nc.tensor.matmul(bank[j][:, 0:hi - lo], oh_d[:, s, :], oh_s[:, s, lo:hi],
                                                   start=False, stop=False, skip_group_check=True)
                        ins.then_inc(cnt_psum, 1)
            pe.wait_ge(counts_ready, 1)
            pe.wait_ge(cnt_copied, (UNITS + 1) * len(CBANKS))
            for c in range(NT):
                for g, (a, b) in enumerate(NBANKS):
                    i = c * len(NBANKS) + g
                    if i >= 6:
                        pe.wait_ge(cT_ready, i - 5)
                    for n in range(a // P, cdiv(b, P)):
                        r = rows(n)
                        ins = nc.tensor.transpose(bank[i % 6][0:rows(c), n * P - a:n * P - a + r],
                                                  counts[0:r, n, c * P:c * P + rows(c)], ident[0:r, 0:r])
                    ins.then_inc(cT_psum, 1)
            pe.wait_ge(cT_ready, NT * len(NBANKS))

            def gat(g, ones_wait):
                nb = [0]

                def row():
                    pe.wait_ge(g.diag, nb[0] + 1)
                    if nb[0]:
                        pe.wait_ge(g.bc, nb[0])
                    nb[0] += 1
                    flat = diag.rearrange("p n q -> p (n q)")
                    for j, (a, b) in enumerate(NBANKS):
                        ins = nc.tensor.matmul(bank[5 + j][:, 0:b - a], ones[:, :], flat[:, a:b], start=True, stop=True)
                    ins.then_inc(g.bc_psum, 1)

                for h in range(g.H):
                    row()
                pe.wait_ge(h_ones, ones_wait)
                row()
                row()
                for h in range(g.H):
                    for c in range(NT):
                        pe.wait_ge(g.p, h * NT + c + 1)
                        if c == 0 and h:
                            pe.wait_ge(g.out, h)
                        rc = rows(c)
                        for b in range(NT):
                            r = rows(b)
                            ins = nc.tensor.matmul(g.acc(b, r), ring[(h * NT + c) % 4][0:rc, b * P:b * P + r],
                                                   g.h[0:rc, c, h, :], start=(c == 0 and b % g.per == 0),
                                                   stop=(c == NT - 1), skip_group_check=True)
                        ins.then_inc(g.pv, 1)
                        if c >= NT - 2 and h + 1 < g.H:
                            row()

            gat(gat1, 1)
            pe.wait_ge(gat1.out, H1)
            for g, (a, b) in enumerate(NBANKS):
                for k in range(KT):
                    i = g * KT + k
                    if i >= 6:
                        pe.wait_ge(o1T_ready, i - 5)
                    for n in range(a // P, cdiv(b, P)):
                        r = rows(n)
                        ins = nc.tensor.transpose(bank[i % 6][:, n * P - a:n * P - a + r], out1[0:r, n, k * P:(k + 1) * P],
                                                  ident[0:r, 0:r])
                    ins.then_inc(o1T_psum, 1)
            pe.wait_ge(o1T_ready, len(NBANKS) * KT)
            pe.wait_ge(w2_loaded, 16)
            for n in range(NT):
                r = rows(n)
                if n >= 4:
                    pe.wait_ge(h2_ready, n - 3)
                for k in range(KT):
                    ins = nc.tensor.matmul(bank[n % 4][0:r, 0:D2], o1T[:, k, n * P:n * P + r], W2s[:, k, :],
                                           start=(k == 0), stop=(k == KT - 1))
                ins.then_inc(h2_psum, 1)
            pe.wait_ge(w2a_ready, 1)
            w = 2 * H2
            for n in range(NT):
                r = rows(n)
                for k in range(KT):
                    ins = nc.tensor.matmul(bank[7][0:r, w * n:w * n + w], o1T[:, k, n * P:n * P + r], W2a[:, k, :],
                                           start=(k == 0), stop=(k == KT - 1))
            ins.then_inc(s2_psum, 1)
            pe.wait_ge(h2_ready, NT)
            pe.wait_ge(s2_ready, 1)
            gat(gat2, 2)
            pe.wait_ge(gat2.out, H2)
            pe.wait_ge(gat2.bc, 3 * H2)
            for j in range(H2):
                for g, (a, b) in enumerate(NBANKS):
                    i = j * len(NBANKS) + g
                    for n in range(a // P, cdiv(b, P)):
                        r = rows(n)
                        ins = nc.tensor.transpose(bank[i][0:C2, n * P - a:n * P - a + r], out2[0:r, n, j * C2:(j + 1) * C2],
                                                  ident[0:r, 0:r])
                    ins.then_inc(o2T_psum, 1)
            pe.wait_ge(o2T_ready, H2 * len(NBANKS))

            def x1_turn(n):
                r = rows(n)
                pe.wait_ge(x1_ready, n + 1)
                if n:
                    pe.wait_ge(x1_lo, n)
                for k in range(KT):
                    ins = nc.tensor.transpose(bank[6 + k // 4][:, (k % 4) * P:(k % 4) * P + r],
                                              yt[n % 2][0:r, k * P:(k + 1) * P], ident[0:r, 0:r])
                ins.then_inc(x1T_psum, 1)

            def x_turn(n):
                r = rows(n)
                pe.wait_ge(xt_loaded[n % XB], 16 * (n // XB + 1))
                for k in range(KT):
                    ins = nc.tensor.transpose(bank[k // 4][:, (k % 4) * P:(k % 4) * P + r],
                                              xt[n % XB][0:r, k * P:(k + 1) * P], ident[0:r, 0:r])
                ins.then_inc(xT_psum, 1)

            pe.wait_ge(wu_loaded, 32)
            x_turn(0)
            for n in range(NT):
                r = rows(n)
                pe.wait_ge(xT_ready, n + 1)
                if n + 1 < NT:
                    x_turn(n + 1)
                if n >= 2:
                    pe.wait_ge(x1_ready, n - 1)
                for q in range(HALVES):
                    o = slice(q * CH, (q + 1) * CH)
                    acc = bank[2 + 2 * (n % 2) + q][0:r, 0:CH]
                    for k in range(KT):
                        nc.tensor.matmul(acc, xT[n % 2][:, k, 0:r], Wux[:, k, o], start=(k == 0), stop=False)
                    for j in range(H2):
                        ins = nc.tensor.matmul(acc, o2T[:, j, n * P:n * P + r], Wuo[:, j, o], start=False,
                                               stop=(j == H2 - 1))
                ins.then_inc(y_psum, 1)
                if n:
                    x1_turn(n - 1)
            x1_turn(NT - 1)

            def edge_sum(q, i, m, c):
                V, place, _ = unit(q, i, m, c)
                acc = bank[SUMS + place][:, 0:CH]
                pe.wait_ge(e_added, V + 1)
                for t in range(UT):
                    pe.wait_ge(e_lo, V * UT + (t + 1 + 2 * UT))
                    nc.tensor.matmul(acc, agg_oh[:, t, :], agg_hi[:, t, :], start=(t == 0), stop=False)
                    nc.tensor.matmul(acc, agg_oh[:, t, :], agg_lo[:, t, :], start=False, stop=(t == UT - 1))\
                        .then_inc(e_sum, 1)

            def one_step(q, i, j, edges):
                c, m = wslot(q, j), step(q, i, j)
                pe.wait_ge(w_lo_ready, m + 1)
                for n in range(NT):
                    r = rows(n)
                    if edges and n in UNIT_AT:
                        edge_sum(q - 1, i, 2 * PER, j * PER + UNIT_AT.index(n))
                    if n >= RB or not (q == 0 and j < 0):
                        pe.wait_ge(r_copied, m * NT + (n - RB + 1))
                    acc = bank[n % RB][0:r, 0:CH]
                    for k in range(KT):
                        xh, xl = XH[:, k, n * P:n * P + r], XL[:, k, n * P:n * P + r]
                        nc.tensor.matmul(acc, xh, w_hi[c][:, k, :], start=(k == 0), stop=False)
                        nc.tensor.matmul(acc, xh, w_lo[c][:, k, :], start=False, stop=False)
                        ins = nc.tensor.matmul(acc, xl, w_hi[c][:, k, :], start=False, stop=(k == KT - 1))
                    ins.then_inc(r_psum, 1)

            pe.wait_ge(x1_lo, NT)
            nc.tensor.matmul(bank[7][:, 0:2], zeros[:, :], iota[:, 0:2], start=True, stop=True)\
                .then_inc(e_sum, UT)
            for q in range(HALVES):
                one_step(q, 0, -1, False)
                if q:
                    with pe.Fori(0, AGG_PAIRS) as i:
                        for j in range(2):
                            one_step(q, i, j, True)
                with pe.Fori(AGG_PAIRS if q else 0, PAIRS) as i:
                    for j in range(2):
                        one_step(q, i, j, False)
            with pe.Fori(0, UNITS // 2) as i:
                edge_sum(HALVES - 1, i, 2, 0)
                edge_sum(HALVES - 1, i, 2, 1)

            pe.wait_ge(e_added, HALVES * UNITS + 2)
            pe.wait_ge(r_copied, STEPS * NT)
            pe.wait_ge(wg_loaded, 16)

            def xw(n):
                r = rows(n)
                pe.wait_ge(hT_ready, n + 1)
                if n >= 2:
                    pe.wait_ge(xw_ready, HALVES * (n - 1))
                for q in range(HALVES):
                    for k in range(KT):
                        ins = nc.tensor.matmul(bank[2 + 2 * (n % 2) + q][0:r, 0:CH], hT[n % 2][:, k, 0:r],
                                               Wg[:, k, q * CH:(q + 1) * CH], start=(k == 0), stop=(k == KT - 1))
                    ins.then_inc(xw_psum, 1)

            for n in range(NT):
                r = rows(n)
                if n:
                    pe.wait_ge(hT_ready, n)
                for k in range(KT):
                    ins = nc.tensor.transpose(bank[k // 4][:, (k % 4) * P:(k % 4) * P + r], hs[0:r, n, k * P:(k + 1) * P],
                                              ident[0:r, 0:r])
                ins.then_inc(hT_psum, 1)
                if n:
                    xw(n - 1)
            xw(NT - 1)
            pe.wait_ge(xw_ready, HALVES * NT)
            for n in range(NT):
                r = rows(n)
                if n >= 2:
                    pe.wait_ge(o_var, n - 1)
                for q in range(HALVES):
                    for c in range(NT):
                        rc = rows(c)
                        ins = nc.tensor.matmul(bank[2 + 2 * (n % 2) + q][0:r, 0:CH], cT[0:rc, c, n * P:n * P + r],
                                               hs[0:rc, c, q * CH:(q + 1) * CH], start=(c == 0), stop=(c == NT - 1))
                ins.then_inc(gcn_psum, 1)


_INS = ['x', 'src', 'dst', 'edge_type_34', 'L0_gnn_norm_g', 'L0_gnn_norm_b', 'L0_gnn_W1', 'L0_gnn_a_src1',
        'L0_gnn_a_dst1', 'L0_gnn_b1', 'L0_gnn_W2', 'L0_gnn_a_src2', 'L0_gnn_a_dst2', 'L0_gnn_b2', 'L0_gnn_Wu',
        'L0_gnn_bu', 'L1_gnn_W_rel', 'L1_gnn_W_root', 'L1_gnn_b_rgcn', 'L1_gnn_W_gcn', 'L1_gnn_b_gcn']
_OUTS = [((1250, 768), 'float32')]


def kernel(**inputs):
    import numpy as _np
    import concourse.bacc as _bacc
    from concourse import mybir as _mybir
    from concourse.bass_utils import run_bass_kernel_spmd as _run

    nc = _bacc.Bacc("TRN2", target_bir_lowering=False, num_devices=1)
    arrays, args = {}, []
    for name in _INS:
        a = _np.ascontiguousarray(inputs[name])
        arrays[f"in_{name}_dram"] = a
        args.append(nc.dram_tensor(f"in_{name}_dram", a.shape, _mybir.dt.from_np(a.dtype), kind="ExternalInput").ap())
    for i, (shape, dtype) in enumerate(_OUTS):
        dt = _mybir.dt.from_np(_np.dtype(dtype))
        args.append(nc.dram_tensor(f"out_{i}_dram", shape, dt, kind="ExternalOutput").ap())
    program(nc, *args)
    r = _run(nc, [arrays], core_ids=[0])
    got = tuple(r.results[0][f"out_{i}_dram"] for i in range(len(_OUTS)))
    return got[0]
```

```python
from contextlib import ExitStack

import concourse.bass as bass
from concourse import mybir

ALU = mybir.AluOpType
ACT = mybir.ActivationFunctionType
AX = mybir.AxisListType
F32, F32R, F16, BF16, I32 = (mybir.dt.float32, mybir.dt.float32r, mybir.dt.float16,
                             mybir.dt.bfloat16, mybir.dt.int32)
ABSMAX = bass.bass_isa.ReduceOp.absmax

P = 128


def cdiv(a, b):
    return -(-a // b)


def program(nc, x, src, dst, etype, norm_g, norm_b, W1, a_src1, a_dst1, b1, W2, a_src2, a_dst2, b2,
            Wu, bu, W_rel, W_root, b_rgcn, W_gcn, b_gcn, out):
    N, D = x.shape
    E = src.shape[0]
    R = W_rel.shape[0]
    H1, C1 = a_src1.shape
    H2, C2 = a_src2.shape
    D2 = H2 * C2
    NT = cdiv(N, P)
    KT = D // P
    LAST = N - (NT - 1) * P
    EPS, SLOPE, BIG = 1e-5, 0.2, 1e30
    XBITS = 10
    XSCALE = float(1 << XBITS)

    def rows(n):
        return LAST if n == NT - 1 else P

    EP = max(p for p in range(1, P + 1) if E % p == 0)
    EC = E // EP
    UT = 4
    UE = UT * P
    UNITS = (E + NT * UE) // UE
    ET = UNITS * UT
    CW = N + R
    BANK = 512
    CBANKS = [(a, min(a + BANK, CW)) for a in range(0, CW, BANK)]
    NBANKS = [(a, min(a + BANK, N)) for a in range(0, N, BANK)]
    HALVES = 2
    CH = D // HALVES

    ctx = ExitStack()
    with ctx:
        def sb(name, shape, dt):
            return ctx.enter_context(nc.sbuf_tensor(name, shape, dt))

        def sem(name):
            return ctx.enter_context(nc.semaphore(name))

        bank = [ctx.enter_context(nc.psum_tensor(f"bank{i}", [P, BANK], F32)) for i in range(8)]

        A0 = 0
        B0 = A0 + NT * CW * 4
        H0 = B0 + NT * N * 4
        M0 = H0 + NT * H1 * (C1 + 1) * 4
        V0 = M0 + NT * N * 2
        VSIZE = 22656
        arena = sb("arena", [P, (V0 + VSIZE) // 4], F32)

        def view(at, shape, dt=F32, parts=P):
            n = 1
            for s in shape:
                n *= s
            size = n * (2 if dt in (F16, BF16) else 4)
            assert at % 4 == 0 and size % 4 == 0 and at + size <= V0 + VSIZE, (at, size)
            v = arena[0:parts, at // 4:(at + size) // 4]
            if dt != F32:
                v = v.bitcast(dt)
            if len(shape) == 2:
                v = v.rearrange("p (a b) -> p a b", a=shape[0])
            elif len(shape) == 3:
                v = v.rearrange("p (a b c) -> p a b c", a=shape[0], b=shape[1])
            return v

        ident = sb("ident", [P, P], F32)
        ones = sb("ones", [P, P], F32)
        tri = sb("tri", [P, P], F32)
        iota = sb("iota", [P, N], F16)
        zeros = sb("zeros", [P, P], F16)
        src_s = sb("src_s", [P, ET], F32)
        dst_s = sb("dst_s", [P, ET], F32)
        typ_s = sb("typ_s", [P, ET], F32)
        w_s = typ_s
        idx_y = sb("idx_y", [P, ET + UT], I32)
        idx_w = sb("idx_w", [P, ET], I32)
        unit_bucket = sb("unit_bucket", [P, UNITS], I32)
        row_a = sb("row_a", [P, D], F32)
        w_now = sb("w_now", [P, UT], F32)
        IDXB = 3
        idx_now = sb("idx_now", [P, IDXB, UT], I32)
        gcol = sb("gcol", [P, KT], F32)
        bcol = sb("bcol", [P, KT], F32)
        s1 = sb("s1", [P, NT, 2 * H1], F32)
        s2 = sb("s2", [P, NT, 2 * H2], F32)
        mx = sb("mx", [P, NT, H1], F32)
        zz = sb("zz", [P, NT, H1], F32)
        lmax = sb("lmax", [P, NT, H1], F32)
        rden = sb("rden", [P, NT], F32)
        stats = sb("stats", [P, NT, 12], F32)
        mv = sb("mv", [P, NT, 2], F32)
        sd = sb("sd", [P, NT], F32)
        rstd = sb("rstd", [P, NT], F32)
        deg = sb("deg", [P, NT], F32)
        dsq = sb("dsq", [P, NT], F32)
        dinv = sb("dinv", [P, NT], F32)
        rel_inv = src_s[:, 0:NT * R].rearrange("p (b r) -> p b r", r=R)
        epsc = sb("epsc", [P, 1], F32)
        small = sb("small", [P, 8 * NT], F32)
        credit = sb("credit", [P, 8], F32)
        smalli = sb("smalli", [P, NT], I32)
        agg_oh = sb("agg_oh", [P, UT, P], F32R)
        agg_hi = sb("agg_hi", [P, UT, CH], F32R)
        agg_lo = sb("agg_lo", [P, UT, CH], F32R)
        wabs = sb("wabs", [P, 2], F32)
        wgm = sb("wgm", [P, 2], F32)
        wexp = sb("wexp", [P, 4], I32)
        wscale = sb("wscale", [P, 2], F32)
        winv = sb("winv", [P, 2], F32)

        y_dram = [nc.dram_tensor(f"y_half{q}", (R * N, CH), F32, kind="Internal").ap() for q in range(HALVES)]
        w_dram = nc.dram_tensor("rel_inv_dram", (NT * P * R, 1), F32, kind="Internal").ap()
        credit_dram = nc.dram_tensor("credit_dram", (4, 16), F32, kind="Internal").ap()
        x1_dram = nc.dram_tensor("x1_dram", (N, D), F32, kind="Internal").ap()

        ia = [A0]

        def ix(shape, dt=F32):
            n = 1
            for s in shape:
                n *= s
            v = view(ia[0], shape, dt, EP)
            ia[0] += n * 4
            return v
        src_i, dst_i, typ_i, tmp_i = (ix([EC], I32) for _ in range(4))
        one_f, two_f, dloc_f, dbk_f, lane_f, tile_f = (ix([EC]) for _ in range(6))
        ohb = ix([NT, EC])
        scan = ix([NT, EC])
        ones_e = ix([EC])
        oh_t = ohb[:, :, :].rearrange("p b c -> p (b c)").bitcast(F16)
        bu_f, bt_f = (view(ia[0] + 4 * k, [n]) for k, n in ((0, UNITS), (UNITS, ET)))
        assert ia[0] + 4 * (UNITS + ET) <= B0
        counts = view(A0, [NT, CW])
        countsf = view(A0, [NT * CW])
        out1 = view(A0, [NT, D])
        TILE = 5000
        wkA = A0 + NT * D * 4
        ring = [view(wkA + TILE * i, [N]) for i in range(4)]
        assert wkA + 4 * TILE <= B0
        h2 = view(A0, [NT, H2, C2 + 1])
        out2 = view(A0 + NT * H2 * (C2 + 1) * 4, [NT, D2])
        xnT = view(B0, [KT, N])
        cT = view(B0, [NT, N])
        xs = view(H0, [NT, D])
        h1a = view(H0, [NT, H1, C1 + 1])
        o1T = view(H0, [KT, N])
        W1s = view(M0, [KT, D + 2 * H1])
        a1s = view(M0 + KT * (D + 2 * H1) * 4, [D])
        a1d = view(M0 + KT * (D + 2 * H1) * 4 + D * 4, [D])
        mask = view(M0, [NT, N], BF16)
        NL = 15
        oh_l = view(V0, [NL, 3, P], F16)
        oh_t = oh_t[:, 0:NL * ET].rearrange("p (s t) -> p s t", s=NL)
        assert EC % NL == 0 and NL * 3 * P * 2 <= 18432
        oh_s = view(V0, [2 * UT, CW], F16)
        DU = 3
        oh_d = view(B0 + KT * N * 4, [DU * UT, P], F16)
        assert UNITS % (2 * DU) == 0
        prod = view(V0 + 18432, [D])
        W2s = view(V0, [KT, D2 + 2 * H2])
        rowsV = V0 + KT * (D2 + 2 * H2) * 4
        bc1 = view(rowsV, [N])
        bcL = view(rowsV + TILE, [N])
        unused = view(rowsV + 2 * TILE, [N])
        vecV = rowsV + 3 * TILE
        iota_i = view(V0, [N], I32)

        prod2 = ring[0][:, 0:D2]
        a2s = view(vecV, [D2])
        a2d = view(vecV + 4 * D2, [D2])
        b2row = view(vecV + 8 * D2, [D2])
        o2T = view(V0 + 2 * D * 4, [H2, N], F32, C2)
        xt = [view(at, [D]) for at in (wkA, wkA + D * 4, V0, V0 + D * 4)]
        XB = len(xt)
        xT = [view(wkA + (2 + i) * D * 4, [KT, P]) for i in range(2)]
        yt = [view(wkA + (4 + i) * D * 4, [D]) for i in range(2)]
        Wux = view(M0, [KT, D])
        Wuo = view(M0 + KT * D * 4, [H2, D], F32, C2)
        XH = view(H0, [KT, N], F16)
        XL = view(H0 + KT * N * 2, [KT, N], F16)
        WB = KT * CH * 4
        w_raw = [view(A0 + i * WB, [KT, CH]) for i in range(2)]
        w_hi = [view(A0 + 2 * WB + i * WB, [KT, CH], F16) for i in range(2)]
        w_lo = [view(A0 + 2 * WB + i * WB + WB // 2, [KT, CH], F16) for i in range(2)]
        ybuf = [view(A0 + 4 * WB + i * CH * 4, [CH]) for i in range(4)]
        graw = [view(A0 + 4 * WB + (4 + i) * CH * 4, [CH]) for i in range(UT)]
        graw += [view(M0 + NT * D * 4 + i * CH * 4, [CH]) for i in range(UT)]
        hs = view(M0, [NT, D])
        hs_flat = view(M0, [NT * D])
        Wg = view(A0, [KT, D])
        HK = KT // HALVES
        uT = view(A0 + 2 * WB, [HK, N])
        share = view(H0, [NT, D])
        afterV = M0 + NT * D * 4
        ot = [view(afterV + i * D * 4, [D]) for i in range(2)]
        x1t = [view(afterV + (2 + i) * D * 4, [D]) for i in range(2)]
        assert HK * N * 4 <= 2 * WB and NT * D * 4 <= M0 - H0 and afterV + 4 * D * 4 <= V0 + VSIZE
        assert A0 + 4 * WB + 8 * CH * 4 <= B0 and UT * CH * 4 == 2 * D * 4
        assert M0 + NT * D * 4 + UT * CH * 4 <= V0 + VSIZE and M0 + (KT + 1) * D * 4 + D * 4 <= V0 + VSIZE

        idx_loaded, w1_loaded, w2_loaded, vec_loaded = (sem(n) for n in (
            "idx_loaded", "w1_loaded", "w2_loaded", "vec_loaded"))
        XP = 2
        x_loaded = [sem(f"x_loaded{i}") for i in range(NT // XP)]
        const_ready = sem("const_ready")
        pool_seq, dve_seq = sem("pool_seq"), sem("dve_seq")
        iota_ready = sem("iota_ready")
        std_ready = sem("std_ready")
        var_ready = sem("var_ready")
        xn_ready = sem("xn_ready")
        w1a_ready = sem("w1a_ready")
        xnT_psum, xnT_ready = sem("xnT_psum"), sem("xnT_ready")
        s1_ready, s2_ready = sem("s1_ready"), sem("s2_ready")
        h_psum, h_ready = sem("h_psum"), sem("h_ready")
        part_tot, part_psum = sem("part_tot"), sem("part_psum")
        oh_lane, oh_ready, oh_one, oh_two, oh_free = (sem(n) for n in (
            "oh_lane", "oh_ready", "oh_one", "oh_two", "oh_free"))
        sort_psum, sorted_ready = sem("sort_psum"), sem("sorted_ready")
        units_ready = sem("units_ready")
        cnt_oh, cnt_diff, cnt_square, cnt_dst = (sem(n) for n in ("cnt_oh", "cnt_diff", "cnt_square", "cnt_dst"))
        cnt_psum, cnt_copied = sem("cnt_psum"), sem("cnt_copied")
        counts_ready, mask_ready, h_ones = sem("counts_ready"), sem("mask_ready"), sem("h_ones")
        rel_inv_ready, rel_inv_stored = sem("rel_inv_ready"), sem("rel_inv_stored")
        deg_summed, deg_ready, deg_sqrt = sem("deg_summed"), sem("deg_ready"), sem("deg_sqrt")
        cT_psum, cT_ready = sem("cT_psum"), sem("cT_ready")
        row_loaded = sem("row_loaded")
        a2_loaded, w2a_ready = sem("a2_loaded"), sem("w2a_ready")

        class Gat:
            def __init__(g, name, H, C, s, s_ready, h, res, brow):
                g.s_ready = s_ready
                g.H, g.C, g.s, g.h, g.res, g.brow = H, C, s, h, res, brow
                g.per = BANK // (C + 1)
                g.banks = cdiv(NT, g.per)
                g.bc_psum, g.bc = sem(f"{name}_bc_psum"), sem(f"{name}_bc")
                g.max, g.lk, g.t, g.ex = sem(f"{name}_max"), sem(f"{name}_lk"), sem(f"{name}_t"), sem(f"{name}_ex")
                g.shift = sem(f"{name}_shift")
                g.turned = [0]
                g.p, g.pv, g.out = sem(f"{name}_p"), sem(f"{name}_pv"), sem(f"{name}_out")

            def acc(g, b, r, lo=0, hi=None):
                at = (b % g.per) * (g.C + 1)
                return bank[b // g.per][0:r, at + lo:at + (g.C + 1 if hi is None else hi)]

        gat1 = Gat("gat1", H1, C1, s1, s1_ready, h1a, out1, row_a)
        gat2 = Gat("gat2", H2, C2, s2, s2_ready, h2, out2, b2row)
        o1T_psum, o1T_ready = sem("o1T_psum"), sem("o1T_ready")
        h2_psum, h2_ready = sem("h2_psum"), sem("h2_ready")
        o2T_psum, o2T_ready = sem("o2T_psum"), sem("o2T_ready")
        wu_loaded = sem("wu_loaded")
        xt_loaded = [sem(f"xt_loaded{i}") for i in range(XB)]
        xT_psum, xT_ready, y_psum, y_var, y_std, x1_ready = (sem(n) for n in (
            "xT_psum", "xT_ready", "y_psum", "y_var", "y_std", "x1_ready"))
        x1T_psum, x1_hi, x1_lo = (sem(n) for n in ("x1T_psum", "x1_hi", "x1_lo"))
        x1_stored = [sem("x1_stored0"), sem("x1_stored1")]
        w_loaded = [sem("w_loaded0"), sem("w_loaded1")]
        w_max, w_gmax, w_chain, w_scaled, w_hi_ready, w_lo_ready = (sem(n) for n in (
            "w_max", "w_gmax", "w_chain", "w_scaled", "w_hi_ready", "w_lo_ready"))
        r_psum, r_copied, hs_set = sem("r_psum"), sem("r_copied"), sem("hs_set")
        root_psum, root_added = sem("root_psum"), sem("root_added")
        y_stored = [sem(f"y_stored{i}") for i in range(4)]
        edge_w = sem("edge_w")
        w_loaded_now = [sem(f"w_loaded_now{t}") for t in range(UT)]
        idx_copied = sem("idx_copied")
        g_loaded = [sem(f"g_loaded{i}") for i in range(2 * UT)]
        e_hi, e_lo, e_sum, e_added = sem("e_hi"), sem("e_lo"), sem("e_sum"), sem("e_added")
        wg_loaded, scaled, uT_psum, uT_ready, share_psum, share_ready = (sem(n) for n in (
            "wg_loaded", "scaled", "uT_psum", "uT_ready", "share_psum", "share_ready"))
        x1_added, rest_added = sem("x1_added"), sem("rest_added")
        x1_loaded = [sem("x1_loaded0"), sem("x1_loaded1")]
        gcn_psum, o_var, o_std, o_ready = sem("gcn_psum"), sem("o_var"), sem("o_std"), sem("o_ready")
        out_stored = [sem("out_stored0"), sem("out_stored1")]

        TLOW = 2048 // P
        LEVELS = cdiv(R, TLOW)
        HALF = LEVELS * N // 2
        assert LEVELS * N - HALF <= 2048 and HALF <= 2048 and (TLOW - 1) + TLOW * (HALF // N) < R
        SORT_PARTS = 11
        SORT_STEPS = EC // NL // SORT_PARTS
        H_BANK, HB = 3, 3
        H_EARLY = 6
        H_FIRST = 12
        H_ORDER = ([(n, 0) for n in range(H_EARLY)] + [(n, 1) for n in range(H_EARLY)]
                   + [(n, q) for n in range(H_EARLY, NT) for q in range(HALVES)])
        assert SORT_PARTS * SORT_STEPS * NL == EC

        def h_with(m):
            left = NT * HALVES - H_FIRST
            return range(H_FIRST + left * m // SORT_PARTS, H_FIRST + left * (m + 1) // SORT_PARTS)

        PAIRS = R // 2
        STEPS = HALVES * (R + 1)
        RB = 5
        SUMS = 5
        YB = 4
        PER = cdiv(UNITS, 2 * (PAIRS - 2))
        AGG_PAIRS = UNITS // (2 * PER)
        SPLIT_AT = [1, 4, 7][:PER]
        UNIT_AT = [4, 7, 10][:PER]
        assert R % 2 == 0 and UNITS == AGG_PAIRS * 2 * PER and UNITS % 2 == 0 and AGG_PAIRS <= PAIRS - 2
        assert NT % RB == 0 and 2 * NT % YB == 0 and R * NT % YB == 0

        W_EARLY = NT - 3
        PARTS = NT // 2
        ROOT_AT = [1, 3, 5, 7]
        ROOTS = len(ROOT_AT)
        PART = 2 * ROOTS
        assert HALVES == 2 and NT % 2 == 0
        SUM_GROUPS = [(g, k) for g in range(len(NBANKS)) for k in range(HK)]
        UB = 3
        PIECES = []
        for j, (g, k) in enumerate(SUM_GROUPS):
            if NBANKS[g][1] - NBANKS[g][0] == BANK:
                PIECES += [("sums", j, range(0, NT // 2)), ("sums", j, range(NT // 2, NT))]
            else:
                PIECES += [("sums", j, range(0, NT))]
        PIECES += [("share", n, None) for n in range(NT)]
        sums_of = lambda n: HK * (n * P // BANK + 1)
        FINAL, ahead = [], 1
        for j in range(len(SUM_GROUPS)):
            FINAL.append(("sums", j))
            n = sum(kind == "share" for kind, _ in FINAL)
            if n < NT and sums_of(n) + ahead <= j + 1:
                FINAL.append(("share", n))
        FINAL += [("share", n) for n in range(sum(kind == "share" for kind, _ in FINAL), NT)]
        REST = UNITS - PARTS * PART
        assert REST == 2 * len(PIECES)

        CHAIN = 5

        assert UNITS % (2 * IDXB) == 0 and 2 * PER % IDXB == 0

        def step(q, i, j):
            return i * 2 + (q * R + j)

        def wuse(q, i, j):
            return i + (q * PAIRS + 1)

        def yslot(j, n):
            return (j * NT + n) % YB

        def yuse(q, i, j, n):
            return i * (2 * NT // YB) + (q * R * NT // YB + (j * NT + n) // YB)

        def unit(q, i, m, c):
            return i * m + (c + q * UNITS), c % 2, i * (m // 2) + (c // 2 + q * (UNITS // 2))

        class Count:
            def __init__(self, s):
                self.s, self.n = s, 0

            def add(self, ins, k=1):
                self.n += k
                ins.then_inc(self.s, k)
                return self.n

        block = ctx.enter_context(nc.Block())

        @block.sync
        def _(sp):
            for i in range(NT // XP):
                a = i * XP
                if i < NT // XP - 1:
                    sp.dma_start(xs[:, a:a + XP, :], x[a * P:(a + XP) * P, :].rearrange("(n p) d -> p n d", p=P))\
                        .then_inc(x_loaded[i], 16)
                else:
                    for n in range(a, NT):
                        sp.dma_start(xs[0:rows(n), n, :], x[n * P:n * P + rows(n), :]).then_inc(x_loaded[i], 16)
            for t, v in ((dst, dst_i), (src, src_i), (etype, typ_i)):
                sp.dma_start(v, t.rearrange("(p c) -> p c", p=EP)).then_inc(idx_loaded, 16)
            sp.dma_start(W1s[:, :, 0:D], W1.rearrange("(k p) o -> p k o", p=P)).then_inc(w1_loaded, 16)
            sp.dma_start(row_a[:, :], b1.partition_broadcast(P)).then_inc(row_loaded, 16)
            sp.wait_ge(counts_ready, 1)
            sp.dma_start(W2s[:, :, 0:D2], W2.rearrange("(k p) o -> p k o", p=P)).then_inc(w2_loaded, 16)
            for t, v in ((a_src2, a2s), (a_dst2, a2d)):
                sp.dma_start(v, t.rearrange("h c -> (h c)").partition_broadcast(P)).then_inc(a2_loaded, 16)
            sp.dma_start(b2row, b2.partition_broadcast(P)).then_inc(a2_loaded, 16)
            sp.wait_ge(rel_inv_ready, 1)
            sp.dma_start(w_dram.rearrange("(b p r) one -> p b (r one)", b=NT, p=P), rel_inv[:, :, :])\
                .then_inc(rel_inv_stored, 16)
            sp.wait_ge(gat1.out, H1 * gat1.banks)
            sp.dma_start(row_a[:, :], bu.partition_broadcast(P)).then_inc(row_loaded, 16)
            sp.wait_ge(gat2.max, NT * H2)
            sp.dma_start(Wux, Wu[0:D, :].rearrange("(k p) o -> p k o", p=P)).then_inc(wu_loaded, 16)
            sp.dma_start(Wuo, Wu[D:D + D2, :].rearrange("(k p) o -> p k o", p=C2)).then_inc(wu_loaded, 16)
            W_rel_v = W_rel.rearrange("r (k p) o -> p r k o", p=P)
            W_root_v = W_root.rearrange("(k p) o -> p k o", p=P)

            def load(q, i, j):
                if q == HALVES:
                    v = W_root_v[:, :, j * CH:(j + 1) * CH]
                    sp.dma_start(w_raw[j], v).then_inc(w_loaded[j], 16)
                    return
                o = slice(q * CH, (q + 1) * CH)
                v = W_rel_v[:, bass.ds(i * 2 + j, 1), :, o].rearrange("p a k o -> p (a k) o")
                sp.dma_start(w_raw[j], v).then_inc(w_loaded[j], 16)

            sp.wait_ge(gat2.out, H2 * gat2.banks)
            for n in range(NT):
                r = rows(n)
                m = n - XB
                if m >= 0:
                    sp.wait_ge(x1_ready, m + 1)
                    sp.dma_start(x1_dram[m * P:(m + 1) * P, :], yt[m % 2][:, :]).then_inc(x1_stored[m % 2], 16)
                sp.dma_start(xt[n % XB][0:r, :], x[n * P:n * P + r, :]).then_inc(xt_loaded[n % XB], 16)
                if n == XB - 1:
                    sp.wait_ge(o2T_ready, H2 * len(NBANKS))
                    for j in range(2):
                        load(0, 0, j)
            for m in range(NT - XB, NT):
                sp.wait_ge(x1_ready, m + 1)
                sp.dma_start(x1_dram[m * P:m * P + rows(m), :], yt[m % 2][0:rows(m), :]).then_inc(x1_stored[m % 2], 16)
            for i in range(2):
                sp.wait_ge(x1_stored[i], 16 * len(range(i, NT, 2)))
            sp.dma_start(row_a[:, :], b_gcn.partition_broadcast(P)).then_inc(row_loaded, 16)
            for n in range(NT):
                sp.dma_start(hs[:, n, :], b_rgcn.partition_broadcast(P)).then_inc(hs_set, 16)
            for i in range(YB):
                sp.dma_start(credit_dram[i:i + 1, :], ones[0:1, 0:16]).then_inc(y_stored[i], 16)

            def store(q, i, j):
                for n in range(NT):
                    sp.wait_ge(r_copied, step(q, i, j) * NT + (n + 1 + RB))
                    sp.dma_start(y_dram[q][bass.ds((i * 2 + j) * N + n * P, rows(n)), :],
                                 ybuf[yslot(j, n)][0:rows(n), :]).then_inc(y_stored[yslot(j, n)], 16)

            for q in range(HALVES):
                with sp.Fori(0, PAIRS - 1) as i:
                    for j in range(2):
                        sp.wait_ge(w_lo_ready, step(q, i, j) + 1)
                        load(q, i + 1, j)
                        store(q, i, j)
                for j in range(2):
                    sp.wait_ge(w_lo_ready, step(q, PAIRS - 1, j) + 1)
                    load(q + 1, 0, j)
                    store(q, PAIRS - 1, j)
            sp.wait_ge(w_lo_ready, STEPS)
            sp.dma_start(Wg, W_gcn.rearrange("(k p) o -> p k o", p=P)).then_inc(wg_loaded, 16)
            for n in range(NT):
                if n >= 2:
                    sp.wait_ge(rest_added, n - 1)
                sp.dma_start(x1t[n % 2][0:rows(n), :], x1_dram[n * P:n * P + rows(n), :]).then_inc(x1_loaded[n % 2], 16)
            for n in range(NT):
                sp.wait_ge(o_ready, n + 1)
                sp.dma_start(out[n * P:n * P + rows(n), :], ot[n % 2][0:rows(n), :]).then_inc(out_stored[n % 2], 16)
            for i in range(2):
                sp.wait_ge(out_stored[i], 16 * len(range(i, NT, 2)))

        @block.gpsimd
        def _(pool):
            n = Count(pool_seq)
            nc.gpsimd.iota(iota_i, pattern=[[1, N]], base=0, channel_multiplier=0).then_inc(iota_ready, 1)
            nc.gpsimd.memset(ones[:, :], 1.0).then_inc(const_ready, 1)
            nc.gpsimd.memset(zeros[:, :], 0.0).then_inc(const_ready, 1)
            nc.gpsimd.memset(epsc[:, :], EPS).then_inc(const_ready, 1)
            nc.gpsimd.memset(s1[:, :, :], 0.0).then_inc(const_ready, 1)
            nc.gpsimd.memset(s2[:, :, :], 0.0).then_inc(const_ready, 1)
            n.add(nc.gpsimd.memset(ident[:, :], 0.0))
            n.add(nc.gpsimd.memset(tri[:, :], 1.0))
            pool.wait_ge(pool_seq, 2)
            nc.gpsimd.affine_select(out=ident[:, :], in_=ident[:, :], compare_op=ALU.not_equal, fill=1.0, base=0,
                                    pattern=[[-1, P]], channel_multiplier=1).then_inc(const_ready, 1)
            nc.gpsimd.affine_select(out=tri[:, :], in_=tri[:, :], compare_op=ALU.is_gt, fill=0.0, base=0,
                                    pattern=[[1, P]], channel_multiplier=-1).then_inc(const_ready, 1)
            pool.wait_ge(xnT_psum, len(NBANKS) * KT)
            nc.gpsimd.memset(h1a[:, :, :, C1:C1 + 1], 1.0).then_inc(h_ones, 1)
            with pool.Fori(0, EC // NL) as i:
                for k in range(NL):
                    c = i * NL + k
                    pool.wait_ge(oh_lane, c + 1)
                    nc.gpsimd.tensor_tensor(oh_l[0:EP, k, 2, :], oh_l[0:EP, k, 0, :],
                                            two_f[:, bass.ds(c, 1)].broadcast_to([EP, P]), ALU.mult).then_inc(oh_two, 1)
            pool.wait_ge(sorted_ready, 1)
            with pool.Fori(0, UNITS // DU) as i:
                for j in range(DU):
                    u = i * DU + j
                    pool.wait_ge(cnt_psum, u * len(CBANKS) + 1)
                    off = oh_d[:, j * UT:(j + 1) * UT, :]
                    nc.gpsimd.tensor_tensor(off, iota[:, 0:P].unsqueeze(1).broadcast_to([P, UT, P]),
                                            dst_s[:, bass.ds(u * UT, UT)].unsqueeze(2).broadcast_to([P, UT, P]),
                                            ALU.subtract).then_inc(cnt_diff, 1)
                    pool.wait_ge(cnt_diff, u + 1)
                    nc.gpsimd.tensor_tensor(off, off, off, ALU.mult).then_inc(cnt_square, 1)
            pool.wait_ge(o1T_psum, len(NBANKS) * KT)
            nc.gpsimd.memset(h2[:, :, :, C2:C2 + 1], 1.0).then_inc(h_ones, 1)

            def largest(q, i, j):
                c = slice(j, j + 1)
                pool.wait_ge(w_max, step(q, i, j) + 1)
                pool.nop(nofuse=True)
                nc.gpsimd.partition_all_reduce(wgm[:, c], wabs[:, c], P, ABSMAX).then_inc(w_gmax, 1)

            def weigh(u):
                nc.gpsimd.tensor_copy(idx_now[:, 0, :], idx_w[:, bass.ds(u * UT, UT)]).then_inc(idx_copied, 1)
                pool.wait_ge(idx_copied, u + 1)
                pool.nop(nofuse=True)
                for t in range(UT):
                    nc.gpsimd.indirect_dma_start(
                        out=w_now[:, t:t + 1], out_offset=None, in_=w_dram,
                        in_offset=bass.IndirectOffsetOnAxis(ap=idx_now[:, 0, t:t + 1], axis=0)).then_inc(w_loaded_now[t], 16)
                for t in range(UT):
                    pool.wait_ge(w_loaded_now[t], (u + 1) * 16)
                nc.gpsimd.tensor_copy(w_s[:, bass.ds(u * UT, UT)], w_now[:, :]).then_inc(edge_w, 1)
                pool.wait_ge(edge_w, u + 1)

            def next_rows(q, i, m, c):
                nc.gpsimd.tensor_copy(idx_now[:, c % IDXB, :], idx_y[:, bass.ds((i * m + c) * UT, UT)]).then_inc(idx_copied, 1)

            def gather(q, i, m, c):
                V, place, _ = unit(q, i, m, c)
                pool.wait_ge(idx_copied, i * m + (c + UNITS + q * (UNITS + 1) + 1))
                for t in range(UT):
                    if t == UT - 1:
                        pool.wait_ge(e_hi, V * UT + UT)
                        next_rows(q, i, m, c + 1)
                    pool.wait_ge(e_lo, V * UT + t + 1)
                    pool.nop(nofuse=True)
                    nc.gpsimd.indirect_dma_start(
                        out=graw[place * UT + t], out_offset=None, in_=y_dram[q],
                        in_offset=bass.IndirectOffsetOnAxis(ap=idx_now[:, c % IDXB, t:t + 1], axis=0))\
                        .then_inc(g_loaded[place * UT + t], 16)

            def stored(q):
                for i in range(YB):
                    pool.wait_ge(y_stored[i], 16 * ((q + 1) * R * NT // YB + 1))

            largest(0, 0, 0)
            largest(0, 0, 1)
            for q in range(HALVES):
                if q:
                    stored(q - 1)
                    next_rows(q - 1, 0, 2 * PER, 0)
                else:
                    pool.wait_ge(rel_inv_stored, 16)
                with pool.Fori(0, AGG_PAIRS) as i:
                    for j in range(2):
                        for k in range(PER):
                            if q:
                                gather(q - 1, i, 2 * PER, j * PER + k)
                            else:
                                weigh(i * (2 * PER) + (j * PER + k))
                        largest(q, i + 1, j)
                with pool.Fori(AGG_PAIRS, PAIRS - 1) as i:
                    for j in range(2):
                        largest(q, i + 1, j)
                for j in range(2):
                    largest(q + 1, 0, j)
            stored(HALVES - 1)
            next_rows(HALVES - 1, 0, 2 * IDXB, 0)
            with pool.Fori(0, UNITS // (2 * IDXB)) as i:
                for c in range(2 * IDXB):
                    gather(HALVES - 1, i, 2 * IDXB, c)
            pool.wait_ge(row_loaded, 48)
            for n in range(NT):
                r = rows(n)
                pool.wait_ge(x1_loaded[n % 2], 16 * (n // 2 + 1))
                pool.wait_ge(share_ready, n + 1)
                nc.gpsimd.tensor_tensor(share[0:r, n, :], share[0:r, n, :], x1t[n % 2][0:r, :], ALU.add).then_inc(x1_added, 1)
                pool.wait_ge(x1_added, n + 1)
                nc.gpsimd.tensor_tensor(share[0:r, n, :], share[0:r, n, :], row_a[0:r, :], ALU.add).then_inc(rest_added, 1)

        @block.scalar
        def _(act):
            col = lambda v: v.rearrange("(k p) -> p k", p=P)
            with nc.allow_non_contiguous_dma(reason="short vectors, a few hundred elements"):
                act.dma_start(gcol[:, :], col(norm_g)).then_inc(vec_loaded, 16)
                act.dma_start(bcol[:, :], col(norm_b)).then_inc(vec_loaded, 16)
            act.dma_start(a1s, a_src1.rearrange("h c -> (h c)").partition_broadcast(P)).then_inc(vec_loaded, 16)
            act.dma_start(a1d, a_dst1.rearrange("h c -> (h c)").partition_broadcast(P)).then_inc(vec_loaded, 16)
            act.wait_ge(const_ready, 7)
            act.wait_ge(var_ready, NT)
            nc.scalar.activation(sd[:, :], mv[:, :, 1], ACT.Sqrt, bias=epsc[:, 0:1]).then_inc(std_ready, 1)
            act.wait_ge(vec_loaded, 64)
            for g in range(len(NBANKS)):
                a, b = NBANKS[g]
                for k in range(KT):
                    act.wait_ge(xnT_psum, g * KT + k + 1)
                    nc.scalar.activation(xnT[:, k, a:b], bank[(g * KT + k) % 6][:, 0:b - a], ACT.Identity,
                                         bias=bcol[:, k:k + 1], scale=gcol[:, k:k + 1]).then_inc(xnT_ready, 1)
            act.wait_ge(const_ready, 7)
            hh = H1 // HALVES

            def h_copy(i):
                n, q = H_ORDER[i]
                r = rows(n)
                act.wait_ge(h_psum, i + 1)
                if q == HALVES - 1:
                    nc.scalar.copy(s1[0:r, n, :], bank[H_BANK + i % HB][0:r, CH:CH + 2 * H1]).then_inc(s1_ready, 1)
                nc.scalar.copy(h1a[0:r, n, q * hh:(q + 1) * hh, 0:C1],
                               bank[H_BANK + i % HB][0:r, 0:CH].rearrange("p (h c) -> p h c", h=hh)).then_inc(h_ready, 1)

            for i in range(H_FIRST):
                h_copy(i)
            for m in range(SORT_PARTS):
                with act.Fori(m * SORT_STEPS, (m + 1) * SORT_STEPS) as i:
                    for k in range(NL):
                        c = i * NL + k
                        at = bass.ds(c, 1)
                        act.wait_ge(oh_lane, c + 1)
                        nc.scalar.activation(oh_l[0:EP, k, 1, :], oh_l[0:EP, k, 0, :], ACT.Copy,
                                             scale=one_f[:, at]).then_inc(oh_one, 1)
                if m:
                    for i in h_with(m - 1):
                        h_copy(i)
            for i in h_with(SORT_PARTS - 1):
                h_copy(i)
            act.wait_ge(units_ready, 1)
            nc.scalar.copy(credit[:, 0:1], ones[:, 0:1]).then_inc(cnt_copied, len(CBANKS))
            def dst_onehot(i, c):
                act.wait_ge(cnt_square, i * DU + (c + 1))
                off = oh_d[:, c % DU * UT:(c % DU + 1) * UT, :]
                nc.scalar.activation(off, off, ACT.Relu, bias=ones[:, 0:1], scale=-1.0).then_inc(cnt_dst, 1)

            def count_copy(i, c):
                b = act.value_load(unit_bucket[0:1, bass.ds(i * DU + c, 1)], min_val=0, max_val=NT - 1)
                for j, (lo, hi) in enumerate(CBANKS):
                    act.wait_ge(cnt_psum, i * (DU * len(CBANKS)) + ((c + DU - 1) * len(CBANKS) + j + 2))
                    nc.scalar.copy(countsf[:, bass.ds(b * CW + lo, hi - lo)],
                                   bank[j][:, 0:hi - lo]).then_inc(cnt_copied, 1)

            dst_onehot(0, 0)
            dst_onehot(0, 1)
            with act.Fori(0, UNITS // DU - 1) as i:
                for c in range(DU):
                    count_copy(i, c)
                    dst_onehot(i, c + 2)
            count_copy(0, UNITS - DU)
            dst_onehot(0, UNITS - 1)
            for c in range(UNITS - DU + 1, UNITS):
                count_copy(0, c)
            def spread_copy(g, i, dst):
                act.wait_ge(g.bc_psum, i + 1)
                for j, (a, b) in enumerate(NBANKS):
                    ins = nc.scalar.copy(dst[:, a:b], bank[5 + j][:, 0:b - a])
                ins.then_inc(g.bc, 1)

            spread_copy(gat1, 0, bc1)
            for c in range(NT):
                for g, (a, b) in enumerate(NBANKS):
                    i = c * len(NBANKS) + g
                    act.wait_ge(cT_psum, i + 1)
                    nc.scalar.copy(cT[0:rows(c), c, a:b], bank[i % 5][0:rows(c), 0:b - a]).then_inc(cT_ready, 1)

            def gat(g):
                row = lambda i, dst: spread_copy(g, i, dst)
                for h in range(1 if g is gat1 else 0, g.H):
                    if h:
                        act.wait_ge(g.max, NT * h)
                    row(h, bc1)

                def leaky(i):
                    h, c = divmod(i, NT)
                    r = rows(c)
                    if c == 0:
                        act.wait_ge(g.bc, g.H + 2 * h + 1)
                    if i >= 4:
                        act.wait_ge(g.pv, i - 3)
                    nc.scalar.activation(ring[i % 4][0:r, :], bc1[0:r, :], ACT.Identity,
                                         bias=mx[0:r, c, h:h + 1]).then_inc(g.lk, 1)

                act.wait_ge(g.max, NT * g.H)
                row(g.H, bc1)
                row(g.H + 1, bcL)
                act.wait_ge(g.shift, 2)
                leaky(0)
                for i in range(g.H * NT):
                    h, c = divmod(i, NT)
                    if c + 1 < NT:
                        leaky(i + 1)
                    r = rows(c)
                    act.wait_ge(g.t, i + 1)
                    nc.scalar.activation(ring[i % 4][0:r, :], ring[i % 4][0:r, :], ACT.Exp).then_inc(g.ex, 1)
                    if h + 1 < g.H and c == NT - 2:
                        act.wait_ge(g.lk, NT * (h + 1))
                        row(g.H + 2 * h + 2, bc1)
                    if h + 1 < g.H and c == NT - 1:
                        leaky(i + 1)
                        act.wait_ge(g.t, NT * (h + 1))
                        row(g.H + 2 * h + 3, bcL)

            gat(gat1)
            for g, (a, b) in enumerate(NBANKS):
                for k in range(KT):
                    i = g * KT + k
                    act.wait_ge(o1T_psum, i + 1)
                    nc.scalar.copy(o1T[:, k, a:b], bank[i % 6][:, 0:b - a]).then_inc(o1T_ready, 1)
            for n in range(NT):
                r = rows(n)
                act.wait_ge(h2_psum, n + 1)
                nc.scalar.copy(s2[0:r, n, :], bank[n % 4][0:r, D2:D2 + 2 * H2]).then_inc(s2_ready, 1)
                nc.scalar.copy(h2[0:r, n, :, 0:C2],
                               bank[n % 4][0:r, 0:D2].rearrange("p (h c) -> p h c", h=H2)).then_inc(h2_ready, 1)
            gat(gat2)
            for j in range(H2):
                for g, (a, b) in enumerate(NBANKS):
                    i = j * len(NBANKS) + g
                    act.wait_ge(o2T_psum, i + 1)
                    nc.scalar.copy(o2T[:, j, a:b], bank[i][0:C2, 0:b - a]).then_inc(o2T_ready, 1)

            def high(q, i, j):
                c = j
                act.wait_ge(w_scaled, step(q, i, j) + 1)
                nc.scalar.activation(w_hi[c], w_raw[c], ACT.Copy, scale=wscale[:, c:c + 1]).then_inc(w_hi_ready, 1)

            def x1_high(n):
                r = rows(n)
                act.wait_ge(x1T_psum, n + 1)
                for j in range(2):
                    k0, k1 = (0, 4) if j == 0 else (4, KT)
                    ins = nc.scalar.activation(XH[:, k0:k1, n * P:n * P + r],
                                               bank[6 + j][:, 0:(k1 - k0) * P].rearrange("p (k n) -> p k n", n=P)[:, :, 0:r],
                                               ACT.Copy, scale=XSCALE)
                ins.then_inc(x1_hi, 1)

            def x_copy(n):
                r = rows(n)
                act.wait_ge(xT_psum, n + 1)
                if n >= 2:
                    act.wait_ge(y_psum, n - 1)
                for j in range(2):
                    k0, k1 = (0, 4) if j == 0 else (4, KT)
                    ins = nc.scalar.copy(xT[n % 2][:, k0:k1, 0:r],
                                         bank[j][:, 0:(k1 - k0) * P].rearrange("p (k n) -> p k n", n=P)[:, :, 0:r])
                ins.then_inc(xT_ready, 1)

            x_copy(0)
            for n in range(NT):
                r = rows(n)
                if n + 1 < NT:
                    x_copy(n + 1)
                act.wait_ge(y_var, n + 1)
                nc.scalar.activation(sd[0:r, n:n + 1], rstd[0:r, n:n + 1], ACT.Sqrt).then_inc(y_std, 1)
                if n:
                    x1_high(n - 1)
                if n == W_EARLY:
                    high(0, 0, 0)
            x1_high(NT - 1)

            def edge_high(q, i, m, c):
                V, place, uses = unit(q, i, m, c)
                for t in range(UT):
                    act.wait_ge(g_loaded[place * UT + t], (uses + 1) * 16)
                    act.wait_ge(e_sum, V * UT + t + 1)
                    nc.scalar.activation(agg_hi[:, t, :], graw[place * UT + t], ACT.Copy,
                                         scale=w_s[:, bass.ds((i * m + c) * UT + t, 1)]).then_inc(e_hi, 1)

            def copy_out(q, i, j, n):
                c = j
                r = rows(n)
                act.wait_ge(r_psum, step(q, i, j) * NT + n + 1)
                to = ybuf[yslot(j, n)][0:r, :]
                act.wait_ge(y_stored[yslot(j, n)], (yuse(q, i, j, n) + 1) * 16)
                nc.scalar.activation(to, bank[n % RB][0:r, 0:CH], ACT.Copy, scale=winv[0:r, c:c + 1]).then_inc(r_copied, 1)

            def one_step(q, i, j, edges):
                for n in range(NT):
                    if edges and n in SPLIT_AT:
                        edge_high(q - 1, i, 2 * PER, j * PER + SPLIT_AT.index(n))
                    copy_out(q, i, j, n)

            nc.scalar.copy(credit[:, 1:2], ones[:, 0:1]).then_inc(e_hi, 2 * UT)
            nc.scalar.copy(credit[:, 3:4], ones[:, 0:1]).then_inc(r_copied, RB)
            high(0, 0, 1)
            for q in range(HALVES):
                if q:
                    act.wait_ge(edge_w, UNITS)
                    with act.Fori(0, AGG_PAIRS) as i:
                        for j in range(2):
                            one_step(q, i, j, True)
                            high(q, i + 1, j)
                with act.Fori(AGG_PAIRS if q else 0, PAIRS - 1) as i:
                    for j in range(2):
                        one_step(q, i, j, False)
                        high(q, i + 1, j)
                for j in range(2):
                    one_step(q, PAIRS - 1, j, False)
                    high(q + 1, 0, j)
            act.wait_ge(deg_ready, 1)
            nc.scalar.activation(dsq[:, :], deg[:, :], ACT.Sqrt).then_inc(deg_sqrt, 1)
            def sums_out(q, j):
                g, k = SUM_GROUPS[j]
                a, b = NBANKS[g]
                act.wait_ge(uT_psum, q * len(SUM_GROUPS) + j + 1)
                nc.scalar.copy(uT[:, k, a:b], bank[j % UB][:, 0:b - a]).then_inc(uT_ready, 1)

            def share_out(n):
                r = rows(n)
                act.wait_ge(share_psum, n + 1)
                for q in range(HALVES):
                    ins = nc.scalar.activation(share[0:r, n, q * CH:(q + 1) * CH], bank[3 + q][0:r, 0:CH], ACT.Copy,
                                               scale=dinv[0:r, n:n + 1])
                ins.then_inc(share_ready, 1)

            def piece_out(m):
                kind, j, cs = PIECES[m]
                if kind == "share":
                    share_out(j)
                elif cs[-1] == NT - 1:
                    sums_out(0, j)

            with act.Fori(0, PARTS * ROOTS) as i:
                edge_high(HALVES - 1, i, 2, 0)
                edge_high(HALVES - 1, i, 2, 1)
            for m in range(len(PIECES)):
                edge_high(HALVES - 1, 0, 2, PARTS * PART + 2 * m)
                edge_high(HALVES - 1, 0, 2, PARTS * PART + 2 * m + 1)
                if m:
                    piece_out(m - 1)
            piece_out(len(PIECES) - 1)
            for kind, j in FINAL:
                if kind == "sums":
                    sums_out(1, j)
                else:
                    act.wait_ge(o_var, j + 1)
                    nc.scalar.activation(sd[0:rows(j), j:j + 1], rstd[0:rows(j), j:j + 1], ACT.Sqrt).then_inc(o_std, 1)

        @block.vector
        def _(dve):
            seq = Count(dve_seq)

            def after(ins):
                dve.wait_ge(dve_seq, seq.add(ins))

            dve.wait_ge(iota_ready, 1)
            nc.vector.memset(mv[:, :, :], 1.0)
            nc.vector.memset(deg[:, :], 1.0)
            after(nc.vector.tensor_copy(iota[:, :], iota_i))
            for n in range(NT):
                r = rows(n)
                if n % XP == 0:
                    dve.wait_ge(x_loaded[n // XP], 16 * (XP if n + XP >= NT else 1))
                nc.vector.bn_stats(stats[0:r, n, 0:6], xs[0:r, n, 0:D // 2])
                after(nc.vector.bn_stats(stats[0:r, n, 6:12], xs[0:r, n, D // 2:D]))
                nc.vector.bn_aggr(mv[0:r, n, :], stats[0:r, n, :]).then_inc(var_ready, 1)
            dve.wait_ge(std_ready, 1)
            after(nc.vector.reciprocal(rstd[:, :], sd[:, :]))
            for n in range(NT):
                r = rows(n)
                nc.vector.tensor_scalar(xs[0:r, n, :], xs[0:r, n, :], mv[0:r, n, 0:1], rstd[0:r, n:n + 1],
                                        ALU.subtract, ALU.mult).then_inc(xn_ready, 1)
            dve.wait_ge(w1_loaded, 16)
            dve.wait_ge(vec_loaded, 64)
            for k in range(KT):
                for j, a in enumerate((a1s, a1d)):
                    after(nc.vector.tensor_tensor(prod, W1s[:, k, 0:D], a, ALU.mult))
                    ins = nc.vector.tensor_reduce(W1s[:, k, D + j * H1:D + (j + 1) * H1],
                                                  prod.rearrange("p (h c) -> p h c", h=H1), AX.X, ALU.add)
                    after(ins)
            nc.vector.memset(prod[:, 0:1], 0.0).then_inc(w1a_ready, 1)

            dve.wait_ge(idx_loaded, 48)
            nc.vector.memset(ones_e, 1.0)
            after(nc.vector.tensor_scalar(tmp_i, dst_i, P - 1, None, ALU.bitwise_and))
            after(nc.vector.tensor_scalar(dloc_f, tmp_i, 1.0, None, ALU.add))
            after(nc.vector.tensor_scalar(tmp_i, dst_i, 7, None, ALU.arith_shift_right))
            after(nc.vector.tensor_copy(dbk_f, tmp_i))
            for k in range(NT):
                after(nc.vector.tensor_scalar(ohb[:, k, :], dbk_f, float(k), None, ALU.is_equal))
                after(nc.vector.tensor_tensor_scan(scan[:, k, :], ones_e, ohb[:, k, :], 0.0, ALU.mult, ALU.add))
            tot = small[0:EP, 0:NT]
            nc.vector.tensor_copy(tot, scan[:, :, EC - 1]).then_inc(part_tot, 1)
            after(nc.vector.tensor_scalar(tmp_i, typ_i, TLOW - 1, None, ALU.bitwise_and))
            after(nc.vector.scalar_tensor_tensor(one_f, tmp_i, float(P), dloc_f, ALU.mult, ALU.add))
            after(nc.vector.tensor_scalar(tmp_i, typ_i, TLOW.bit_length() - 1, None, ALU.arith_shift_right))
            after(nc.vector.scalar_tensor_tensor(two_f, tmp_i, float(N), src_i, ALU.mult, ALU.add))
            after(nc.vector.tensor_scalar(two_f, two_f, float(-HALF), None, ALU.add))
            dve.wait_ge(part_psum, 1)
            fcnt, uend, ustart, base = (small[:, i * NT:(i + 1) * NT] for i in range(1, 5))
            after(nc.vector.tensor_scalar(smalli[:, :], bank[6][:, NT:2 * NT], float(UE - 1), None, ALU.add))
            after(nc.vector.tensor_scalar(smalli[:, :], smalli[:, :], UE.bit_length() - 1, None, ALU.arith_shift_right))
            after(nc.vector.tensor_scalar(fcnt, smalli[:, :], 1.0, None, ALU.max))
            after(nc.vector.tensor_tensor_scan(uend, ones[:, 0:NT], fcnt, 0.0, ALU.mult, ALU.add))
            after(nc.vector.tensor_tensor(ustart, uend, fcnt, ALU.subtract))
            after(nc.vector.tensor_scalar(base, ustart, float(UE), -1.0, ALU.mult, ALU.add))
            after(nc.vector.tensor_tensor(base[0:EP], base[0:EP], bank[6][0:EP, 0:NT], ALU.add))
            for k in range(NT):
                after(nc.vector.scalar_tensor_tensor(scan[:, k, :], scan[:, k, :], base[0:EP, k:k + 1], ohb[:, k, :],
                                                     ALU.add, ALU.mult))
                if k:
                    after(nc.vector.tensor_tensor(scan[:, 0, :], scan[:, 0, :], scan[:, k, :], ALU.add))
            after(nc.vector.tensor_copy(dst_i, scan[:, 0, :]))
            after(nc.vector.tensor_scalar(tmp_i, dst_i, P - 1, None, ALU.bitwise_and))
            after(nc.vector.tensor_copy(lane_f, tmp_i))
            after(nc.vector.tensor_scalar(tmp_i, dst_i, 7, None, ALU.arith_shift_right))
            after(nc.vector.tensor_copy(tile_f, tmp_i))
            after(nc.vector.tensor_scalar(bu_f, iota[:, 0:UNITS], uend[:, 0:1], None, ALU.is_ge))
            for k in range(1, NT - 1):
                after(nc.vector.scalar_tensor_tensor(bu_f, iota[:, 0:UNITS], uend[:, k:k + 1], bu_f, ALU.is_ge, ALU.add))
            after(nc.vector.tensor_copy(bt_f.rearrange("p (u t) -> p u t", t=UT),
                                        bu_f.unsqueeze(2).broadcast_to([P, UNITS, UT])))
            nc.vector.tensor_copy(unit_bucket[:, :], bu_f).then_inc(units_ready, 1)
            with dve.Fori(0, EC // NL) as i:
                for k in range(NL):
                    c = i * NL + k
                    at = bass.ds(c, 1)
                    dve.wait_ge(oh_free, c + 1)
                    nc.vector.tensor_scalar(oh_l[0:EP, k, 0, :], iota[0:EP, 0:P], lane_f[:, at], None,
                                            ALU.is_equal).then_inc(oh_lane, 1)
                    nc.vector.tensor_scalar(oh_t[0:EP, k, :], iota[0:EP, 0:ET], tile_f[:, at], None,
                                            ALU.is_equal).then_inc(oh_ready, 1)
            dve.wait_ge(sort_psum, 1)
            first, second, whole = bank[0][:, 0:ET], bank[1][:, 0:ET], idx_y[:, 0:ET]
            after(nc.vector.tensor_scalar(whole, first, -1.0, None, ALU.add))
            after(nc.vector.tensor_scalar(idx_w[:, :], whole, P - 1, None, ALU.bitwise_and))
            after(nc.vector.tensor_tensor(dst_s[:, :], whole, idx_w[:, :], ALU.min))
            after(nc.vector.tensor_scalar(whole, whole, 7, TLOW - 1, ALU.arith_shift_right, ALU.bitwise_and))
            after(nc.vector.tensor_scalar(typ_s[:, :], second, float(N - HALF), None, ALU.is_ge))
            for k in range(2, LEVELS):
                after(nc.vector.scalar_tensor_tensor(typ_s[:, :], second, float(k * N - HALF), typ_s[:, :], ALU.is_ge, ALU.add))
            after(nc.vector.scalar_tensor_tensor(src_s[:, :], typ_s[:, :], float(-N), second, ALU.mult, ALU.add))
            after(nc.vector.tensor_scalar(src_s[:, :], src_s[:, :], float(HALF), None, ALU.add))
            nc.vector.scalar_tensor_tensor(typ_s[:, :], typ_s[:, :], float(TLOW), whole, ALU.mult, ALU.add)\
                .then_inc(sorted_ready, 1)
            dve.wait_ge(sorted_ready, 1)
            nc.vector.memset(idx_y[:, ET:ET + UT], 0)
            nc.vector.scalar_tensor_tensor(idx_y[:, 0:ET], typ_s[:, :], float(N), src_s[:, :], ALU.mult, ALU.add)
            after(nc.vector.scalar_tensor_tensor(bt_f, bt_f, float(P), dst_s[:, :], ALU.mult, ALU.add))
            after(nc.vector.scalar_tensor_tensor(bt_f, bt_f, float(R), typ_s[:, :], ALU.mult, ALU.add))
            after(nc.vector.tensor_scalar(idx_w[:, :], bt_f, 0.0, None, ALU.max))
            with dve.Fori(0, UNITS // 2) as i:
                for j in range(2):
                    u = i * 2 + j
                    dve.wait_ge(cnt_psum, u * len(CBANKS) + ((DU - 2) * len(CBANKS) + 1))
                    nc.vector.tensor_tensor(oh_s[:, j * UT:(j + 1) * UT, N:CW],
                                            iota[:, 0:R].unsqueeze(1).broadcast_to([P, UT, R]),
                                            typ_s[:, bass.ds(u * UT, UT)].unsqueeze(2).broadcast_to([P, UT, R]),
                                            ALU.is_equal)
                    for t in range(UT):
                        at = bass.ds(u * UT + t, 1)
                        s = j * UT + t
                        nc.vector.tensor_scalar(oh_s[:, s, 0:N], iota[:, 0:N], src_s[:, at], None,
                                                ALU.is_equal).then_inc(cnt_oh, 1)
            dve.wait_ge(cnt_copied, (UNITS + 1) * len(CBANKS))
            for b in range(NT - 1, 0, -1):
                after(nc.vector.tensor_tensor(counts[:, b, :], counts[:, b, :], counts[:, b - 1, :], ALU.subtract))
            for b in range(NT):
                r = rows(b)
                ins = nc.vector.tensor_tensor(counts[0:r, b, b * P:b * P + r], counts[0:r, b, b * P:b * P + r],
                                              ident[0:r, 0:r], ALU.add)
            ins.then_inc(counts_ready, 1)
            dve.wait_ge(counts_ready, 1)
            after(nc.vector.tensor_scalar(rel_inv[:, :, :], counts[:, :, N:CW], 1.0, None, ALU.max))
            dve.wait_ge(h_ready, NT * HALVES)
            for b in range(NT):
                nc.vector.tensor_scalar(mask[:, b, :], counts[:, b, 0:N], 0.0, -BIG, ALU.is_equal,
                                        ALU.mult).then_inc(mask_ready, 1)

            def rsqrt(r, sq, v):
                after(nc.vector.reciprocal(r, sq))
                after(nc.vector.tensor_tensor(v, v, r, ALU.mult))
                after(nc.vector.tensor_tensor(v, v, r, ALU.mult))
                after(nc.vector.tensor_scalar(v, v, -0.5, 1.5, ALU.mult, ALU.add))
                after(nc.vector.tensor_tensor(r, r, v, ALU.mult))

            def gat(g):
                for h in range(g.H):
                    dve.wait_ge(g.bc, h + 1)
                    for b in range(NT):
                        i = h * NT + b
                        if i >= 2:
                            dve.wait_ge(g.max, i - 1)
                        nc.vector.tensor_tensor_reduce((bcL, unused)[i % 2], bc1, mask[:, b, :], 1.0, -3e38, ALU.add, ALU.max,
                                                       mx[:, b, h:h + 1]).then_inc(g.max, 1)
                dve.wait_ge(g.max, NT * g.H)
                if g is gat1:
                    dve.wait_ge(deg_summed, 1)
                    nc.vector.tensor_scalar(deg[:, 0:NT - 1], bank[0][:, 0:NT - 1], 1.0, None, ALU.max)
                    nc.vector.tensor_scalar(deg[0:LAST, NT - 1:NT], bank[0][0:LAST, NT - 1:NT], 1.0, None,
                                            ALU.max).then_inc(deg_ready, 1)
                z, l = zz[:, :, 0:g.H], lmax[:, :, 0:g.H]
                after(nc.vector.tensor_tensor(z, mx[:, :, 0:g.H], g.s[:, :, g.H:2 * g.H], ALU.add))
                after(nc.vector.scalar_tensor_tensor(l, z, SLOPE, z, ALU.mult, ALU.max))
                g_src, g_dst = g.s[:, :, 0:g.H], g.s[:, :, g.H:2 * g.H]
                after(nc.vector.tensor_tensor(z, g_dst, l, ALU.subtract))
                nc.vector.scalar_tensor_tensor(l, g_dst, SLOPE, l, ALU.mult, ALU.subtract).then_inc(g.shift, 1)
                nc.vector.tensor_scalar(mx[:, :, 0:g.H], g_src, SLOPE, None, ALU.mult).then_inc(g.shift, 1)
                dve.wait_ge(g.shift, 2)

                def minus(i):
                    h, c = divmod(i, NT)
                    r = rows(c)
                    if c == 0:
                        dve.wait_ge(g.bc, g.H + 2 * h + 2)
                    dve.wait_ge(g.lk, i + 1)
                    nc.vector.scalar_tensor_tensor(ring[i % 4][0:r, :], bcL[0:r, :], g.s[0:r, c, h:h + 1],
                                                   ring[i % 4][0:r, :], ALU.add, ALU.max).then_inc(g.t, 1)

                def normalise(h):
                    dve.wait_ge(g.pv, NT * (h + 1))
                    for k in range(g.banks):
                        tiles = range(k * g.per, min((k + 1) * g.per, NT))
                        full = [b for b in tiles if rows(b) == P]
                        den = bank[k][:, 0:g.per * (g.C + 1)].rearrange("p (a c) -> p a c", c=g.C + 1)[:, 0:len(full), g.C]
                        ins = nc.vector.reciprocal(rden[:, full[0]:full[-1] + 1], den)
                        for b in tiles:
                            if b not in full:
                                ins = nc.vector.reciprocal(rden[0:rows(b), b:b + 1], g.acc(b, rows(b), g.C))
                        after(ins)
                        for b in tiles:
                            r = rows(b)
                            at = slice(h * g.C, (h + 1) * g.C)
                            ins = nc.vector.scalar_tensor_tensor(g.res[0:r, b, at], g.acc(b, r, 0, g.C), rden[0:r, b:b + 1],
                                                                 g.brow[0:r, at], ALU.mult, ALU.add)
                        ins.then_inc(g.out, 1)
                    dve.wait_ge(g.out, g.banks * (h + 1))

                dve.wait_ge(cT_psum, NT * len(NBANKS))
                minus(0)
                for i in range(g.H * NT):
                    h, c = divmod(i, NT)
                    r = rows(c)
                    if (i + 1) % NT:
                        minus(i + 1)
                    dve.wait_ge(g.ex, i + 1)
                    dve.wait_ge(cT_ready, NT * len(NBANKS)) if i == 0 else None
                    nc.vector.scalar_tensor_tensor(ring[i % 4][0:r, :], ring[i % 4][0:r, :], 1.0, cT[0:r, c, :],
                                                   ALU.min, ALU.mult).then_inc(g.p, 1)
                    if c == 0 and h:
                        normalise(h - 1)
                    if c == NT - 1 and h + 1 < g.H:
                        minus(i + 1)
                normalise(g.H - 1)

            dve.wait_ge(mask_ready, NT)
            dve.wait_ge(row_loaded, 16)
            dve.wait_ge(s1_ready, NT)
            gat(gat1)
            nc.vector.reciprocal(rel_inv[:, :, :], rel_inv[:, :, :]).then_inc(rel_inv_ready, 1)
            dve.wait_ge(w2_loaded, 16)
            dve.wait_ge(a2_loaded, 48)
            dve.wait_ge(gat1.pv, NT * H1)
            for k in range(KT):
                for j, a in enumerate((a2s, a2d)):
                    after(nc.vector.tensor_tensor(prod2, W2s[:, k, 0:D2], a, ALU.mult))
                    after(nc.vector.tensor_reduce(W2s[:, k, D2 + j * H2:D2 + (j + 1) * H2],
                                                  prod2.rearrange("p (h c) -> p h c", h=H2), AX.X, ALU.add))
            nc.vector.memset(credit[:, 2:3], 0.0).then_inc(w2a_ready, 1)

            dve.wait_ge(s2_ready, NT)
            gat(gat2)

            def scale(q, i, j):
                c, m = j, step(q, i, j)
                dve.wait_ge(w_loaded[c], wuse(q, i, j) * 16)
                nc.vector.tensor_reduce(wabs[:, c:c + 1], w_raw[c], AX.XY, ALU.max, apply_absolute_value=True)\
                    .then_inc(w_max, 1)
                dve.wait_ge(w_gmax, m + 1)
                e, f = wexp[:, 2 * c:2 * c + 1], wexp[:, 2 * c + 1:2 * c + 2]
                bits = lambda v: v[:, c:c + 1].bitcast(I32)
                chain = (
                    (e, bits(wgm), 23, None, ALU.logical_shift_right),
                    (e, e, -1.0, float(127 + 127 + 14), ALU.mult, ALU.add),
                    (e, e, 240.0, 1.0, ALU.min, ALU.max),
                    (f, e, -1.0, float(2 * 127 - XBITS), ALU.mult, ALU.add))
                for k, op in enumerate(chain):
                    nc.vector.tensor_scalar(*op).then_inc(w_chain, 1)
                    dve.wait_ge(w_chain, m * CHAIN + k + 1)
                nc.vector.tensor_scalar(bits(wscale), e, 23, None, ALU.logical_shift_left).then_inc(w_scaled, 1)

            def low(q, i, j):
                c, m = j, step(q, i, j)
                nc.vector.tensor_scalar(winv[:, c:c + 1].bitcast(I32), wexp[:, 2 * c + 1:2 * c + 2], 23, None,
                                        ALU.logical_shift_left).then_inc(w_chain, 1)
                dve.wait_ge(w_chain, (m + 1) * CHAIN)
                dve.wait_ge(w_hi_ready, m + 1)
                nc.vector.scalar_tensor_tensor(w_lo[c], w_raw[c], wscale[:, c:c + 1], w_hi[c],
                                               ALU.mult, ALU.subtract).then_inc(w_lo_ready, 1)

            dve.wait_ge(row_loaded, 32)

            def x1_low(n):
                r = rows(n)
                dve.wait_ge(x1_hi, n + 1)
                for j in range(2):
                    k0, k1 = (0, 4) if j == 0 else (4, KT)
                    ins = nc.vector.scalar_tensor_tensor(
                        XL[:, k0:k1, n * P:n * P + r],
                        bank[6 + j][:, 0:(k1 - k0) * P].rearrange("p (k n) -> p k n", n=P)[:, :, 0:r], XSCALE,
                        XH[:, k0:k1, n * P:n * P + r], ALU.mult, ALU.subtract)
                ins.then_inc(x1_lo, 1)

            def layernorm(y, r, n, sem_var, sem_std, done_):
                nc.vector.bn_stats(stats[0:r, n, 0:6], y[0:r, 0:D // 2])
                after(nc.vector.bn_stats(stats[0:r, n, 6:12], y[0:r, D // 2:D]))
                after(nc.vector.bn_aggr(mv[0:r, n, :], stats[0:r, n, :]))
                c = slice(n, n + 1)
                nc.vector.tensor_scalar(rstd[0:r, c], mv[0:r, n, 1:2], EPS, None, ALU.add).then_inc(sem_var, 1)
                dve.wait_ge(sem_std, n + 1)
                rsqrt(small[0:r, c], sd[0:r, c], rstd[0:r, c])
                nc.vector.tensor_scalar(y[0:r, :], y[0:r, :], mv[0:r, n, 0:1], small[0:r, c],
                                        ALU.subtract, ALU.mult).then_inc(done_, 1)

            for n in range(NT):
                r = rows(n)
                y = yt[n % 2]
                dve.wait_ge(xt_loaded[n % XB], 16 * (n // XB + 1))
                dve.wait_ge(y_psum, n + 1)
                if n >= 2:
                    dve.wait_ge(x1_stored[n % 2], 16 * (n // 2))
                    dve.wait_ge(x1T_psum, n - 1)
                for q in range(HALVES):
                    o = slice(q * CH, (q + 1) * CH)
                    ins = nc.vector.tensor_tensor(y[0:r, o], bank[2 + 2 * (n % 2) + q][0:r, 0:CH], xt[n % XB][0:r, o], ALU.add)
                after(ins)
                after(nc.vector.tensor_tensor(y[0:r, :], y[0:r, :], row_a[0:r, :], ALU.add))
                layernorm(y, r, n, y_var, y_std, x1_ready)
                if n:
                    x1_low(n - 1)
                if n == W_EARLY:
                    scale(0, 0, 0)
                    low(0, 0, 0)
            x1_low(NT - 1)

            def edge_low(q, i, m, c):
                V, place, _ = unit(q, i, m, c)
                for t in range(UT):
                    at = bass.ds((i * m + c) * UT + t, 1)
                    dve.wait_ge(e_sum, V * UT + t + 1)
                    nc.vector.tensor_scalar(agg_oh[:, t, :], iota[:, 0:P], dst_s[:, at], None, ALU.is_equal)
                    dve.wait_ge(e_hi, V * UT + (t + 1 + 2 * UT))
                    nc.vector.scalar_tensor_tensor(agg_lo[:, t, :], graw[place * UT + t], w_s[:, at],
                                                   agg_hi[:, t, :].bitcast(F32), ALU.mult, ALU.subtract).then_inc(e_lo, 1)

            def edge_add(q, i, m, c, roots=0):
                V, place, _ = unit(q, i, m, c)
                b = dve.value_load(unit_bucket[0:1, bass.ds(i * m + c, 1)], min_val=0, max_val=NT - 1)
                o = bass.ds(b * D + q * CH, CH)
                dve.wait_ge(e_sum, V * UT + 2 * UT)
                dve.wait_ge(e_added, V + 2)
                dve.wait_ge(root_added, roots + ROOTS)
                nc.vector.tensor_tensor(hs_flat[:, o], hs_flat[:, o], bank[SUMS + place][:, 0:CH], ALU.add).then_inc(e_added, 1)

            nc.vector.memset(credit[:, 4:5], 0.0).then_inc(e_lo, 2 * UT)
            nc.vector.memset(credit[:, 5:6], 0.0).then_inc(e_added, 2)
            nc.vector.memset(credit[:, 6:7], 0.0).then_inc(root_added, ROOTS)
            scale(0, 0, 1)
            low(0, 0, 1)
            for q in range(HALVES):
                if q:
                    dve.wait_ge(hs_set, 16 * NT)
                    with dve.Fori(0, AGG_PAIRS) as i:
                        for j in range(2):
                            for k in range(PER):
                                edge_low(q - 1, i, 2 * PER, j * PER + k)
                                if k == PER - 1:
                                    scale(q, i + 1, j)
                                edge_add(q - 1, i, 2 * PER, j * PER + k)
                            dve.wait_ge(r_copied, step(q, i, j) * NT + (NT + RB))
                            low(q, i + 1, j)
                with dve.Fori(AGG_PAIRS if q else 0, PAIRS - 1) as i:
                    for j in range(2):
                        scale(q, i + 1, j)
                        dve.wait_ge(r_copied, step(q, i, j) * NT + (NT + RB))
                        low(q, i + 1, j)
                for j in range(2):
                    scale(q + 1, 0, j)
                    dve.wait_ge(r_copied, step(q, PAIRS - 1, j) * NT + (NT + RB))
                    low(q + 1, 0, j)
            def root_add(i, k):
                n, q = i * 2 + k // 2, k % 2
                r = rows(n) if isinstance(i, int) else P
                o = bass.ds(n * D + q * CH, CH)
                dve.wait_ge(root_psum, i * ROOTS + (k + 1))
                dve.wait_ge(e_added, i * PART + ((HALVES - 1) * UNITS + ROOT_AT[k] + 2))
                dve.wait_ge(root_added, i * ROOTS + (k + ROOTS))
                nc.vector.scalar_tensor_tensor(hs_flat[0:r, o], bank[k][0:r, 0:CH], winv[0:r, q:q + 1], hs_flat[0:r, o],
                                               ALU.mult, ALU.add).then_inc(root_added, 1)
                if q == 0:
                    dve.wait_ge(root_added, i * ROOTS + (k + ROOTS + 1))
                    nc.vector.tensor_scalar(hs_flat[0:r, o], hs_flat[0:r, o], dinv[0:r, bass.ds(n, 1)], None,
                                            ALU.mult).then_inc(scaled, 1)

            def last_part(i):
                q = HALVES - 1
                for c in range(PART):
                    edge_low(q, i, PART, c + 1)
                    edge_add(q, i, PART, c, i * ROOTS + sum(at <= c for at in ROOT_AT))
                    if c + 1 in ROOT_AT:
                        root_add(i, ROOT_AT.index(c + 1))

            edge_low(HALVES - 1, 0, PART, 0)
            dve.wait_ge(deg_sqrt, 1)
            rsqrt(dinv[:, :], dsq[:, :], deg[:, :])
            with dve.Fori(0, PARTS - 1) as i:
                last_part(i)
            last_part(PARTS - 1)
            first, last = PARTS * PART, HALVES - 1
            with dve.Fori(0, REST // 2 - 1) as i:
                edge_low(last, i, 2, first + 1)
                edge_add(last, i, 2, first, 2 * NT)
                edge_low(last, i, 2, first + 2)
                edge_add(last, i, 2, first + 1, 2 * NT)
            edge_low(last, 0, 2, UNITS - 1)
            edge_add(last, 0, 2, UNITS - 2, 2 * NT)
            edge_add(last, 0, 2, UNITS - 1, 2 * NT)
            dve.wait_ge(e_added, HALVES * UNITS + 2)
            for n in range(NT):
                r = rows(n)
                nc.vector.tensor_scalar(hs[0:r, n, CH:D], hs[0:r, n, CH:D], dinv[0:r, n:n + 1], None,
                                        ALU.mult).then_inc(scaled, 1)

            for n in range(NT):
                r = rows(n)
                y = ot[n % 2]
                dve.wait_ge(gcn_psum, n + 1)
                dve.wait_ge(rest_added, n + 1)
                if n >= 2:
                    dve.wait_ge(out_stored[n % 2], 16 * (n // 2))
                for q in range(HALVES):
                    o = slice(q * CH, (q + 1) * CH)
                    ins = nc.vector.scalar_tensor_tensor(y[0:r, o], bank[3 + 2 * (n % 2) + q][0:r, 0:CH],
                                                         dinv[0:r, n:n + 1], share[0:r, n, o], ALU.mult, ALU.add)
                after(ins)
                layernorm(y, r, n, o_var, o_std, o_ready)

        @block.tensor
        def _(pe):
            pe.wait_ge(const_ready, 7)
            for g, (a, b) in enumerate(NBANKS):
                pe.wait_ge(xn_ready, cdiv(b, P))
                for k in range(KT):
                    i = g * KT + k
                    if i >= 6:
                        pe.wait_ge(xnT_ready, i - 5)
                    for n in range(a // P, cdiv(b, P)):
                        r = rows(n)
                        ins = nc.tensor.transpose(bank[i % 6][:, n * P - a:n * P - a + r], xs[0:r, n, k * P:(k + 1) * P],
                                                  ident[0:r, 0:r])
                    ins.then_inc(xnT_psum, 1)
            pe.wait_ge(xnT_ready, len(NBANKS) * KT)
            def h_product(i):
                n, q = H_ORDER[i]
                r = rows(n)
                if i >= HB:
                    pe.wait_ge(h_ready, i - HB + 1)
                o = slice(q * CH, (q + 1) * CH + (2 * H1 if q == HALVES - 1 else 0))
                for k in range(KT):
                    ins = nc.tensor.matmul(bank[H_BANK + i % HB][0:r, 0:o.stop - o.start], xnT[:, k, n * P:n * P + r],
                                           W1s[:, k, o], start=(k == 0), stop=(k == KT - 1))
                ins.then_inc(h_psum, 1)

            pe.wait_ge(w1_loaded, 16)
            for i in range(H_EARLY):
                h_product(i)
            pe.wait_ge(part_tot, 1)
            nc.tensor.matmul(bank[6][0:EP, 0:NT], tri[0:EP, 0:EP], small[0:EP, 0:NT], start=True, stop=True)
            nc.tensor.matmul(bank[6][:, NT:2 * NT], ones[0:EP, :], small[0:EP, 0:NT], start=True,
                             stop=True).then_inc(part_psum, 1)
            pe.wait_ge(w1a_ready, 1)
            for i in range(H_EARLY, H_FIRST):
                h_product(i)
            for f in range(2):
                ins = nc.tensor.matmul(bank[f][:, 0:ET], zeros[:, :], iota[:, 0:ET], start=True, stop=True)
            ins.then_inc(oh_free, NL)
            for m in range(SORT_PARTS):
                with pe.Fori(m * SORT_STEPS, (m + 1) * SORT_STEPS) as i:
                    for k in range(NL):
                        c = i * NL + k
                        pe.wait_ge(oh_ready, c + 1)
                        pe.wait_ge(oh_one, c + 1)
                        pe.wait_ge(oh_two, c + 1)
                        for f in range(2):
                            ins = nc.tensor.matmul(bank[f][:, 0:ET], oh_l[0:EP, k, 1 + f, :], oh_t[0:EP, k, :],
                                                   start=False, stop=False, skip_group_check=True)
                        ins.then_inc(oh_free, 1)
                for i in h_with(m):
                    h_product(i)
            nc.tensor.matmul(bank[6][:, 0:8], zeros[:, :], iota[:, 0:8], start=True, stop=True).then_inc(sort_psum, 1)
            pe.wait_ge(h_ready, NT * HALVES)
            pe.wait_ge(sorted_ready, 1)
            for j, (lo, hi) in enumerate(CBANKS):
                ins = nc.tensor.matmul(bank[j][:, 0:hi - lo], zeros[:, :], iota[:, 0:hi - lo], start=True, stop=True)
            ins.then_inc(cnt_psum, (DU - 1) * len(CBANKS) + 1)
            with pe.Fori(0, UNITS // (2 * DU)) as i:
                for jj in range(2 * DU):
                    u = i * (2 * DU) + jj
                    for j, (lo, hi) in enumerate(CBANKS):
                        pe.wait_ge(cnt_copied, u * len(CBANKS) + j + 1)
                        for t in range(UT):
                            if j == 0 and t == 0:
                                pe.wait_ge(cnt_dst, u + 1)
                            if j == 0:
                                pe.wait_ge(cnt_oh, u * UT + t + 1)
                            ins = nc.tensor.matmul(bank[j][:, 0:hi - lo], oh_d[:, jj % DU * UT + t, :],
                                                   oh_s[:, jj % 2 * UT + t, lo:hi],
                                                   start=False, stop=False, skip_group_check=True)
                        ins.then_inc(cnt_psum, 1)
            def spread_row(g):
                done = g.turned[0]
                if done == 0:
                    pe.wait_ge(g.s_ready, NT)
                if done == g.H:
                    pe.wait_ge(g.shift, 1)
                if done:
                    pe.wait_ge(g.bc, done)
                g.turned[0] = done + 1
                h, k = divmod(done - g.H, 2)
                column = g.s[:, :, done] if done < g.H else (lmax, zz)[k][:, :, h]
                for n in range(NT):
                    r = rows(n)
                    at = n * P % BANK
                    ins = nc.tensor.transpose(bank[5 + n * P // BANK][:, at:at + r],
                                              column[0:r, n:n + 1].broadcast_to([r, P]), ident[0:r, 0:r])
                ins.then_inc(g.bc_psum, 1)

            spread_row(gat1)
            pe.wait_ge(counts_ready, 1)
            pe.wait_ge(cnt_copied, (UNITS + 1) * len(CBANKS))
            for c in range(NT):
                for g, (a, b) in enumerate(NBANKS):
                    i = c * len(NBANKS) + g
                    if i >= 5:
                        pe.wait_ge(cT_ready, i - 4)
                    for n in range(a // P, cdiv(b, P)):
                        r = rows(n)
                        ins = nc.tensor.transpose(bank[i % 5][0:rows(c), n * P - a:n * P - a + r],
                                                  counts[0:r, n, c * P:c * P + rows(c)], ident[0:r, 0:r])
                    ins.then_inc(cT_psum, 1)
            pe.wait_ge(cT_ready, NT * len(NBANKS))

            def gat(g, ones_wait, beside=None):
                row = lambda: spread_row(g)
                for h in range(g.H):
                    if g.turned[0] == h:
                        row()
                    if beside:
                        beside(h)
                pe.wait_ge(h_ones, ones_wait)
                row()
                row()
                for h in range(g.H):
                    for c in range(NT):
                        pe.wait_ge(g.p, h * NT + c + 1)
                        rc = rows(c)
                        for b in range(NT):
                            r = rows(b)
                            if c == 0 and h and b % g.per == 0:
                                pe.wait_ge(g.out, g.banks * (h - 1) + b // g.per + 1)
                            ins = nc.tensor.matmul(g.acc(b, r), ring[(h * NT + c) % 4][0:rc, b * P:b * P + r],
                                                   g.h[0:rc, c, h, :], start=(c == 0 and b % g.per == 0),
                                                   stop=(c == NT - 1), skip_group_check=True)
                        ins.then_inc(g.pv, 1)
                        if c in (NT - 3, NT - 2) and h + 1 < g.H:
                            row()

            def degrees(h):
                for n in range(NT * h // H1, NT * (h + 1) // H1):
                    r = rows(n)
                    for c in range(NT):
                        rc = rows(c)
                        ins = nc.tensor.matmul(bank[0][0:r, n:n + 1], cT[0:rc, c, n * P:n * P + r], ones[0:rc, 0:1],
                                               start=(c == 0), stop=(c == NT - 1))
                if h == H1 - 1:
                    ins.then_inc(deg_summed, 1)
                    pe.wait_ge(deg_ready, 1)

            gat(gat1, 1, degrees)
            pe.wait_ge(gat1.out, H1 * gat1.banks)
            for g, (a, b) in enumerate(NBANKS):
                for k in range(KT):
                    i = g * KT + k
                    if i >= 6:
                        pe.wait_ge(o1T_ready, i - 5)
                    for n in range(a // P, cdiv(b, P)):
                        r = rows(n)
                        ins = nc.tensor.transpose(bank[i % 6][:, n * P - a:n * P - a + r], out1[0:r, n, k * P:(k + 1) * P],
                                                  ident[0:r, 0:r])
                    ins.then_inc(o1T_psum, 1)
            pe.wait_ge(o1T_ready, len(NBANKS) * KT)
            pe.wait_ge(w2a_ready, 1)
            w = D2 + 2 * H2
            for n in range(NT):
                r = rows(n)
                if n >= 4:
                    pe.wait_ge(h2_ready, n - 3)
                for k in range(KT):
                    ins = nc.tensor.matmul(bank[n % 4][0:r, 0:w], o1T[:, k, n * P:n * P + r], W2s[:, k, :],
                                           start=(k == 0), stop=(k == KT - 1))
                ins.then_inc(h2_psum, 1)
            pe.wait_ge(h2_ready, NT)
            gat(gat2, 2)
            pe.wait_ge(gat2.out, H2 * gat2.banks)
            pe.wait_ge(gat2.bc, 3 * H2)
            for j in range(H2):
                for g, (a, b) in enumerate(NBANKS):
                    i = j * len(NBANKS) + g
                    for n in range(a // P, cdiv(b, P)):
                        r = rows(n)
                        ins = nc.tensor.transpose(bank[i][0:C2, n * P - a:n * P - a + r], out2[0:r, n, j * C2:(j + 1) * C2],
                                                  ident[0:r, 0:r])
                    ins.then_inc(o2T_psum, 1)
            pe.wait_ge(o2T_ready, H2 * len(NBANKS))

            def x1_turn(n):
                r = rows(n)
                pe.wait_ge(x1_ready, n + 1)
                if n:
                    pe.wait_ge(x1_lo, n)
                for k in range(KT):
                    ins = nc.tensor.transpose(bank[6 + k // 4][:, (k % 4) * P:(k % 4) * P + r],
                                              yt[n % 2][0:r, k * P:(k + 1) * P], ident[0:r, 0:r])
                ins.then_inc(x1T_psum, 1)

            def x_turn(n):
                r = rows(n)
                pe.wait_ge(xt_loaded[n % XB], 16 * (n // XB + 1))
                for k in range(KT):
                    ins = nc.tensor.transpose(bank[k // 4][:, (k % 4) * P:(k % 4) * P + r],
                                              xt[n % XB][0:r, k * P:(k + 1) * P], ident[0:r, 0:r])
                ins.then_inc(xT_psum, 1)

            pe.wait_ge(wu_loaded, 32)
            x_turn(0)
            for n in range(NT):
                r = rows(n)
                pe.wait_ge(xT_ready, n + 1)
                if n + 1 < NT:
                    x_turn(n + 1)
                if n >= 2:
                    pe.wait_ge(x1_ready, n - 1)
                for q in range(HALVES):
                    o = slice(q * CH, (q + 1) * CH)
                    acc = bank[2 + 2 * (n % 2) + q][0:r, 0:CH]
                    for k in range(KT):
                        nc.tensor.matmul(acc, xT[n % 2][:, k, 0:r], Wux[:, k, o], start=(k == 0), stop=False)
                    for j in range(H2):
                        ins = nc.tensor.matmul(acc, o2T[:, j, n * P:n * P + r], Wuo[:, j, o], start=False,
                                               stop=(j == H2 - 1))
                ins.then_inc(y_psum, 1)
                if n:
                    x1_turn(n - 1)
            x1_turn(NT - 1)

            def edge_sum(q, i, m, c):
                V, place, _ = unit(q, i, m, c)
                acc = bank[SUMS + place][:, 0:CH]
                pe.wait_ge(e_added, V + 1)
                for t in range(UT):
                    pe.wait_ge(e_lo, V * UT + (t + 1 + 2 * UT))
                    nc.tensor.matmul(acc, agg_oh[:, t, :], agg_hi[:, t, :], start=(t == 0), stop=False)
                    nc.tensor.matmul(acc, agg_oh[:, t, :], agg_lo[:, t, :], start=False, stop=(t == UT - 1))\
                        .then_inc(e_sum, 1)

            def product(n, c, acc):
                at = slice(n * P, n * P + rows(n)) if isinstance(n, int) else n
                for k in range(KT):
                    xh, xl = XH[:, k, at], XL[:, k, at]
                    nc.tensor.matmul(acc, xh, w_hi[c][:, k, :], start=(k == 0), stop=False)
                    nc.tensor.matmul(acc, xh, w_lo[c][:, k, :], start=False, stop=False)
                    ins = nc.tensor.matmul(acc, xl, w_hi[c][:, k, :], start=False, stop=(k == KT - 1))
                return ins

            def one_step(q, i, j, edges):
                pe.wait_ge(w_lo_ready, step(q, i, j) + 1)
                for n in range(NT):
                    if edges and n in UNIT_AT:
                        edge_sum(q - 1, i, 2 * PER, j * PER + UNIT_AT.index(n))
                    pe.wait_ge(r_copied, step(q, i, j) * NT + (n + 1))
                    product(n, j, bank[n % RB][0:rows(n), 0:CH]).then_inc(r_psum, 1)
                if edges and NT in UNIT_AT:
                    edge_sum(q - 1, i, 2 * PER, j * PER + UNIT_AT.index(NT))

            pe.wait_ge(x1_lo, NT)
            nc.tensor.matmul(bank[7][:, 0:2], zeros[:, :], iota[:, 0:2], start=True, stop=True)\
                .then_inc(e_sum, UT)
            for q in range(HALVES):
                if q:
                    with pe.Fori(0, AGG_PAIRS) as i:
                        for j in range(2):
                            one_step(q, i, j, True)
                with pe.Fori(AGG_PAIRS if q else 0, PAIRS) as i:
                    for j in range(2):
                        one_step(q, i, j, False)

            def last_part(i):
                for c in range(PART):
                    if c in ROOT_AT:
                        k = ROOT_AT.index(c)
                        pe.wait_ge(root_added, i * ROOTS + (k + 1))
                        n, r = i * 2 + k // 2, P
                        if isinstance(i, int):
                            r, at = rows(n), n
                        else:
                            at = bass.ds(n * P, P)
                        product(at, k % 2, bank[k][0:r, 0:CH]).then_inc(root_psum, 1)
                    edge_sum(HALVES - 1, i, PART, c)

            pe.wait_ge(w_lo_ready, STEPS)
            pe.wait_ge(r_copied, HALVES * R * NT + RB)
            with pe.Fori(0, PARTS - 1) as i:
                last_part(i)
            last_part(PARTS - 1)

            def sums(q, j, cs):
                g, k = SUM_GROUPS[j]
                a, b = NBANKS[g]
                if cs[0] == 0 and q * len(SUM_GROUPS) + j >= UB:
                    pe.wait_ge(uT_ready, q * len(SUM_GROUPS) + j - UB + 1)
                for c in cs:
                    rc = rows(c)
                    at = q * CH + k * P
                    if j == 0:
                        pe.wait_ge(scaled, q * NT + c + 1)
                    ins = nc.tensor.matmul(bank[j % UB][:, 0:b - a], hs[0:rc, c, at:at + P], cT[0:rc, c, a:b],
                                           start=(c == 0), stop=(c == NT - 1))
                if cs[-1] == NT - 1:
                    ins.then_inc(uT_psum, 1)

            def times_wg(q, n, first_bank):
                r = rows(n)
                for o in range(HALVES):
                    for k in range(HK):
                        ins = nc.tensor.matmul(bank[first_bank + o][0:r, 0:CH], uT[:, k, n * P:n * P + r],
                                               Wg[:, q * HK + k, o * CH:(o + 1) * CH], start=(k == 0), stop=(k == HK - 1))
                return ins

            pe.wait_ge(root_added, 2 * NT + ROOTS)
            for m, (kind, j, cs) in enumerate(PIECES):
                edge_sum(HALVES - 1, 0, 2, PARTS * PART + 2 * m)
                edge_sum(HALVES - 1, 0, 2, PARTS * PART + 2 * m + 1)
                if kind == "sums":
                    sums(0, j, cs)
                else:
                    if j == 0:
                        pe.wait_ge(wg_loaded, 16)
                        pe.wait_ge(uT_ready, len(SUM_GROUPS))
                    else:
                        pe.wait_ge(share_ready, j)
                    times_wg(0, j, 3).then_inc(share_psum, 1)

            pe.wait_ge(e_added, HALVES * UNITS + 2)
            pe.wait_ge(share_ready, NT)
            for kind, j in FINAL:
                if kind == "sums":
                    sums(1, j, range(NT))
                else:
                    pe.wait_ge(uT_ready, len(SUM_GROUPS) + sums_of(j))
                    if j >= 2:
                        pe.wait_ge(o_var, j - 1)
                    times_wg(1, j, 3 + 2 * (j % 2)).then_inc(gcn_psum, 1)


_INS = ['x', 'src', 'dst', 'edge_type_34', 'L0_gnn_norm_g', 'L0_gnn_norm_b', 'L0_gnn_W1', 'L0_gnn_a_src1',
        'L0_gnn_a_dst1', 'L0_gnn_b1', 'L0_gnn_W2', 'L0_gnn_a_src2', 'L0_gnn_a_dst2', 'L0_gnn_b2', 'L0_gnn_Wu',
        'L0_gnn_bu', 'L1_gnn_W_rel', 'L1_gnn_W_root', 'L1_gnn_b_rgcn', 'L1_gnn_W_gcn', 'L1_gnn_b_gcn']
_OUTS = [((1250, 768), 'float32')]


def kernel(**inputs):
    import numpy as _np
    import concourse.bacc as _bacc
    from concourse import mybir as _mybir
    from concourse.bass_utils import run_bass_kernel_spmd as _run

    nc = _bacc.Bacc("TRN2", target_bir_lowering=False, num_devices=1)
    arrays, args = {}, []
    for name in _INS:
        a = _np.ascontiguousarray(inputs[name])
        arrays[f"in_{name}_dram"] = a
        args.append(nc.dram_tensor(f"in_{name}_dram", a.shape, _mybir.dt.from_np(a.dtype), kind="ExternalInput").ap())
    for i, (shape, dtype) in enumerate(_OUTS):
        dt = _mybir.dt.from_np(_np.dtype(dtype))
        args.append(nc.dram_tensor(f"out_{i}_dram", shape, dt, kind="ExternalOutput").ap())
    program(nc, *args)
    r = _run(nc, [arrays], core_ids=[0])
    got = tuple(r.results[0][f"out_{i}_dram"] for i in range(len(_OUTS)))
    return got[0]
```
